# Optimizing a Trainium2 kernel written in Bass

```python
import numpy as np
import jax
import jax.numpy as jnp

def _softmax(x, axis=-1):
    return jax.nn.softmax(x, axis=axis)

def _gelu(x):
    return jax.nn.gelu(x, approximate=True)

def _silu(x):
    return jax.nn.silu(x)

def _sigmoid(x):
    return jax.nn.sigmoid(x)

def _layernorm(x, axis=-1, eps=1e-05):
    m = jnp.mean(x, axis=axis, keepdims=True)
    v = jnp.var(x, axis=axis, keepdims=True)
    return (x - m) / jnp.sqrt(v + eps)

def _scatter_add(tgt, idx, src, axis=0):
    return tgt.at[idx].add(src)

def _segment_sum(src, seg, n):
    return jax.ops.segment_sum(src, seg, n)
kernel_name = 'mk_adj_preln_d2_adj_r2_ae166f'

def setup_inputs(seed: int=0):
    np.random.seed(seed)
    _w = jnp.asarray

    def _rec_inputs():
        import jax
        import jax.numpy as jnp
        _gk = jax.random.key(seed)
        x = -0.0002928 + 1 * jax.random.normal(jax.random.fold_in(_gk, 1), (1354, 512), jnp.float32)
        _a = jax.random.bernoulli(jax.random.fold_in(_gk, 2), 0.0118168, (1354, 1354))
        _a = jnp.logical_or(_a, jnp.eye(1354, dtype=bool))
        _af = _a.astype(jnp.float32)
        _af = _af * jax.random.uniform(jax.random.fold_in(_gk, 3), (1354, 1354), jnp.float32, 0.05, 1)
        adj = _af
        return (x, adj)
    x, adj = _rec_inputs()

    def _L0_gnn_setup():
        import jax, jax.numpy as jnp
        import numpy as np
        D_IN, D_ATTN, STEPS = (512, 64, 2)
        P_TOP, TAU, LN_EPS = (0.9, 1.0, 1e-05)
        N = 2048

        def _xavier(key, shape):
            fan_in, fan_out = (shape[0], shape[1])
            lim = jnp.sqrt(6.0 / (fan_in + fan_out))
            return jax.random.uniform(key, shape, jnp.float32, -lim, lim)

        def _adj_from_feats(Xa, W1, W2, W3):
            Q = Xa @ W1
            K = Xa @ W3
            logits = Q @ W2 @ K.T / TAU
            n = logits.shape[1]
            order = jnp.argsort(-logits, axis=1)
            vals = jnp.take_along_axis(logits, order, axis=1)
            probs = jax.nn.softmax(vals, axis=1)
            csum = jnp.cumsum(probs, axis=1)
            k_i = jnp.sum(csum < P_TOP, axis=1) + 1
            keep = jnp.arange(n)[None, :] < k_i[:, None]
            masked_sorted = jnp.where(keep, vals, -jnp.inf)
            rows = jnp.arange(n)[:, None]
            masked = jnp.full_like(logits, -jnp.inf).at[rows, order].set(masked_sorted)
            return jax.nn.softmax(masked, axis=1)
        key = jax.random.key(seed)
        ks = jax.random.split(key, 12)
        X = jax.random.normal(ks[0], (N, D_IN), jnp.float32)
        S = jax.random.uniform(ks[1], (N, N), jnp.float32)
        W1 = _xavier(ks[2], (D_IN, D_ATTN))
        W3 = _xavier(ks[3], (D_IN, D_ATTN))
        W2 = _xavier(ks[4], (D_ATTN, D_ATTN))
        U1_0 = _xavier(ks[5], (D_IN, D_IN))
        U1_1 = _xavier(ks[6], (D_IN, D_IN))
        U2_0 = _xavier(ks[7], (D_IN, D_IN))
        U2_1 = _xavier(ks[8], (D_IN, D_IN))
        gamma = jnp.ones((D_IN,), jnp.float32)
        beta = jnp.zeros((D_IN,), jnp.float32)
        return {'X': X, 'S': S, 'W1': W1, 'W2': W2, 'W3': W3, 'U1_0': U1_0, 'U1_1': U1_1, 'U2_0': U2_0, 'U2_1': U2_1, 'gamma': gamma, 'beta': beta}
    _L0_gnn_all = _L0_gnn_setup()
    _L0_gnn_in = {k: v for k, v in _L0_gnn_all.items() if k in ('W1', 'W2', 'W3', 'U1_0', 'U1_1', 'U2_0', 'U2_1', 'gamma', 'beta')}
    del _L0_gnn_all

    def _L1_gnn_setup():
        import jax, jax.numpy as jnp
        import numpy as np
        N = 4096
        D = 512

        def adjacent_mat(adj):
            adj = adj + jnp.eye(adj.shape[0], dtype=adj.dtype)
            deg = jnp.sum(adj, axis=1)
            dinv = jnp.where(deg > 0, deg ** (-0.5), 0.0).astype(adj.dtype)
            return dinv[:, None] * adj * dinv[None, :]
        key = jax.random.key(seed)
        k1, k2 = jax.random.split(key)
        x = jax.random.normal(k1, (N, D), dtype=jnp.float32)
        Coefficient2 = 1e-08 * jnp.ones((N, N), dtype=jnp.float32)
        A = jax.random.uniform(k2, (N, N), dtype=jnp.float32)
        return {'x': x, 'Coefficient2': Coefficient2, 'A': A}
    _L1_gnn_all = _L1_gnn_setup()
    _L1_gnn_in = {k: v for k, v in _L1_gnn_all.items() if k in ()}
    del _L1_gnn_all
    return {'x': x, 'adj': adj, 'L0_gnn_W1': _L0_gnn_in['W1'], 'L0_gnn_W2': _L0_gnn_in['W2'], 'L0_gnn_W3': _L0_gnn_in['W3'], 'L0_gnn_U1_0': _L0_gnn_in['U1_0'], 'L0_gnn_U1_1': _L0_gnn_in['U1_1'], 'L0_gnn_U2_0': _L0_gnn_in['U2_0'], 'L0_gnn_U2_1': _L0_gnn_in['U2_1'], 'L0_gnn_gamma': _L0_gnn_in['gamma'], 'L0_gnn_beta': _L0_gnn_in['beta']}

def reference(x, adj, L0_gnn_W1, L0_gnn_W2, L0_gnn_W3, L0_gnn_U1_0, L0_gnn_U1_1, L0_gnn_U2_0, L0_gnn_U2_1, L0_gnn_gamma, L0_gnn_beta):
    import jax
    import jax.numpy as jnp

    def _L0_gnn_ref(X, S, W1, W2, W3, U1_0, U1_1, U2_0, U2_1, gamma, beta):
        import jax, jax.numpy as jnp
        import numpy as np
        D_IN, D_ATTN, STEPS = (512, 64, 2)
        P_TOP, TAU, LN_EPS = (0.9, 1.0, 1e-05)
        N = 2048

        def _xavier(key, shape):
            fan_in, fan_out = (shape[0], shape[1])
            lim = jnp.sqrt(6.0 / (fan_in + fan_out))
            return jax.random.uniform(key, shape, jnp.float32, -lim, lim)

        def _adj_from_feats(Xa, W1, W2, W3):
            Q = Xa @ W1
            K = Xa @ W3
            logits = Q @ W2 @ K.T / TAU
            n = logits.shape[1]
            order = jnp.argsort(-logits, axis=1)
            vals = jnp.take_along_axis(logits, order, axis=1)
            probs = jax.nn.softmax(vals, axis=1)
            csum = jnp.cumsum(probs, axis=1)
            k_i = jnp.sum(csum < P_TOP, axis=1) + 1
            keep = jnp.arange(n)[None, :] < k_i[:, None]
            masked_sorted = jnp.where(keep, vals, -jnp.inf)
            rows = jnp.arange(n)[:, None]
            masked = jnp.full_like(logits, -jnp.inf).at[rows, order].set(masked_sorted)
            return jax.nn.softmax(masked, axis=1)
        n = X.shape[0]
        S = S + jnp.eye(n, dtype=X.dtype)
        R = S / jnp.clip(S.sum(axis=1, keepdims=True), 1e-12)
        Z = jnp.zeros_like(X)
        Xf, Xa = (X, X)
        U1s, U2s = ((U1_0, U1_1), (U2_0, U2_1))
        for s in range(STEPS):
            A = _adj_from_feats(Xa, W1, W2, W3)
            Xf = R @ Xf
            Xa = A @ Xa
            Z = Z + (Xf @ U1s[s] + Xa @ U2s[s])
        Y = X + Z
        mu = Y.mean(axis=-1, keepdims=True)
        var = Y.var(axis=-1, keepdims=True)
        return (Y - mu) * jax.lax.rsqrt(var + LN_EPS) * gamma + beta

    def _L1_gnn_ref(x, Coefficient2, A):
        import jax, jax.numpy as jnp
        import numpy as np
        N = 4096
        D = 512

        def adjacent_mat(adj):
            adj = adj + jnp.eye(adj.shape[0], dtype=adj.dtype)
            deg = jnp.sum(adj, axis=1)
            dinv = jnp.where(deg > 0, deg ** (-0.5), 0.0).astype(adj.dtype)
            return dinv[:, None] * adj * dinv[None, :]
        A_c = jax.lax.stop_gradient(A)
        adj = adjacent_mat((A_c + A_c.T) * 0.5)
        y = Coefficient2 @ adj
        y = y @ x
        return y
    h = jnp.maximum(_layernorm(x, axis=-1), 0.0)
    x = x + _L0_gnn_ref(h, adj, L0_gnn_W1, L0_gnn_W2, L0_gnn_W3, L0_gnn_U1_0, L0_gnn_U1_1, L0_gnn_U2_0, L0_gnn_U2_1, L0_gnn_gamma, L0_gnn_beta)
    h = jnp.maximum(_layernorm(x, axis=-1), 0.0)
    x = x + _L1_gnn_ref(h, adj, adj)
    return x

_drawn_inputs = setup_inputs


def setup_inputs(seed=0):
    import zlib

    import numpy as np

    out = dict(_drawn_inputs(seed))
    spreads = {'L0_gnn_gamma': (1.0, 0.2), 'L0_gnn_beta': (0.0, 0.1)}
    factors = {}
    for name, (base, spread) in spreads.items():
        noise = np.random.default_rng([zlib.crc32(name.encode()), seed]).standard_normal(out[name].shape)
        drawn = base * np.exp(spread * noise) if base else spread * noise
        out[name] = jnp.asarray(drawn.astype(out[name].dtype))
    for name, factor in factors.items():
        out[name] = (out[name] * factor).astype(out[name].dtype)
    return out
```

```python
from contextlib import ExitStack

import concourse.bass as bass
from concourse import mybir

F32 = mybir.dt.float32
F32R = mybir.dt.float32r
BF16 = mybir.dt.bfloat16
I32 = mybir.dt.int32
U32 = mybir.dt.uint32
ALU = mybir.AluOpType
ACT = mybir.ActivationFunctionType
AX = mybir.AxisListType
RMAX = bass.bass_isa.ReduceOp.max

P = 128
TOP_P = 0.9
LN_EPS = 1e-5
LAYER_EPS = 1e-5
HALVINGS = (4, 4)
INTERPOLATIONS = (2, 4)
ROUNDS = (1, 2)
MORE_ROUNDS = 2
AIM = 3.0
CLIP = 0.03


def gnn_kernel(nc, x, adj, w1, w2, w3, u1_0, u1_1, u2_0, u2_1, gamma, beta, out):
    N, D = x.shape
    NT = -(-N // P)
    KB = D // P
    DA = w2.shape[0]
    LAST = N - (NT - 1) * P
    FULL = (NT - 1) * P
    NW = NT * P
    HALF = KB * D
    ALL_ROUNDS = -(-N // 8)
    FLOOR = (1 - TOP_P) * 0.999 / N
    SPAN = 1.001 / FLOOR

    def rows(i):
        return P if i < NT - 1 else LAST

    def span(i):
        return slice(i * P, i * P + rows(i))

    chunks = [(a, min(a + 512, N)) for a in range(0, N, 512)]

    ctx = ExitStack()
    with ctx:
        def sb(name, shape, dt=F32):
            return ctx.enter_context(nc.sbuf_tensor(name, shape, dt))

        def sem(name):
            return ctx.enter_context(nc.semaphore(name))

        def dram(name, shape, dt):
            return nc.dram_tensor(name, shape, dt, kind="Internal").ap()

        panels_d = dram("panels_d", (NT, P, 2 * NW), F32)
        ht_d = dram("ht_d", (NT, P, 2 * D), F32)
        xat_d = dram("xat_d", (NT, P, 2 * D), F32)
        g_d = dram("g_d", (N, 2, D), F32)
        h_d = dram("h_d", (N, D), F32)
        part_d = dram("part_d", (N, D), F32)
        part2_d = dram("part2_d", (N, D), F32)
        x1_d = dram("x1_d", (N, D), F32)

        E = sb("E", [P, NT * N])
        XA = sb("XA", [P, 2 * NT * D], F32R)
        XB = sb("XB", [P, 2 * NT * D], F32R)
        PAN = sb("PAN", [P, 4 * HALF], F32R)
        AR = sb("AR", [P, 2 * N])
        X = sb("X", [P, 2 * (N + 8)])
        Q = sb("Q", [P, N], F32R)
        TR = sb("TR", [P, 2 * 2 * D], F32R)
        STG = sb("STG", [P, 4 * D])
        ident_r = sb("ident_r", [P, P], F32R)
        ident2_r = sb("ident2_r", [P, P], F32R)
        ident = ident_r[:, :].bitcast(F32)
        state = sb("state", [P, 13 * NT])
        mask = sb("mask", [P, 2 * NT], U32)
        cand = sb("cand", [P, 8])
        take = sb("take", [P, 8])
        cum = sb("cum", [P, 9])
        flag = sb("flag", [P, 2])
        small = sb("small", [P, 16])
        stats = take[:, 0:6]
        turn = sb("turn", [P, 32], BF16)
        turned_flags = sb("turned_flags", [P, 32], BF16)

        S, T, lo, hi, m_lo, m_hi, t_try, m_try, nmax, rD, rowsum, colsum, rR = (
            state[:, k * NT:(k + 1) * NT] for k in range(13))
        lo_var, ln_rstd, ln_shift, up_f = nmax, m_hi, t_try, rD
        mean_var = state[:, 2 * NT:4 * NT]
        half_dinv = t_try
        dinv = S
        up, down = mask[:, 0:NT], mask[:, NT:2 * NT]

        def Et(i):
            return E[0:rows(i), i * N:(i + 1) * N]

        def xh(i):
            return E[0:rows(i), i * D:(i + 1) * D]

        def u1_raw(j):
            o = NT * D + j * HALF
            return E[:, o:o + HALF]

        def nat(buf, half, i):
            o = (half * NT + i) * D
            return buf[0:rows(i), o:o + D]

        def u1(j, half, k):
            o = (2 * j + half) * HALF + k * D
            return XB[:, o:o + D]

        KO = 4 * HALF

        def keys(half, a, b):
            o = KO + half * N
            return XB[:, o + a:o + b]

        def htl(slot):
            o = KO + slot * 2 * D
            return XB[:, o:o + 2 * D]

        def gst(half, i):
            o = KO + 4 * D + half * D
            return XB[0:rows(i), o:o + D]

        def pan(slot, half):
            o = (2 * slot + half) * NW
            return PAN[:, o:o + NW]

        WO = 4 * NW

        def wqk(which, half, k=None):
            o = WO + (2 * which + half) * D
            return PAN[:, o:o + D] if k is None else PAN[:, o + k * P:o + (k + 1) * P]

        def u2(j, half, k=None):
            o = (2 * j + half) * HALF
            return PAN[:, o:o + HALF] if k is None else PAN[:, o + k * D:o + (k + 1) * D]

        def tr(slot, half, k=None):
            o = (2 * slot + half) * D
            return TR[:, o:o + D] if k is None else TR[:, o + k * P:o + (k + 1) * P]

        def ar(i):
            return AR[0:rows(i), (i % 2) * N:(i % 2 + 1) * N]

        def xs(i, pad=False):
            o = (i % 2) * (N + 8)
            return X[0:rows(i), o:o + N + (8 if pad else 0)]

        def stg(slot, i=0):
            return STG[0:rows(i), slot * D:(slot + 1) * D]

        def row2(i):
            o = (i % 2) * NW
            return E[0:rows(i), o:o + N]

        def col2(i):
            o = (2 + i % 2) * NW
            return E[:, o:o + NW]

        draft_ident = X[:, 0:P]

        BIG = [ctx.enter_context(nc.psum_tensor(f"BIG{k}", [P, 3 * 512], F32)) for k in range(2)]
        ACC = [ctx.enter_context(nc.psum_tensor(f"ACC{k}", [P, 512], F32)) for k in range(2)]

        x_loaded = [sem(f"x_loaded{i}") for i in range(NT)]
        w_loaded = sem("w_loaded")
        u_loaded = sem("u_loaded")
        u2_loaded = sem("u2_loaded")
        adj_loaded = [sem(f"adj_loaded{k}") for k in range(2)]
        ht_loaded = [sem(f"ht_loaded{k}") for k in range(2)]
        xat_loaded = [sem(f"xat_loaded{k}") for k in range(2)]
        h_loaded = [sem(f"h_loaded{k}") for k in range(2)]
        g_loaded = sem("g_loaded")
        panel_loaded = [sem(f"panel_loaded{k}") for k in range(2)]
        part_loaded = [sem(f"part_loaded{k}") for k in range(2)]
        xin_loaded = [sem(f"xin_loaded{k}") for k in range(2)]
        gb_loaded = sem("gb_loaded")
        row2_loaded = [sem(f"row2_loaded{k}") for k in range(2)]
        x1_loaded = [sem(f"x1_loaded{k}") for k in range(2)]
        tr_stored = [sem(f"tr_stored{k}") for k in range(2)]
        h_stored = sem("h_stored")
        panel_stored = [sem(f"panel_stored{k}") for k in range(2)]
        g_stored = sem("g_stored")
        part_stored = [sem(f"part_stored{k}") for k in range(2)]
        part2_stored = [sem(f"part2_stored{k}") for k in range(2)]
        x1_stored = [sem(f"x1_stored{k}") for k in range(2)]
        out_stored = [sem(f"out_stored{k}") for k in range(2)]

        ident_zeroed = sem("ident_zeroed")
        ident_made = sem("ident_made")
        idents_r_made = sem("idents_r_made")
        zeroed = sem("zeroed")
        ln_var = sem("ln_var")
        ln_root = sem("ln_root")
        ln_scale = sem("ln_scale")
        h_made = sem("h_made")
        h_high = sem("h_high")
        h_low = sem("h_low")
        w1t_turned = sem("w1t_turned")
        w1t_copied = sem("w1t_copied")
        w12_made = sem("w12_made")
        wqk_high = sem("wqk_high")
        wqk_low = sem("wqk_low")
        u1_high = sem("u1_high")
        u1_low = sem("u1_low")
        u2_high = sem("u2_high")
        u2_low = sem("u2_low")
        turned = sem("turned")
        t_high = sem("t_high")
        t_low = sem("t_low")
        qk_made = sem("qk_made")
        qk_high = sem("qk_high")
        qk_low = sem("qk_low")
        logits_made = sem("logits_made")
        max_made = sem("max_made")
        exp_made = sem("exp_made")
        row_summed = sem("row_summed")
        rR_made = sem("rR_made")
        panel_turned = sem("panel_turned")
        panel_high = sem("panel_high")
        panel_low = sem("panel_low")
        product_made = sem("product_made")
        product_read = sem("product_read")
        g_made = sem("g_made")
        g_high = sem("g_high")
        g_low = sem("g_low")
        weights_made = sem("weights_made")
        flags_made = sem("flags_made")
        flags_joined = sem("flags_joined")
        v_made = sem("v_made")
        v_high = sem("v_high")
        v_low = sem("v_low")
        part_made = sem("part_made")
        rg_made = sem("rg_made")
        part2_made = sem("part2_made")
        dinv_root_in = sem("dinv_root_in")
        dinv_root = sem("dinv_root")
        y_var = sem("y_var")
        y_root = sem("y_root")
        y_scale = sem("y_scale")
        y_normed = sem("y_normed")
        x1_made = sem("x1_made")
        x1_var = sem("x1_var")
        x1_root = sem("x1_root")
        x1_scale = sem("x1_scale")
        w_normed = sem("w_normed")
        w_high = sem("w_high")
        w_low = sem("w_low")
        both_summed = sem("both_summed")
        y1_made = sem("y1_made")
        y1_high = sem("y1_high")
        y1_low = sem("y1_low")
        last_made = sem("last_made")
        out_made = sem("out_made")
        act_own = sem("act_own")
        dve_own = sem("dve_own")

        def uses(i):
            return i // 2 + 1

        def total(slot):
            return (NT - slot + 1) // 2

        def tr_stores(n):
            return sum(1 for m in range(n % 2, n + 1, 2) if m < NT or m >= 2 * NT)

        def bank(n):
            return n % 2 if n < NT else 1

        def tile_used(eng, n):
            if n < NT:
                eng.wait_ge(qk_made, n + 1)
            elif n < 2 * NT:
                eng.wait_ge(g_made, n - NT + 1)
            else:
                eng.wait_ge(qk_made, n - NT + 1)

        u1_first_tile = (NT * D) // N

        block = ctx.enter_context(nc.Block())

        @block.sync
        def _(sp):
            for i in range(NT):
                sp.dma_start(xh(i), x[span(i), :]).then_inc(x_loaded[i], 16)
                if i == 1:
                    sp.dma_start(stg(0)[:, 0:KB * DA].rearrange("p (k a) -> p k a", k=KB),
                                 w1.rearrange("(k p) a -> p k a", p=P)).then_inc(w_loaded, 16)
                    sp.dma_start(stg(1)[:, 0:KB * DA].rearrange("p (k a) -> p k a", k=KB),
                                 w3.rearrange("(k p) a -> p k a", p=P)).then_inc(w_loaded, 16)
                    sp.dma_start(stg(2)[0:DA, 0:DA], w2).then_inc(w_loaded, 16)
            for j, u in enumerate((u1_0, u1_1)):
                sp.dma_start(u1_raw(j).rearrange("p (k d) -> p k d", k=KB),
                             u.rearrange("(k p) d -> p k d", p=P)).then_inc(u_loaded, 16)
            for i in range(2):
                sp.dma_start(ar(i), adj[span(i), :]).then_inc(adj_loaded[i], 16)
            for i in range(NT):
                sp.wait_ge(h_made, i + 1)
                sp.dma_start(h_d[span(i), :], xh(i)).then_inc(h_stored, 16)
                sp.wait_ge(t_high, i + 1)
                sp.wait_ge(t_low, i + 1)
                sp.dma_start(ht_d[i], TR[:, (i % 2) * 2 * D:(i % 2 + 1) * 2 * D].bitcast(F32)).then_inc(tr_stored[i % 2], 16)

            def store_g(i):
                sp.wait_ge(g_high, i + 1)
                sp.wait_ge(g_low, i + 1)
                o = KO + 4 * D
                sp.dma_start(g_d[span(i)], XB[0:rows(i), o:o + 2 * D].bitcast(F32).rearrange("p (a d) -> p a d", a=2)
                             ).then_inc(g_stored, 16)

            def load_ht(i):
                if i >= 2:
                    sp.wait_ge(g_made, i - 1)
                sp.wait_ge(tr_stored[i % 2], 16 * uses(i))
                sp.dma_start(htl(i % 2).bitcast(F32), ht_d[i]).then_inc(ht_loaded[i % 2], 16)

            sp.wait_ge(logits_made, NT)
            load_ht(0)
            load_ht(1)
            for i in range(NT):
                if i + 2 < NT:
                    sp.wait_ge(panel_turned, i + 1)
                    sp.wait_ge(row_summed, i + 1)
                    sp.dma_start(ar(i + 2), adj[span(i + 2), :]).then_inc(adj_loaded[i % 2], 16)
                sp.wait_ge(panel_high, i + 1)
                sp.wait_ge(panel_low, i + 1)
                sp.dma_start(panels_d[i], PAN[:, (i % 2) * 2 * NW:(i % 2 + 1) * 2 * NW].bitcast(F32)).then_inc(panel_stored[i % 2], 16)
                if i >= 2:
                    store_g(i - 2)
                    if i < NT:
                        load_ht(i)

            store_g(NT - 2)
            store_g(NT - 1)

            sp.wait_ge(panel_turned, NT)
            sp.wait_ge(row_summed, NT)
            sp.dma_start(AR[:, 0:HALF].rearrange("p (k d) -> p k d", k=KB),
                         u2_0.rearrange("(k p) d -> p k d", p=P)).then_inc(u2_loaded, 16)
            for i in range(NT):
                n = 2 * NT + i
                sp.wait_ge(t_high, n + 1)
                sp.wait_ge(t_low, n + 1)
                sp.dma_start(xat_d[i], TR[:, (n % 2) * 2 * D:(n % 2 + 1) * 2 * D].bitcast(F32)).then_inc(tr_stored[n % 2], 16)

            def load_xat(i):
                n = 2 * NT + i
                if i < 2:
                    tile_used(sp, 3 * NT - 1)
                    sp.wait_ge(tr_stored[(3 * NT - 2) % 2], 16 * tr_stores(3 * NT - 2))
                    sp.wait_ge(tr_stored[(3 * NT - 1) % 2], 16 * tr_stores(3 * NT - 1))
                    sp.wait_ge(h_stored, 16 * NT)
                else:
                    sp.wait_ge(v_made, i - 1)
                sp.dma_start(TR[:, (i % 2) * 2 * D:(i % 2 + 1) * 2 * D].bitcast(F32), xat_d[i]).then_inc(xat_loaded[i % 2], 16)

            def load_h(i):
                if i >= 2:
                    sp.wait_ge(part_stored[i % 2], 16 * uses(i - 2))
                sp.dma_start(stg(i % 2, i), h_d[span(i), :]).then_inc(h_loaded[i % 2], 16)

            def load_g():
                sp.wait_ge(product_made, 2 * NT)
                sp.wait_ge(g_stored, 16 * NT)
                for half in range(2):
                    o = half * NT * D
                    sp.dma_start(XA[:, o:o + (NT - 1) * D].bitcast(F32).rearrange("p (t d) -> p t d", d=D),
                                 g_d[0:FULL, half, :].rearrange("(t p) d -> p t d", p=P)).then_inc(g_loaded, 16)
                    sp.dma_start(nat(XA, half, NT - 1).bitcast(F32), g_d[FULL:N, half, :]).then_inc(g_loaded, 16)

            load_xat(0)
            load_h(0)
            load_xat(1)
            load_h(1)
            sp.wait_ge(u2_high, 1)
            sp.wait_ge(u2_low, 1)
            sp.dma_start(AR[:, 0:HALF].rearrange("p (k d) -> p k d", k=KB),
                         u2_1.rearrange("(k p) d -> p k d", p=P)).then_inc(u2_loaded, 16)
            load_g()
            for i in range(NT):
                sp.wait_ge(part_made, i + 1)
                sp.dma_start(part_d[span(i), :], stg(i % 2, i)).then_inc(part_stored[i % 2], 16)
                if i + 2 < NT:
                    load_xat(i + 2)
                    load_h(i + 2)
            sp.wait_ge(u2_high, 2)
            sp.wait_ge(u2_low, 2)
            for j, v in enumerate((gamma, beta)):
                sp.dma_start(AR[:, j * D:(j + 1) * D],
                             v.partition_broadcast(P)).then_inc(gb_loaded, 16)

            def load_panel(i, free, count):
                sp.wait_ge(free, count)
                sp.wait_ge(panel_stored[i % 2], 16 * total(i % 2))
                sp.dma_start(PAN[:, (i % 2) * 2 * NW:(i % 2 + 1) * 2 * NW].bitcast(F32), panels_d[i]).then_inc(panel_loaded[i % 2], 16)

            def load_part(i):
                if i >= 2:
                    sp.wait_ge(part2_stored[i % 2], 16 * uses(i - 2))
                sp.wait_ge(part_stored[i % 2], 16 * uses(i))
                if i < 2:
                    sp.wait_ge(part_stored[i % 2], 16 * total(i % 2))
                sp.dma_start(stg(i % 2, i), part_d[span(i), :]).then_inc(part_loaded[i % 2], 16)

            for i in range(2):
                load_panel(i, v_made, NT)
                load_part(i)
            for i in range(NT):
                if i + 2 < NT:
                    load_panel(i + 2, rg_made, i + 1)
                sp.wait_ge(part2_made, i + 1)
                sp.dma_start(part2_d[span(i), :], stg(i % 2, i)).then_inc(part2_stored[i % 2], 16)
                if i + 2 < NT:
                    load_part(i + 2)

            def load_part2(i):
                if i < 2:
                    sp.wait_ge(part2_stored[i % 2], 16 * total(i % 2))
                else:
                    sp.wait_ge(x1_made, i - 1)
                sp.dma_start(stg(i % 2, i), part2_d[span(i), :]).then_inc(part_loaded[i % 2], 16)
                if i >= 2:
                    sp.wait_ge(x1_stored[i % 2], 16 * uses(i - 2))
                    sp.wait_ge(w_normed, i - 1)
                sp.dma_start(stg(2 + i % 2, i), x[span(i), :]).then_inc(xin_loaded[i % 2], 16)

            load_part2(0)
            load_part2(1)
            for i in range(NT):
                sp.wait_ge(x1_made, i + 1)
                sp.dma_start(x1_d[span(i), :], stg(2 + i % 2, i)).then_inc(x1_stored[i % 2], 16)
                if i + 2 < NT:
                    load_part2(i + 2)

            def load_row2(i):
                if i < 2:
                    sp.wait_ge(weights_made, NT + -(-4 * NW // N))
                else:
                    sp.wait_ge(panel_turned, 3 * NT + i - 1)
                    sp.wait_ge(panel_high, 3 * NT + i - 1)
                    sp.wait_ge(panel_low, 3 * NT + i - 1)
                sp.dma_start(row2(i), adj[span(i), :]).then_inc(row2_loaded[i % 2], 16)
                c = col2(i).rearrange("p (k c) -> p k c", c=P)
                sp.dma_start(c[:, 0:NT - 1, 0:rows(i)],
                             adj[0:FULL, span(i)].rearrange("(k p) c -> p k c", p=P)).then_inc(row2_loaded[i % 2], 16)
                sp.dma_start(c[0:LAST, NT - 1, 0:rows(i)], adj[FULL:N, span(i)]).then_inc(row2_loaded[i % 2], 16)

            load_row2(0)
            load_row2(1)
            for i in range(2, NT):
                load_row2(i)

            def load_x1(i):
                if i < 2:
                    sp.wait_ge(y1_low, NT)
                    sp.wait_ge(x1_stored[i % 2], 16 * total(i % 2))
                else:
                    sp.wait_ge(out_stored[i % 2], 16 * uses(i - 2))
                sp.dma_start(stg(i % 2, i), x1_d[span(i), :]).then_inc(x1_loaded[i % 2], 16)

            load_panel(0, product_made, 4 * NT - 1)
            load_panel(1, product_made, 4 * NT)
            load_x1(0)
            load_x1(1)
            for i in range(NT):
                if i + 2 < NT:
                    load_panel(i + 2, last_made, i + 1)
                sp.wait_ge(out_made, i + 1)
                sp.dma_start(out[span(i), :], stg(i % 2, i)).then_inc(out_stored[i % 2], 16)
                if i + 2 < NT:
                    load_x1(i + 2)
            for k in range(2):
                sp.wait_ge(out_stored[k], 16 * total(k))

        @block.gpsimd
        def _(pool):
            nc.gpsimd.memset(draft_ident, 0.0).then_inc(ident_zeroed, 1)
            pool.wait_ge(ident_zeroed, 1)
            nc.gpsimd.affine_select(out=draft_ident, in_=draft_ident, compare_op=ALU.not_equal, fill=1.0, base=0,
                                    pattern=[[-1, P]], channel_multiplier=1).then_inc(ident_made, 1)
            for m in range(2 * NT):
                pool.wait_ge(flags_made, m + 1)
                nc.gpsimd.partition_all_reduce(flag[:, 1:2], flag[:, 0:1], P, RMAX).then_inc(flags_joined, 1)

        @block.scalar
        def _(act):
            own = [0]

            def link(ins):
                own[0] += 1
                ins.then_inc(act_own, 1)
                act.wait_ge(act_own, own[0])

            act.wait_ge(w1t_turned, 1)
            nc.scalar.copy(STG[0:DA, 3 * D:4 * D], ACC[0][0:DA, :]).then_inc(w1t_copied, 1)
            act.wait_ge(w12_made, 1)
            for which, src in ((0, ACC[1][:, 0:KB * DA]), (1, stg(1)[:, 0:KB * DA])):
                for twin in range(2):
                    last = nc.scalar.copy(
                        wqk(which, 0).rearrange("p (k a) -> p k a", k=KB)[:, :, twin * DA:(twin + 1) * DA],
                        src.rearrange("p (k a) -> p k a", k=KB))
            last.then_inc(wqk_high, 1)

            act.wait_ge(ln_var, 1)
            nc.scalar.activation(m_lo, lo_var, ACT.Sqrt).then_inc(ln_root, 1)
            act.wait_ge(ln_scale, 1)

            def t_high_part(n):
                act.wait_ge(turned, n + 1)
                if n >= 2:
                    tile_used(act, n - 2)
                if n >= 2 and tr_stores(n - 2):
                    act.wait_ge(tr_stored[n % 2], 16 * tr_stores(n - 2))
                nc.scalar.copy(tr(n % 2, 0), ACC[bank(n)][:, :]).then_inc(t_high, 1)

            def qk_high_part(j):
                act.wait_ge(qk_made, j + 1)
                i = j % NT
                o = i * P
                c = rows(i)
                a = ACC[bank(j if j < NT else 2 * NT)]
                nc.scalar.copy(Q[:, o:o + c], a[:, 0:c])
                nc.scalar.copy(keys(0, o, o + c), a[:, P:P + c]).then_inc(qk_high, 1)

            for i in range(NT + 2):
                if i < NT:
                    nc.scalar.activation(xh(i), xh(i), ACT.Relu, bias=ln_shift[0:rows(i), i:i + 1],
                                         scale=ln_rstd[0:rows(i), i:i + 1]).then_inc(h_made, 1)
                    act.wait_ge(h_made, i + 1)
                    nc.scalar.copy(nat(XA, 0, i), xh(i)).then_inc(h_high, 1)
                if 1 <= i <= NT:
                    t_high_part(i - 1)
                if i >= 2:
                    qk_high_part(i - 2)

            def exps(s, i):
                act.wait_ge(max_made, NT * s + i + 1)
                R = rows(i)
                nc.scalar.activation(Et(i), BIG[i % 2][0:R, 0:N], ACT.Exp, bias=nmax[0:R, i:i + 1],
                                     accum_out=S[0:R, i:i + 1]).then_inc(exp_made, 1)

            for i in range(NT):
                if i == 0:
                    act.wait_ge(h_stored, 16 * NT)
                    act.wait_ge(h_low, NT)
                    act.wait_ge(turned, NT)
                    act.wait_ge(u_loaded, 32)
                    for j in range(2):
                        last = nc.scalar.copy(XB[:, 2 * j * HALF:(2 * j + 1) * HALF], u1_raw(j))
                    last.then_inc(u1_high, 1)
                if i == u1_first_tile:
                    act.wait_ge(u1_low, 1)
                exps(0, i)

            def row_sum(i):
                act.wait_ge(adj_loaded[i % 2], 16 * uses(i))
                R = rows(i)
                if i:
                    act.wait_ge(row_summed, i)
                nc.scalar.activation(X[0:R, N + 8:2 * N + 8], ar(i), ACT.Copy,
                                     accum_out=rowsum[0:R, i:i + 1]).then_inc(row_summed, 1)

            def panel_high_part(p):
                act.wait_ge(panel_turned, p + 1)
                if p >= 2:
                    act.wait_ge(product_made, p - 1)
                if 2 <= p < NT + 2:
                    act.wait_ge(panel_stored[p % 2], 16 * uses(p - 2))
                if p == 2 * NT:
                    act.wait_ge(rg_made, NT)
                nc.scalar.copy(pan(p % 2, 0), BIG[p % 2][:, 0:NW]).then_inc(panel_high, 1)

            def g_high_part(i):
                act.wait_ge(g_made, i + 1)
                if i >= 1:
                    act.wait_ge(g_stored, 16 * i)
                nc.scalar.copy(gst(0, i), ACC[1][0:rows(i), :]).then_inc(g_high, 1)

            def product_out(p, scale):
                i = p % NT
                act.wait_ge(product_made, p + 1)
                if p >= 2:
                    act.wait_ge(turned, NT + p - 1)
                nc.scalar.activation(stg(2 + p % 2, i), ACC[0][0:rows(i), :], ACT.Copy,
                                     scale=scale[0:rows(i), i:i + 1]).then_inc(product_read, 1)

            row_sum(0)
            panel_high_part(0)
            for i in range(NT):
                if i + 1 < NT:
                    row_sum(i + 1)
                    panel_high_part(i + 1)
                if i >= 1:
                    t_high_part(NT + i - 1)
                act.wait_ge(rR_made, i + 1)
                product_out(i, rR)
                if i >= 1:
                    g_high_part(i - 1)
            t_high_part(2 * NT - 1)
            g_high_part(NT - 1)

            panel_high_part(NT)
            for i in range(NT):
                if i + 1 < NT:
                    panel_high_part(NT + i + 1)
                if i >= 1:
                    t_high_part(2 * NT + i - 1)
                act.wait_ge(weights_made, i + 1)
                product_out(NT + i, rD)
                if i >= 1:
                    qk_high_part(NT + i - 1)
            t_high_part(3 * NT - 1)
            qk_high_part(2 * NT - 1)
            for i in range(NT):
                exps(1, i)

            for j in range(2):
                act.wait_ge(u2_loaded, 16 * (j + 1))
                if j == 0:
                    act.wait_ge(product_made, 2 * NT)
                    act.wait_ge(qk_made, 2 * NT)
                nc.scalar.copy(u2(j, 0), AR[:, 0:HALF]).then_inc(u2_high, 1)
            for i in range(NT):
                act.wait_ge(v_made, i + 1)
                nc.scalar.copy(nat(XB, 0, i), BIG[i % 2][0:rows(i), D:2 * D]).then_inc(v_high, 1)

            act.wait_ge(dinv_root_in, 1)
            nc.scalar.activation(colsum, rowsum, ACT.Sqrt).then_inc(dinv_root, 1)

            def y_root_of(i):
                act.wait_ge(y_var, i + 1)
                R = rows(i)
                nc.scalar.activation(small[0:R, 8:9], small[0:R, 2:3], ACT.Sqrt).then_inc(y_root, 1)

            def y_norm(i):
                act.wait_ge(y_scale, i + 1)
                R = rows(i)
                nc.scalar.activation(stg(i % 2, i), stg(i % 2, i), ACT.Identity, bias=small[0:R, 4:5],
                                     scale=small[0:R, 3:4]).then_inc(y_normed, 1)

            def x1_root_of(i):
                act.wait_ge(x1_var, i + 1)
                R = rows(i)
                nc.scalar.activation(small[0:R, 9:10], small[0:R, 12:13], ACT.Sqrt).then_inc(x1_root, 1)

            def wst(i):
                o = (2 + i % 2) * D
                return AR[0:rows(i), o:o + D]

            def w_parts(i):
                act.wait_ge(x1_scale, i + 1)
                if i >= 2:
                    act.wait_ge(w_low, i - 1)
                R = rows(i)
                nc.scalar.activation(wst(i), stg(2 + i % 2, i), ACT.Relu, bias=small[0:R, 14:15],
                                     scale=small[0:R, 13:14]).then_inc(w_normed, 1)
                act.wait_ge(w_normed, i + 1)
                act.wait_ge(rg_made, NT)
                nc.scalar.copy(nat(XA, 0, i), wst(i)).then_inc(w_high, 1)

            panel_high_part(2 * NT)
            for i in range(NT + 4):
                if i + 1 < NT:
                    panel_high_part(2 * NT + i + 1)
                if 0 <= i - 2 < NT:
                    y_norm(i - 2)
                if 0 <= i - 3 < NT:
                    w_parts(i - 3)
                if 0 <= i - 2 < NT:
                    x1_root_of(i - 2)
                if 0 <= i - 1 < NT:
                    y_root_of(i - 1)

            def sum_high_part(p):
                i = p - 3 * NT
                act.wait_ge(both_summed, i + 1)
                act.wait_ge(product_made, p - 1)
                nc.scalar.copy(pan(p % 2, 0), col2(i)).then_inc(panel_high, 1)

            def y1_part(i):
                act.wait_ge(product_made, 3 * NT + i + 1)
                if i >= 2:
                    act.wait_ge(y1_low, i - 1)
                else:
                    act.wait_ge(x1_stored[i % 2], 16 * total(i % 2))
                    act.wait_ge(x1_stored[1 - i % 2], 16 * total(1 - i % 2))
                R = rows(i)
                nc.scalar.activation(stg(2 + i % 2, i), ACC[(3 * NT + i) % 2][0:R, :], ACT.Copy,
                                     scale=half_dinv[0:R, i:i + 1]).then_inc(product_read, 1)
                act.wait_ge(product_read, 3 * NT + i + 1)
                nc.scalar.copy(nat(XB, 0, i), stg(2 + i % 2, i)).then_inc(y1_high, 1)

            sum_high_part(3 * NT)
            for i in range(NT):
                if i + 1 < NT:
                    sum_high_part(3 * NT + i + 1)
                y1_part(i)

        @block.vector
        def _(dve):
            own = [0]

            def link(ins):
                own[0] += 1
                ins.then_inc(dve_own, 1)
                dve.wait_ge(dve_own, own[0])

            nc.vector.memset(state[:, :], 1.0)
            nc.vector.memset(mask[:, :], 0)
            nc.vector.memset(small[:, :], 1.0)
            nc.vector.memset(flag[:, :], 0.0)
            nc.vector.memset(cum[:, :], 0.0)
            for k in range(2):
                nc.vector.memset(X[:, k * (N + 8) + N:(k + 1) * (N + 8)], 0.0)
            for a in BIG:
                nc.vector.memset(a[:, :], 0.0)
            nc.vector.memset(ACC[0][:, :], 0.0)
            nc.vector.memset(ACC[1][:, :], 0.0).then_inc(zeroed, 1)
            dve.wait_ge(zeroed, 1)
            dve.wait_ge(ident_made, 1)
            nc.vector.tensor_copy(ident_r[:], draft_ident)
            nc.vector.tensor_scalar(ident2_r[:], draft_ident, 2.0, None, ALU.mult).then_inc(idents_r_made, 1)

            dve.wait_ge(wqk_high, 1)
            for which, src in ((0, ACC[1][:, 0:KB * DA]), (1, stg(1)[:, 0:KB * DA])):
                for twin in range(2):
                    def part(half):
                        return wqk(which, half).rearrange("p (k a) -> p k a", k=KB)[:, :, twin * DA:(twin + 1) * DA]
                    last = nc.vector.tensor_tensor(part(1), src.rearrange("p (k a) -> p k a", k=KB),
                                                   part(0).bitcast(F32), ALU.subtract)
            last.then_inc(wqk_low, 1)

            def inverse_root(out_, a, root, t):
                link(nc.vector.reciprocal(out_, root))
                link(nc.vector.tensor_tensor(t, out_, out_, ALU.mult))
                link(nc.vector.tensor_tensor(t, t, a, ALU.mult))
                link(nc.vector.tensor_scalar(t, t, -0.5, 1.5, ALU.mult, ALU.add))
                link(nc.vector.tensor_tensor(out_, out_, t, ALU.mult))

            for i in range(NT):
                R = rows(i)
                dve.wait_ge(x_loaded[i], 16)
                link(nc.vector.bn_stats(small[0:R, 0:6], xh(i)))
                link(nc.vector.bn_aggr(mean_var[0:R, 2 * i:2 * i + 2], small[0:R, 0:6]))
            mv = mean_var.rearrange("p (t c) -> p c t", c=2)
            nc.vector.tensor_copy(ln_shift, mv[:, 0, :])
            nc.vector.tensor_scalar(lo_var, mv[:, 1, :], LAYER_EPS, None, ALU.add).then_inc(ln_var, 1)
            dve.wait_ge(ln_root, 1)
            inverse_root(ln_rstd, lo_var, m_lo, up_f)
            nc.vector.scalar_tensor_tensor(out=ln_shift, in0=ln_shift, scalar=-1.0, in1=ln_rstd,
                                           op0=ALU.mult, op1=ALU.mult).then_inc(ln_scale, 1)

            def t_low_part(n):
                dve.wait_ge(t_high, n + 1)
                nc.vector.tensor_tensor(tr(n % 2, 1), ACC[bank(n)][:, :], tr(n % 2, 0).bitcast(F32),
                                        ALU.subtract).then_inc(t_low, 1)

            def qk_low_part(j):
                dve.wait_ge(qk_high, j + 1)
                i = j % NT
                o, c = i * P, rows(i)
                a = ACC[bank(j if j < NT else 2 * NT)]
                nc.vector.tensor_tensor(Q[DA:P, o:o + c], a[DA:P, 0:c], Q[DA:P, o:o + c].bitcast(F32), ALU.subtract)
                nc.vector.tensor_tensor(keys(1, o, o + c), a[:, P:P + c], keys(0, o, o + c).bitcast(F32),
                                        ALU.subtract).then_inc(qk_low, 1)

            for i in range(NT + 2):
                if i < NT:
                    dve.wait_ge(h_high, i + 1)
                    nc.vector.tensor_tensor(nat(XA, 1, i), xh(i), nat(XA, 0, i).bitcast(F32),
                                            ALU.subtract).then_inc(h_low, 1)
                if 1 <= i <= NT:
                    t_low_part(i - 1)
                if i >= 2:
                    qk_low_part(i - 2)

            def row_max(s, i):
                dve.wait_ge(logits_made, NT * s + i + 1)
                R = rows(i)
                nc.vector.tensor_reduce(nmax[0:R, i:i + 1], BIG[i % 2][0:R, 0:N], AX.X, ALU.max,
                                        negate=True).then_inc(max_made, 1)

            for i in range(NT):
                row_max(0, i)
                if i == 2:
                    dve.wait_ge(u1_high, 1)
                    for j in range(2):
                        o = 2 * j * HALF
                        last = nc.vector.tensor_tensor(XB[:, o + HALF:o + 2 * HALF], u1_raw(j),
                                                       XB[:, o:o + HALF].bitcast(F32), ALU.subtract)
                    last.then_inc(u1_low, 1)

            def panel_low_part(p):
                dve.wait_ge(panel_high, p + 1)
                nc.vector.tensor_tensor(pan(p % 2, 1), BIG[p % 2][:, 0:NW], pan(p % 2, 0).bitcast(F32),
                                        ALU.subtract).then_inc(panel_low, 1)

            def column_sum(i):
                dve.wait_ge(panel_high, i + 1)
                c = BIG[i % 2][:, 0:NW].rearrange("p (k c) -> p k c", c=P)[:, :, 0:rows(i)]
                if i == 0:
                    link(nc.vector.tensor_reduce(colsum, c, AX.X, ALU.add))
                else:
                    link(nc.vector.tensor_reduce(up_f, c, AX.X, ALU.add))
                    link(nc.vector.tensor_tensor(colsum, colsum, up_f, ALU.add))

            def row_scale(i):
                dve.wait_ge(row_summed, i + 1)
                R = rows(i)
                link(nc.vector.tensor_scalar(rR[0:R, i:i + 1], rowsum[0:R, i:i + 1], 1.0, 1e-12, ALU.add, ALU.max))
                nc.vector.reciprocal(rR[0:R, i:i + 1], rR[0:R, i:i + 1]).then_inc(rR_made, 1)

            def g_low_part(i):
                dve.wait_ge(g_high, i + 1)
                nc.vector.tensor_tensor(gst(1, i), ACC[1][0:rows(i), :], gst(0, i).bitcast(F32),
                                        ALU.subtract).then_inc(g_low, 1)

            def rg1_step(i):
                if 0 <= i - 2 < NT:
                    g_low_part(i - 2)
                if 0 <= i + 1 < NT:
                    row_scale(i + 1)
                    column_sum(i + 1)
                    panel_low_part(i + 1)
                if 0 <= i - 1 < NT:
                    t_low_part(NT + i - 1)

            def u2_low_part(j):
                dve.wait_ge(u2_high, j + 1)
                nc.vector.tensor_tensor(u2(j, 1), AR[:, 0:HALF], u2(j, 0).bitcast(F32),
                                        ALU.subtract).then_inc(u2_low, 1)

            def v_step(i):
                dve.wait_ge(v_made, i + 1)
                dve.wait_ge(h_loaded[i % 2], 16 * uses(i))
                R = rows(i)
                nc.vector.tensor_tensor(stg(i % 2, i), BIG[i % 2][0:R, 0:D], stg(i % 2, i),
                                        ALU.add).then_inc(part_made, 1)
                dve.wait_ge(v_high, i + 1)
                nc.vector.tensor_tensor(nat(XB, 1, i), BIG[i % 2][0:R, D:2 * D], nat(XB, 0, i).bitcast(F32),
                                        ALU.subtract).then_inc(v_low, 1)

            def rg2_step(i):
                dve.wait_ge(rg_made, i + 1)
                dve.wait_ge(part_loaded[i % 2], 16 * uses(i))
                R = rows(i)
                nc.vector.scalar_tensor_tensor(out=stg(i % 2, i), in0=ACC[i % 2][0:R, :], scalar=rR[0:R, i:i + 1],
                                               in1=stg(i % 2, i), op0=ALU.mult, op1=ALU.add).then_inc(part2_made, 1)

            def evaluate(i):
                R = rows(i)
                evaluated.append(own[0] + 1)
                if len(evaluated) > 2:
                    dve.wait_ge(dve_own, evaluated[-3])
                nc.vector.scalar_tensor_tensor(out=scratch(len(evaluated))[0:R, :], in0=Et(i), scalar=t_try[0:R, i:i + 1], in1=Et(i),
                                               op0=ALU.is_gt, op1=ALU.mult,
                                               accum_out=m_try[0:R, i:i + 1]).then_inc(dve_own, 1)
                own[0] += 1

            evaluated = []

            def scratch(n):
                return X[:, 0:N].bitcast(BF16)[:, (n % 2) * N:(n % 2 + 1) * N]

            def narrow():
                dve.wait_ge(dve_own, own[0])
                link(nc.vector.tensor_tensor(up, m_try, T, ALU.is_ge))
                link(nc.vector.tensor_tensor(down, m_try, T, ALU.is_lt))
                nc.vector.copy_predicated(lo, up, t_try)
                nc.vector.copy_predicated(m_lo, up, m_try)
                nc.vector.copy_predicated(hi, down, t_try)
                link(nc.vector.copy_predicated(m_hi, down, m_try))

            def interpolate():
                link(nc.vector.scalar_tensor_tensor(out=t_try, in0=hi, scalar=-AIM, in1=T, op0=ALU.mult, op1=ALU.add))
                nc.vector.tensor_tensor(m_try, m_lo, m_hi, ALU.subtract)
                link(nc.vector.tensor_tensor(t_try, t_try, m_hi, ALU.subtract))
                link(nc.vector.reciprocal(m_try, m_try))
                link(nc.vector.tensor_tensor(t_try, t_try, m_try, ALU.mult))
                nc.vector.tensor_tensor(m_try, lo, hi, ALU.subtract)
                link(nc.vector.tensor_scalar(t_try, t_try, CLIP, 1 - CLIP, ALU.max, ALU.min))
                link(nc.vector.tensor_tensor(t_try, t_try, m_try, ALU.mult))
                link(nc.vector.tensor_tensor(t_try, t_try, hi, ALU.add))

            def search(s, between):
                dve.wait_ge(exp_made, NT * (s + 1))
                dve.wait_ge(panel_turned, 2 * NT * s) if s else None
                nc.vector.tensor_scalar(lo, S, FLOOR, None, ALU.mult)
                nc.vector.tensor_scalar(hi, S, FLOOR * SPAN, None, ALU.mult)
                nc.vector.tensor_scalar(T, S, TOP_P, None, ALU.mult)
                nc.vector.tensor_copy(m_lo, S)
                link(nc.vector.memset(m_hi, 0.0))
                ratio = SPAN
                n = 0
                for r in range(HALVINGS[s] + INTERPOLATIONS[s]):
                    if r < HALVINGS[s]:
                        ratio = ratio ** 0.5
                        link(nc.vector.tensor_scalar(t_try, lo, ratio, None, ALU.mult))
                    else:
                        interpolate()
                    for i in range(NT):
                        evaluate(i)
                        between(n)
                        n += 1
                    narrow()

            def round_of_eight(i, sync):
                R = rows(i)
                sync(nc.vector.max(cand[0:R, :], xs(i)))
                sync(nc.vector.tensor_tensor_scan(cum[0:R, 1:9], cand[0:R, :], cand[0:R, :], cum[0:R, 0:1],
                                                  ALU.add, ALU.max))
                sync(nc.vector.scalar_tensor_tensor(out=take[0:R, :], in0=cum[0:R, 0:8], scalar=T[0:R, i:i + 1],
                                                    in1=cand[0:R, :], op0=ALU.is_lt, op1=ALU.mult,
                                                    accum_out=small[0:R, 0:1]))
                nc.vector.tensor_copy(cum[0:R, 0:1], cum[0:R, 8:9])
                nc.vector.tensor_tensor(rD[0:R, i:i + 1], rD[0:R, i:i + 1], small[0:R, 0:1], ALU.add)
                sync(nc.vector.match_replace(xs(i, pad=True), take[0:R, :], xs(i, pad=True), 0.0))

            def choose(s, i):
                R = rows(i)
                p = NT * (1 + s) + i
                if i >= 2 or s:
                    dve.wait_ge(panel_turned, p - 1)
                if i == 1 and s == 0:
                    dve.wait_ge(row_summed, NT)
                nc.vector.tensor_copy(cum[0:R, 0:1], m_hi[0:R, i:i + 1])
                nc.vector.tensor_copy(rD[0:R, i:i + 1], m_hi[0:R, i:i + 1])
                if i == NT - 1:
                    nc.vector.memset(flag[:, 0:1], 0.0)
                link(nc.vector.scalar_tensor_tensor(out=xs(i), in0=Et(i), scalar=hi[0:R, i:i + 1], in1=Et(i),
                                                    op0=ALU.is_le, op1=ALU.mult))
                for _ in range(ROUNDS[s]):
                    round_of_eight(i, link)
                nc.vector.tensor_tensor(flag[0:R, 0:1], cum[0:R, 0:1], T[0:R, i:i + 1],
                                        ALU.is_lt).then_inc(flags_made, 1)

            def drained(ins):
                dve.drain()

            def weigh(s, i):
                R = rows(i)
                dve.wait_ge(flags_joined, NT * s + i + 1)
                short = dve.value_load(flag[0:1, 1:2].bitcast(I32), min_val=0, max_val=2 ** 30)
                with dve.If(short > 0):
                    with dve.Fori(0, MORE_ROUNDS):
                        round_of_eight(i, drained)
                    nc.vector.memset(turn[:, :], 0.0)
                    dve.drain()
                    nc.vector.tensor_tensor(turn[0:R, 0:1], cum[0:R, 0:1], T[0:R, i:i + 1], ALU.is_lt)
                    dve.drain()
                    nc.vector.transpose(turned_flags[:, :], turn[:, :])
                    dve.drain()
                    nc.vector.tensor_reduce(small[:, 1:2], turned_flags[:, :], AX.X, ALU.add)
                    dve.drain()
                    counts = [dve.value_load(small[q:q + 1, 1:2].bitcast(I32), min_val=0, max_val=2 ** 30)
                              for q in range(0, P, 32)]
                    for q in range(4):
                        with dve.If(counts[q] > 0):
                            with dve.Fori(0, ALL_ROUNDS):
                                round_of_eight(i, drained)
                            dve.drain()
                        dve.drain()
                link(nc.vector.reciprocal(rD[0:R, i:i + 1], rD[0:R, i:i + 1]))
                nc.vector.tensor_tensor(xs(i), Et(i), xs(i), ALU.subtract).then_inc(weights_made, 1)

            row_scale(0)
            column_sum(0)
            panel_low_part(0)
            every0 = NT * (HALVINGS[0] + INTERPOLATIONS[0]) // NT

            def between0(n):
                if n % every0 == 0 and n // every0 < NT:
                    rg1_step(n // every0)

            search(0, between0)

            choose(0, 0)
            rg1_step(NT)
            rg1_step(NT + 1)
            link(nc.vector.tensor_tensor(rowsum, colsum, rowsum, ALU.add))
            link(nc.vector.tensor_scalar(rowsum, rowsum, 0.5, 1.0, ALU.mult, ALU.add))
            weigh(0, 0)

            panel_low_part(NT)
            choose(0, 1)
            for i in range(NT):
                if i + 1 < NT:
                    weigh(0, i + 1)
                if i >= 2:
                    qk_low_part(NT + i - 2)
                if i + 2 < NT:
                    choose(0, i + 2)
                if i >= 1:
                    t_low_part(2 * NT + i - 1)
                if i + 1 < NT:
                    panel_low_part(NT + i + 1)
            qk_low_part(2 * NT - 2)
            t_low_part(3 * NT - 1)
            qk_low_part(2 * NT - 1)
            for i in range(NT):
                row_max(1, i)

            evals = NT * (HALVINGS[1] + INTERPOLATIONS[1])

            def between1(n):
                if n in (0, 2):
                    u2_low_part(n // 2)
                if n >= 4 and (n - 4) % 3 == 0 and (n - 4) // 3 < NT:
                    v_step((n - 4) // 3)
                m = n - 4 - 3 * NT
                if m >= 0 and m % 4 == 0 and m // 4 < NT:
                    rg2_step(m // 4)

            search(1, between1)
            for i in range(NT):
                if 4 + 3 * NT + 4 * i >= evals:
                    rg2_step(i)

            link(nc.vector.tensor_scalar(up_f, rowsum, 0.0, None, ALU.is_gt))
            link(nc.vector.tensor_scalar(rowsum, rowsum, 1e-30, None, ALU.max))
            nc.vector.tensor_copy(nmax, rowsum).then_inc(dinv_root_in, 1)
            dve.wait_ge(dinv_root, 1)
            inverse_root(dinv, rowsum, colsum, nmax)
            link(nc.vector.tensor_tensor(dinv, dinv, up_f, ALU.mult))
            link(nc.vector.tensor_scalar(half_dinv, dinv, 0.5, None, ALU.mult))

            def y_stats(i):
                R = rows(i)
                dve.wait_ge(product_made, 2 * NT + i + 1)
                dve.wait_ge(part_loaded[i % 2], 16 * (total(i % 2) + uses(i)))
                nc.vector.scalar_tensor_tensor(out=stg(i % 2, i), in0=ACC[i % 2][0:R, :], scalar=rD[0:R, i:i + 1],
                                               in1=stg(i % 2, i), op0=ALU.mult, op1=ALU.add).then_inc(product_read, 1)
                dve.wait_ge(product_read, 2 * NT + i + 1)
                link(nc.vector.bn_stats(stats[0:R, :], stg(i % 2, i)))
                link(nc.vector.bn_aggr(small[0:R, 6:8], stats[0:R, :]))
                nc.vector.tensor_scalar(small[0:R, 2:3], small[0:R, 7:8], LN_EPS, None, ALU.add).then_inc(y_var, 1)

            def y_scales(i):
                R = rows(i)
                dve.wait_ge(y_root, i + 1)
                inverse_root(small[0:R, 3:4], small[0:R, 2:3], small[0:R, 8:9], small[0:R, 5:6])
                nc.vector.scalar_tensor_tensor(out=small[0:R, 4:5], in0=small[0:R, 6:7], scalar=-1.0,
                                               in1=small[0:R, 3:4], op0=ALU.mult, op1=ALU.mult).then_inc(y_scale, 1)

            def x1_stats(i):
                R = rows(i)
                dve.wait_ge(y_normed, i + 1)
                if i == 0:
                    dve.wait_ge(gb_loaded, 32)
                y = stg(i % 2, i)
                xt = stg(2 + i % 2, i)
                dve.wait_ge(xin_loaded[i % 2], 16 * uses(i))
                link(nc.vector.tensor_tensor(y, y, AR[0:R, 0:D], ALU.mult))
                link(nc.vector.tensor_tensor(y, y, AR[0:R, D:2 * D], ALU.add))
                nc.vector.tensor_tensor(xt, xt, y, ALU.add).then_inc(x1_made, 1)
                dve.wait_ge(x1_made, i + 1)
                link(nc.vector.bn_stats(stats[0:R, :], xt))
                link(nc.vector.bn_aggr(small[0:R, 10:12], stats[0:R, :]))
                nc.vector.tensor_scalar(small[0:R, 12:13], small[0:R, 11:12], LAYER_EPS, None,
                                        ALU.add).then_inc(x1_var, 1)

            def x1_scales(i):
                R = rows(i)
                dve.wait_ge(x1_root, i + 1)
                if i >= 1:
                    dve.wait_ge(w_normed, i)
                inverse_root(small[0:R, 13:14], small[0:R, 12:13], small[0:R, 9:10], small[0:R, 5:6])
                link(nc.vector.tensor_tensor(small[0:R, 13:14], small[0:R, 13:14], dinv[0:R, i:i + 1], ALU.mult))
                nc.vector.scalar_tensor_tensor(out=small[0:R, 14:15], in0=small[0:R, 10:11], scalar=-1.0,
                                               in1=small[0:R, 13:14], op0=ALU.mult, op1=ALU.mult).then_inc(x1_scale, 1)

            def w_low_part(i):
                o = (2 + i % 2) * D
                dve.wait_ge(w_high, i + 1)
                nc.vector.tensor_tensor(nat(XA, 1, i), AR[0:rows(i), o:o + D], nat(XA, 0, i).bitcast(F32),
                                        ALU.subtract).then_inc(w_low, 1)

            choose(1, 0)
            weigh(1, 0)
            choose(1, 1)
            panel_low_part(2 * NT)
            for i in range(NT + 4):
                if i + 1 < NT:
                    weigh(1, i + 1)
                if 0 <= i - 2 < NT:
                    y_scales(i - 2)
                if 0 <= i - 3 < NT:
                    x1_scales(i - 3)
                if i + 2 < NT:
                    choose(1, i + 2)
                if 0 <= i - 2 < NT:
                    x1_stats(i - 2)
                if i + 1 < NT:
                    panel_low_part(2 * NT + i + 1)
                if 0 <= i - 3 < NT:
                    w_low_part(i - 3)
                if 0 <= i - 1 < NT:
                    y_stats(i - 1)

            def both(i):
                p = 3 * NT + i
                dve.wait_ge(panel_turned, p + 1)
                dve.wait_ge(row2_loaded[i % 2], 48 * uses(i))
                c = col2(i).rearrange("p (k c) -> p k c", c=P)
                b = BIG[p % 2][:, 0:NW].rearrange("p (k c) -> p k c", c=P)
                R = rows(i)
                nc.vector.tensor_tensor(c[:, 0:NT - 1, 0:R], b[:, 0:NT - 1, 0:R], c[:, 0:NT - 1, 0:R], ALU.add)
                nc.vector.tensor_tensor(c[0:LAST, NT - 1, 0:R], b[0:LAST, NT - 1, 0:R], c[0:LAST, NT - 1, 0:R],
                                        ALU.add).then_inc(both_summed, 1)
                dve.wait_ge(panel_high, p + 1)
                nc.vector.tensor_tensor(pan(p % 2, 1), col2(i), pan(p % 2, 0).bitcast(F32),
                                        ALU.subtract).then_inc(panel_low, 1)

            def y1_low_part(i):
                dve.wait_ge(y1_high, i + 1)
                nc.vector.tensor_tensor(nat(XB, 1, i), stg(2 + i % 2, i), nat(XB, 0, i).bitcast(F32),
                                        ALU.subtract).then_inc(y1_low, 1)

            both(0)
            for i in range(NT):
                if i + 1 < NT:
                    both(i + 1)
                y1_low_part(i)

            for i in range(NT):
                dve.wait_ge(last_made, i + 1)
                dve.wait_ge(x1_loaded[i % 2], 16 * uses(i))
                nc.vector.tensor_tensor(stg(i % 2, i), ACC[i % 2][0:rows(i), :], stg(i % 2, i),
                                        ALU.add).then_inc(out_made, 1)

        @block.tensor
        def _(pe):
            PASSES = ((0, 0), (0, 1), (1, 0))

            pe.wait_ge(idents_r_made, 1)
            pe.wait_ge(zeroed, 1)
            pe.wait_ge(w_loaded, 48)
            for k in range(KB):
                last = nc.tensor.transpose(ACC[0][0:DA, k * P:(k + 1) * P], stg(0)[:, k * DA:(k + 1) * DA], ident)
            last.then_inc(w1t_turned, 1)
            pe.wait_ge(w1t_copied, 1)
            for k in range(KB):
                last = nc.tensor.matmul(ACC[1][:, k * DA:(k + 1) * DA], STG[0:DA, 3 * D + k * P:3 * D + (k + 1) * P],
                                        stg(2)[0:DA, 0:DA], start=True, stop=True)
            last.then_inc(w12_made, 1)
            pe.wait_ge(wqk_low, 1)

            def turn_tile(n, src, i):
                R = rows(i)
                for k in range(KB):
                    last = nc.tensor.transpose(ACC[bank(n)][:, k * P:k * P + R], src[:, k * P:(k + 1) * P],
                                               ident[0:R, 0:R])
                last.then_inc(turned, 1)

            def project(j, n):
                pe.wait_ge(t_high, n + 1)
                pe.wait_ge(t_low, n + 1)
                c = rows(j % NT)
                a = ACC[bank(n)]
                for which in range(2):
                    m = 0
                    for wh, th in PASSES:
                        for k in range(KB):
                            last = nc.tensor.matmul(a[:, which * P:which * P + c], wqk(which, wh, k),
                                                    tr(n % 2, th, k)[:, 0:c], start=(m == 0),
                                                    stop=(m == 3 * KB - 1))
                            m += 1
                last.then_inc(qk_made, 1)
                
            for i in range(NT + 1):
                if i < NT:
                    pe.wait_ge(h_made, i + 1)
                    if i >= 2:
                        pe.wait_ge(qk_low, i - 1)
                    turn_tile(i, xh(i), i)
                if i >= 1:
                    project(i - 1, i - 1)

            def logits(s, i):
                pe.wait_ge(qk_low, NT * (s + 1))
                if i >= 2:
                    pe.wait_ge(exp_made, NT * s + i - 1)
                elif s == 1:
                    pe.wait_ge(panel_low, 2 * NT)
                R = rows(i)
                for a, b in chunks:
                    for half in range(2):
                        last = nc.tensor.matmul(BIG[i % 2][0:R, a:b], Q[:, i * P:i * P + R], keys(half, a, b),
                                                start=(half == 0), stop=(half == 1))
                last.then_inc(logits_made, 1)

            for i in range(NT):
                logits(0, i)

            def turn_panel(p, src):
                R = rows(p % NT)
                for k in range(NT):
                    c = rows(k)
                    last = nc.tensor.transpose(BIG[p % 2][0:c, k * P:k * P + R], src[:, k * P:k * P + c],
                                               ident[0:R, 0:R])
                last.then_inc(panel_turned, 1)

            def graph_product(i, slot, rhs, acc, also=None):
                R = rows(i)
                m = 0
                n = 3 * NT + (2 if also is not None else 0)
                if also is not None:
                    for half in range(2):
                        nc.tensor.matmul(acc[0:R, :], also[0:R, 0:R], nat(rhs, half, i), start=(m == 0), stop=False)
                        m += 1
                for k in range(NT):
                    c = rows(k)
                    for ph, rh in PASSES:
                        last = nc.tensor.matmul(acc[0:R, :], pan(slot, ph)[0:c, k * P:k * P + R], nat(rhs, rh, k),
                                                start=(m == 0), stop=(m == n - 1))
                        m += 1
                return last

            def g_tile(i):
                n = NT + i
                pe.wait_ge(t_high, n + 1)
                pe.wait_ge(t_low, n + 1)
                pe.wait_ge(ht_loaded[i % 2], 16 * uses(i))
                R = rows(i)
                m = 0
                for j in range(2):
                    for th, uh in PASSES:
                        for k in range(KB):
                            o = th * D + k * P
                            lhs = htl(i % 2)[:, o:o + P] if j == 0 else tr(n % 2, th, k)
                            last = nc.tensor.matmul(ACC[1][0:R, :], lhs[:, 0:R], u1(j, uh, k), start=(m == 0),
                                                    stop=(m == 6 * KB - 1))
                            m += 1
                last.then_inc(g_made, 1)

            def panel_of_adj(i):
                pe.wait_ge(adj_loaded[i % 2], 16 * uses(i))
                if i < 2:
                    pe.wait_ge(exp_made, NT)
                else:
                    pe.wait_ge(panel_high, i - 1)
                    pe.wait_ge(panel_low, i - 1)
                turn_panel(i, ar(i))

            def turn_product(n, i):
                pe.wait_ge(product_read, n - NT + 1)
                turn_tile(n, stg(2 + (n - NT) % 2, i), i)

            panel_of_adj(0)
            for i in range(NT):
                if i + 1 < NT:
                    panel_of_adj(i + 1)
                if i >= 1:
                    if i >= 2:
                        pe.wait_ge(g_low, i - 1)
                    turn_product(NT + i - 1, i - 1)
                pe.wait_ge(panel_high, i + 1)
                pe.wait_ge(panel_low, i + 1)
                pe.wait_ge(product_read, i) if i else None
                graph_product(i, i % 2, XA, ACC[0], also=ident_r).then_inc(product_made, 1)
                if i == 1:
                    pe.wait_ge(u1_low, 1)
                if i >= 1:
                    g_tile(i - 1)
            pe.wait_ge(g_low, NT - 1)
            turn_product(2 * NT - 1, NT - 1)
            g_tile(NT - 1)

            def panel_of_weights(p):
                i = p % NT
                pe.wait_ge(weights_made, p - NT + 1)
                if i >= 2 or p < 2 * NT:
                    pe.wait_ge(panel_high, p - 1)
                    pe.wait_ge(panel_low, p - 1)
                else:
                    pe.wait_ge(part_made, NT)
                    pe.wait_ge(v_low, NT)
                turn_panel(p, xs(i))

            panel_of_weights(NT)
            for i in range(NT):
                if i + 1 < NT:
                    panel_of_weights(NT + i + 1)
                if i >= 1:
                    if i == 1:
                        pe.wait_ge(g_low, NT)
                    else:
                        pe.wait_ge(qk_low, NT + i - 1)
                    turn_product(2 * NT + i - 1, i - 1)
                pe.wait_ge(panel_high, NT + i + 1)
                pe.wait_ge(panel_low, NT + i + 1)
                pe.wait_ge(product_read, NT + i)
                graph_product(i, (NT + i) % 2, XA, ACC[0]).then_inc(product_made, 1)
                if i >= 1:
                    project(NT + i - 1, 2 * NT + i - 1)
            pe.wait_ge(qk_low, 2 * NT - 1)
            turn_product(3 * NT - 1, NT - 1)
            project(2 * NT - 1, 3 * NT - 1)

            for i in range(NT):
                logits(1, i)

            pe.wait_ge(u2_high, 2)
            pe.wait_ge(u2_low, 2)
            for i in range(NT):
                R = rows(i)
                pe.wait_ge(xat_loaded[i % 2], 16 * uses(i))
                if i < 2:
                    pe.wait_ge(exp_made, 2 * NT)
                else:
                    pe.wait_ge(part_made, i - 1)
                    pe.wait_ge(v_low, i - 1)
                for j in range(2):
                    m = 0
                    for th, uh in PASSES:
                        for k in range(KB):
                            last = nc.tensor.matmul(BIG[i % 2][0:R, j * D:(j + 1) * D], tr(i % 2, th, k)[:, 0:R],
                                                    u2(j, uh, k), start=(m == 0), stop=(m == 3 * KB - 1))
                            m += 1
                last.then_inc(v_made, 1)

            pe.wait_ge(g_loaded, 64)
            pe.wait_ge(product_read, 2 * NT)
            for i in range(NT):
                pe.wait_ge(panel_loaded[i % 2], 16 * uses(i))
                if i >= 2:
                    pe.wait_ge(part2_made, i - 1)
                graph_product(i, i % 2, XA, ACC[i % 2], also=ident_r).then_inc(rg_made, 1)

            panel_of_weights(2 * NT)
            for i in range(NT):
                p = 2 * NT + i
                if i + 1 < NT:
                    panel_of_weights(p + 1)
                pe.wait_ge(panel_high, p + 1)
                pe.wait_ge(panel_low, p + 1)
                if i < 2:
                    pe.wait_ge(part2_made, NT)
                else:
                    pe.wait_ge(product_read, p - 1)
                graph_product(i, p % 2, XB, ACC[i % 2]).then_inc(product_made, 1)

            def panel_of_adj2(i):
                pe.wait_ge(row2_loaded[i % 2], 48 * uses(i))
                if i < 2:
                    pe.wait_ge(panel_low, 3 * NT)
                    pe.wait_ge(panel_high, 3 * NT)
                else:
                    pe.wait_ge(both_summed, i - 1)
                turn_panel(3 * NT + i, row2(i))

            panel_of_adj2(0)
            for i in range(NT):
                p = 3 * NT + i
                if i + 1 < NT:
                    panel_of_adj2(i + 1)
                pe.wait_ge(panel_high, p + 1)
                pe.wait_ge(panel_low, p + 1)
                pe.wait_ge(product_read, p - 1)
                if i == 0:
                    pe.wait_ge(w_high, NT)
                    pe.wait_ge(w_low, NT)
                graph_product(i, p % 2, XA, ACC[p % 2], also=ident2_r).then_inc(product_made, 1)

            pe.wait_ge(y1_high, NT)
            pe.wait_ge(y1_low, NT)
            for i in range(NT):
                pe.wait_ge(panel_loaded[i % 2], 16 * (total(i % 2) + uses(i)))
                if i >= 2:
                    pe.wait_ge(out_made, i - 1)
                graph_product(i, i % 2, XB, ACC[i % 2]).then_inc(last_made, 1)


_INS = ['x', 'adj', 'L0_gnn_W1', 'L0_gnn_W2', 'L0_gnn_W3', 'L0_gnn_U1_0', 'L0_gnn_U1_1', 'L0_gnn_U2_0',
        'L0_gnn_U2_1', 'L0_gnn_gamma', 'L0_gnn_beta']


def kernel(**inputs):
    import numpy as _np
    import concourse.bacc as _bacc
    from concourse import mybir as _mybir
    from concourse.bass_utils import run_bass_kernel_spmd as _run

    nc = _bacc.Bacc("TRN2", target_bir_lowering=False, num_devices=1, dynamic_dma_scratch_size=1024)
    arrays, args = {}, []
    for name in _INS:
        a = _np.ascontiguousarray(inputs[name])
        arrays[f"in_{name}_dram"] = a
        args.append(nc.dram_tensor(f"in_{name}_dram", a.shape, _mybir.dt.from_np(a.dtype), kind="ExternalInput").ap())
    shape = inputs['x'].shape
    args.append(nc.dram_tensor("out_0_dram", shape, _mybir.dt.float32, kind="ExternalOutput").ap())
    gnn_kernel(nc, *args)
    r = _run(nc, [arrays], core_ids=[0])
    return r.results[0]["out_0_dram"]
```

```python
from contextlib import ExitStack

import concourse.bass as bass
from concourse import mybir

F32 = mybir.dt.float32
F32R = mybir.dt.float32r
BF16 = mybir.dt.bfloat16
I32 = mybir.dt.int32
U32 = mybir.dt.uint32
ALU = mybir.AluOpType
ACT = mybir.ActivationFunctionType
AX = mybir.AxisListType
RMAX = bass.bass_isa.ReduceOp.max

P = 128
TOP_P = 0.9
LN_EPS = 1e-5
LAYER_EPS = 1e-5
HALVINGS = (3, 4)
AIMS = ((3.0, 3.0), (5.0, 4.0, 3.0))
ROUNDS = (1, 2)
MORE_ROUNDS = 2
CLIP = 0.03


def gnn_kernel(nc, x, adj, w1, w2, w3, u1_0, u1_1, u2_0, u2_1, gamma, beta, out):
    N, D = x.shape
    NT = -(-N // P)
    KB = D // P
    DA = w2.shape[0]
    LAST = N - (NT - 1) * P
    FULL = (NT - 1) * P
    NW = NT * P
    HALF = KB * D
    ALL_ROUNDS = -(-N // 8)
    FLOOR = (1 - TOP_P) * 0.999 / N
    CEILING = 1.001

    BT = 512 // P
    NB = -(-NT // BT)

    def batch(b):
        return range(b * BT, min((b + 1) * BT, NT))

    def rows(i):
        return P if i < NT - 1 else LAST

    def span(i):
        return slice(i * P, i * P + rows(i))

    chunks = [(a, min(a + 512, N)) for a in range(0, N, 512)]

    ctx = ExitStack()
    with ctx:
        def sb(name, shape, dt=F32):
            return ctx.enter_context(nc.sbuf_tensor(name, shape, dt))

        def sem(name):
            return ctx.enter_context(nc.semaphore(name))

        def dram(name, shape, dt):
            return nc.dram_tensor(name, shape, dt, kind="Internal").ap()

        panels_d = dram("panels_d", (NT, P, 2 * NW), F32)
        ht_d = dram("ht_d", (NT, P, 2 * D), F32)
        xat_d = dram("xat_d", (NT, P, 2 * D), F32)
        g_d = dram("g_d", (N, 2, D), F32)
        h_d = dram("h_d", (N, D), F32)
        part_d = dram("part_d", (N, D), F32)
        part2_d = dram("part2_d", (N, D), F32)
        x1_d = dram("x1_d", (N, D), F32)

        E = sb("E", [P, NT * N])
        XA = sb("XA", [P, 2 * NT * D], F32R)
        XB = sb("XB", [P, 2 * NT * D], F32R)
        PAN = sb("PAN", [P, 4 * HALF], F32R)
        AR = sb("AR", [P, 2 * N])
        X = sb("X", [P, 2 * (N + 8)])
        Q = sb("Q", [P, N], F32R)
        TR = sb("TR", [P, 2 * 2 * D], F32R)
        STG = sb("STG", [P, 4 * D])
        ident_r = sb("ident_r", [P, P], F32R)
        ident2_r = sb("ident2_r", [P, P], F32R)
        ident = ident_r[:, :].bitcast(F32)
        state = sb("state", [P, 13 * NT])
        mask = sb("mask", [P, 2 * NT], U32)
        cand = sb("cand", [P, 8])
        take = sb("take", [P, 8])
        cum = sb("cum", [P, 9])
        flag = sb("flag", [P, 2])
        small = sb("small", [P, 16])
        stats = take[:, 0:6]
        turn = sb("turn", [P, 32], BF16)
        turned_flags = sb("turned_flags", [P, 32], BF16)

        S, T, lo, hi, m_lo, m_hi, t_try, m_try, nmax, rD, rowsum, colsum, rR = (
            state[:, k * NT:(k + 1) * NT] for k in range(13))
        lo_var, ln_rstd, ln_shift, up_f = nmax, m_hi, t_try, rD
        mean_var = state[:, 2 * NT:4 * NT]
        half_dinv = t_try
        dinv = S
        up, down = mask[:, 0:NT], mask[:, NT:2 * NT]

        def Et(i):
            return E[0:rows(i), i * N:(i + 1) * N]

        def xh(i):
            return E[0:rows(i), i * D:(i + 1) * D]

        def u1_raw(j):
            o = NT * D + j * HALF
            return E[:, o:o + HALF]

        def nat(buf, half, i):
            o = (half * NT + i) * D
            return buf[0:rows(i), o:o + D]

        def u1(j, half, k):
            o = (2 * j + half) * HALF + k * D
            return XB[:, o:o + D]

        def ht(i, half):
            o = (i // BT % 2) * 2 * BT * D + half * BT * D
            return XB[:, o:o + BT * D].rearrange("p (k t c) -> p t k c", k=KB, t=BT)[:, i % BT]

        def ht_batch(b, half, k, c):
            o = (b % 2) * 2 * BT * D + half * BT * D + k * BT * P
            return XB[:, o:o + c]

        KO = 4 * HALF

        def keys(half, a, b):
            o = KO + half * N
            return XB[:, o + a:o + b]

        def htl(slot):
            o = KO + slot * 2 * D
            return XB[:, o:o + 2 * D]

        def gst(half, i):
            o = KO + 4 * D + half * D
            return XB[0:rows(i), o:o + D]

        def pan(slot, half):
            o = (2 * slot + half) * NW
            return PAN[:, o:o + NW]

        WO = 4 * NW

        def wqk(which, half, k=None):
            o = WO + (2 * which + half) * D
            return PAN[:, o:o + D] if k is None else PAN[:, o + k * P:o + (k + 1) * P]

        def u2(j, half, k=None):
            o = (2 * j + half) * HALF
            return PAN[:, o:o + HALF] if k is None else PAN[:, o + k * D:o + (k + 1) * D]

        def tr(slot, half, k=None):
            o = (2 * slot + half) * D
            return TR[:, o:o + D] if k is None else TR[:, o + k * P:o + (k + 1) * P]

        def ar(i):
            return AR[0:rows(i), (i % 2) * N:(i % 2 + 1) * N]

        def xs(i, pad=False):
            o = (i % 2) * (N + 8)
            return X[0:rows(i), o:o + N + (8 if pad else 0)]

        def stg(slot, i=0):
            return STG[0:rows(i), slot * D:(slot + 1) * D]

        def row2(i):
            o = (i % 2) * NW
            return E[0:rows(i), o:o + N]

        def col2(i):
            o = (2 + i % 2) * NW
            return E[:, o:o + NW]

        draft_ident = X[:, 0:P]

        BIG = [ctx.enter_context(nc.psum_tensor(f"BIG{k}", [P, 3 * 512], F32)) for k in range(2)]
        ACC = [ctx.enter_context(nc.psum_tensor(f"ACC{k}", [P, 512], F32)) for k in range(2)]

        x_loaded = [sem(f"x_loaded{i}") for i in range(NT)]
        w_loaded = sem("w_loaded")
        u_loaded = sem("u_loaded")
        u2_loaded = sem("u2_loaded")
        adj_loaded = [sem(f"adj_loaded{k}") for k in range(2)]
        ht_loaded = [sem(f"ht_loaded{k}") for k in range(2)]
        xat_loaded = [sem(f"xat_loaded{k}") for k in range(2)]
        h_loaded = [sem(f"h_loaded{k}") for k in range(2)]
        g_loaded = sem("g_loaded")
        panel_loaded = [sem(f"panel_loaded{k}") for k in range(2)]
        part_loaded = [sem(f"part_loaded{k}") for k in range(2)]
        xin_loaded = [sem(f"xin_loaded{k}") for k in range(2)]
        gb_loaded = sem("gb_loaded")
        row2_loaded = [sem(f"row2_loaded{k}") for k in range(2)]
        x1_loaded = [sem(f"x1_loaded{k}") for k in range(2)]
        ht_stored = [sem(f"ht_stored{k}") for k in range(2)]
        tr_stored = [sem(f"tr_stored{k}") for k in range(2)]
        h_stored = sem("h_stored")
        panel_stored = [sem(f"panel_stored{k}") for k in range(2)]
        g_stored = sem("g_stored")
        part_stored = [sem(f"part_stored{k}") for k in range(2)]
        part2_stored = [sem(f"part2_stored{k}") for k in range(2)]
        x1_stored = [sem(f"x1_stored{k}") for k in range(2)]
        out_stored = [sem(f"out_stored{k}") for k in range(2)]

        ident_zeroed = sem("ident_zeroed")
        ident_made = sem("ident_made")
        idents_r_made = sem("idents_r_made")
        zeroed = sem("zeroed")
        big_zeroed = sem("big_zeroed")
        ln_var = sem("ln_var")
        ln_root = sem("ln_root")
        ln_scale = sem("ln_scale")
        h_made = sem("h_made")
        h_high = sem("h_high")
        h_low = sem("h_low")
        w1t_turned = sem("w1t_turned")
        w1t_copied = sem("w1t_copied")
        w12_made = sem("w12_made")
        wqk_high = sem("wqk_high")
        wqk_low = sem("wqk_low")
        u1_high = sem("u1_high")
        u1_low = sem("u1_low")
        u2_high = sem("u2_high")
        u2_low = sem("u2_low")
        turned = sem("turned")
        t_high = sem("t_high")
        t_low = sem("t_low")
        qk_made = sem("qk_made")
        qk_high = sem("qk_high")
        qk_low = sem("qk_low")
        logits_made = sem("logits_made")
        max_made = sem("max_made")
        exp_made = sem("exp_made")
        row_summed = sem("row_summed")
        rR_made = sem("rR_made")
        panel_turned = sem("panel_turned")
        panel_high = sem("panel_high")
        panel_low = sem("panel_low")
        product_made = sem("product_made")
        product_read = sem("product_read")
        g_made = sem("g_made")
        g_high = sem("g_high")
        g_low = sem("g_low")
        weights_made = sem("weights_made")
        flags_made = sem("flags_made")
        flags_joined = sem("flags_joined")
        v_made = sem("v_made")
        v_high = sem("v_high")
        v_low = sem("v_low")
        part_made = sem("part_made")
        rg_made = sem("rg_made")
        part2_made = sem("part2_made")
        dinv_root_in = sem("dinv_root_in")
        dinv_root = sem("dinv_root")
        y_var = sem("y_var")
        y_root = sem("y_root")
        y_scale = sem("y_scale")
        y_normed = sem("y_normed")
        x1_made = sem("x1_made")
        x1_var = sem("x1_var")
        x1_root = sem("x1_root")
        x1_scale = sem("x1_scale")
        w_normed = sem("w_normed")
        w_high = sem("w_high")
        w_low = sem("w_low")
        both_summed = sem("both_summed")
        y1_made = sem("y1_made")
        y1_high = sem("y1_high")
        y1_low = sem("y1_low")
        last_made = sem("last_made")
        out_made = sem("out_made")
        act_own = sem("act_own")
        dve_own = sem("dve_own")
        pool_own = sem("pool_own")
        taken = sem("taken")

        def uses(i):
            return i // 2 + 1

        def total(slot):
            return (NT - slot + 1) // 2

        def tr_stores(n):
            return sum(1 for m in range(n % 2, n + 1, 2) if m >= 2 * NT)

        def qk_count(i):
            return NB + i + 1

        def bank(n):
            return n % 2 if n < NT else 1

        def tile_used(eng, n):
            if n < 2 * NT:
                eng.wait_ge(g_made, n - NT + 1)
            else:
                eng.wait_ge(qk_made, qk_count(n - 2 * NT))

        u1_first_tile = (NT * D) // N

        block = ctx.enter_context(nc.Block())

        @block.sync
        def _(sp):
            for i in range(NT):
                sp.dma_start(xh(i), x[span(i), :]).then_inc(x_loaded[i], 16)
                if i == 1:
                    sp.dma_start(stg(0)[:, 0:KB * DA].rearrange("p (k a) -> p k a", k=KB),
                                 w1.rearrange("(k p) a -> p k a", p=P)).then_inc(w_loaded, 16)
                    sp.dma_start(stg(1)[:, 0:KB * DA].rearrange("p (k a) -> p k a", k=KB),
                                 w3.rearrange("(k p) a -> p k a", p=P)).then_inc(w_loaded, 16)
                    sp.dma_start(stg(2)[0:DA, 0:DA], w2).then_inc(w_loaded, 16)
            for j, u in enumerate((u1_0, u1_1)):
                sp.dma_start(u1_raw(j).rearrange("p (k d) -> p k d", k=KB),
                             u.rearrange("(k p) d -> p k d", p=P)).then_inc(u_loaded, 16)
            for i in range(2):
                sp.dma_start(ar(i), adj[span(i), :]).then_inc(adj_loaded[i], 16)
            for i in range(NT):
                sp.wait_ge(h_made, i + 1)
                sp.dma_start(h_d[span(i), :], xh(i)).then_inc(h_stored, 16)
                sp.wait_ge(t_high, i + 1)
                sp.wait_ge(t_low, i + 1)
                for half in range(2):
                    sp.dma_start(ht_d[i, :, half * D:(half + 1) * D].rearrange("p (k c) -> p k c", k=KB),
                                 ht(i, half).bitcast(F32)).then_inc(ht_stored[i // BT % 2], 16)

            def store_g(i):
                sp.wait_ge(g_high, i + 1)
                sp.wait_ge(g_low, i + 1)
                o = KO + 4 * D
                sp.dma_start(g_d[span(i)], XB[0:rows(i), o:o + 2 * D].bitcast(F32).rearrange("p (a d) -> p a d", a=2)
                             ).then_inc(g_stored, 16)

            def load_ht(i):
                if i >= 2:
                    sp.wait_ge(g_made, i - 1)
                sp.dma_start(htl(i % 2).bitcast(F32), ht_d[i]).then_inc(ht_loaded[i % 2], 16)

            sp.wait_ge(logits_made, NT)
            sp.wait_ge(ht_stored[0], 32 * len([i for i in range(NT) if i // BT % 2 == 0]))
            sp.wait_ge(ht_stored[1], 32 * len([i for i in range(NT) if i // BT % 2 == 1]))
            load_ht(0)
            load_ht(1)
            for i in range(NT):
                if i + 2 < NT:
                    sp.wait_ge(panel_turned, i + 1)
                    sp.wait_ge(row_summed, i + 1)
                    sp.dma_start(ar(i + 2), adj[span(i + 2), :]).then_inc(adj_loaded[i % 2], 16)
                sp.wait_ge(panel_high, i + 1)
                sp.wait_ge(panel_low, i + 1)
                sp.dma_start(panels_d[i], PAN[:, (i % 2) * 2 * NW:(i % 2 + 1) * 2 * NW].bitcast(F32)).then_inc(panel_stored[i % 2], 16)
                if i >= 2:
                    store_g(i - 2)
                    if i < NT:
                        load_ht(i)

            store_g(NT - 2)
            store_g(NT - 1)

            sp.wait_ge(panel_turned, NT)
            sp.wait_ge(row_summed, NT)
            sp.dma_start(AR[:, 0:HALF].rearrange("p (k d) -> p k d", k=KB),
                         u2_0.rearrange("(k p) d -> p k d", p=P)).then_inc(u2_loaded, 16)
            for i in range(NT):
                n = 2 * NT + i
                sp.wait_ge(t_high, n + 1)
                sp.wait_ge(t_low, n + 1)
                sp.dma_start(xat_d[i], TR[:, (n % 2) * 2 * D:(n % 2 + 1) * 2 * D].bitcast(F32)).then_inc(tr_stored[n % 2], 16)

            def load_xat(i):
                n = 2 * NT + i
                if i < 2:
                    tile_used(sp, 3 * NT - 1)
                    sp.wait_ge(tr_stored[(3 * NT - 2) % 2], 16 * tr_stores(3 * NT - 2))
                    sp.wait_ge(tr_stored[(3 * NT - 1) % 2], 16 * tr_stores(3 * NT - 1))
                    sp.wait_ge(h_stored, 16 * NT)
                else:
                    sp.wait_ge(v_made, i - 1)
                sp.dma_start(TR[:, (i % 2) * 2 * D:(i % 2 + 1) * 2 * D].bitcast(F32), xat_d[i]).then_inc(xat_loaded[i % 2], 16)

            def load_h(i):
                if i >= 2:
                    sp.wait_ge(part_stored[i % 2], 16 * uses(i - 2))
                sp.dma_start(stg(i % 2, i), h_d[span(i), :]).then_inc(h_loaded[i % 2], 16)

            def load_g():
                sp.wait_ge(product_made, 2 * NT)
                sp.wait_ge(g_stored, 16 * NT)
                for half in range(2):
                    o = half * NT * D
                    sp.dma_start(XA[:, o:o + (NT - 1) * D].bitcast(F32).rearrange("p (t d) -> p t d", d=D),
                                 g_d[0:FULL, half, :].rearrange("(t p) d -> p t d", p=P)).then_inc(g_loaded, 16)
                    sp.dma_start(nat(XA, half, NT - 1).bitcast(F32), g_d[FULL:N, half, :]).then_inc(g_loaded, 16)

            load_xat(0)
            load_h(0)
            load_xat(1)
            load_h(1)
            sp.wait_ge(u2_high, 1)
            sp.wait_ge(u2_low, 1)
            sp.dma_start(AR[:, 0:HALF].rearrange("p (k d) -> p k d", k=KB),
                         u2_1.rearrange("(k p) d -> p k d", p=P)).then_inc(u2_loaded, 16)
            load_g()
            for i in range(NT):
                sp.wait_ge(part_made, i + 1)
                sp.dma_start(part_d[span(i), :], stg(i % 2, i)).then_inc(part_stored[i % 2], 16)
                if i + 2 < NT:
                    load_xat(i + 2)
                    load_h(i + 2)
            sp.wait_ge(u2_high, 2)
            sp.wait_ge(u2_low, 2)
            for j, v in enumerate((gamma, beta)):
                sp.dma_start(AR[:, j * D:(j + 1) * D],
                             v.partition_broadcast(P)).then_inc(gb_loaded, 16)

            def load_panel(i, free, count):
                sp.wait_ge(free, count)
                sp.wait_ge(panel_stored[i % 2], 16 * total(i % 2))
                sp.dma_start(PAN[:, (i % 2) * 2 * NW:(i % 2 + 1) * 2 * NW].bitcast(F32), panels_d[i]).then_inc(panel_loaded[i % 2], 16)

            def load_part(i):
                if i >= 2:
                    sp.wait_ge(part2_stored[i % 2], 16 * uses(i - 2))
                sp.wait_ge(part_stored[i % 2], 16 * uses(i))
                if i < 2:
                    sp.wait_ge(part_stored[i % 2], 16 * total(i % 2))
                sp.dma_start(stg(i % 2, i), part_d[span(i), :]).then_inc(part_loaded[i % 2], 16)

            for i in range(2):
                load_panel(i, v_made, NT)
                load_part(i)
            for i in range(NT):
                if i + 2 < NT:
                    load_panel(i + 2, rg_made, i + 1)
                sp.wait_ge(part2_made, i + 1)
                sp.dma_start(part2_d[span(i), :], stg(i % 2, i)).then_inc(part2_stored[i % 2], 16)
                if i + 2 < NT:
                    load_part(i + 2)

            def load_part2(i):
                if i < 2:
                    sp.wait_ge(part2_stored[i % 2], 16 * total(i % 2))
                else:
                    sp.wait_ge(x1_made, i - 1)
                sp.dma_start(stg(i % 2, i), part2_d[span(i), :]).then_inc(part_loaded[i % 2], 16)
                if i >= 2:
                    sp.wait_ge(x1_stored[i % 2], 16 * uses(i - 2))
                    sp.wait_ge(w_normed, i - 1)
                sp.dma_start(stg(2 + i % 2, i), x[span(i), :]).then_inc(xin_loaded[i % 2], 16)

            load_part2(0)
            load_part2(1)
            for i in range(NT):
                sp.wait_ge(x1_made, i + 1)
                sp.dma_start(x1_d[span(i), :], stg(2 + i % 2, i)).then_inc(x1_stored[i % 2], 16)
                if i + 2 < NT:
                    load_part2(i + 2)

            def load_row2(i):
                if i < 2:
                    sp.wait_ge(weights_made, NT + -(-4 * NW // N))
                else:
                    sp.wait_ge(panel_turned, 3 * NT + i - 1)
                    sp.wait_ge(panel_high, 3 * NT + i - 1)
                    sp.wait_ge(panel_low, 3 * NT + i - 1)
                sp.dma_start(row2(i), adj[span(i), :]).then_inc(row2_loaded[i % 2], 16)
                c = col2(i).rearrange("p (k c) -> p k c", c=P)
                sp.dma_start(c[:, 0:NT - 1, 0:rows(i)],
                             adj[0:FULL, span(i)].rearrange("(k p) c -> p k c", p=P)).then_inc(row2_loaded[i % 2], 16)
                sp.dma_start(c[0:LAST, NT - 1, 0:rows(i)], adj[FULL:N, span(i)]).then_inc(row2_loaded[i % 2], 16)

            load_row2(0)
            load_row2(1)
            for i in range(2, NT):
                load_row2(i)

            def load_x1(i):
                if i < 2:
                    sp.wait_ge(y1_low, NT)
                    sp.wait_ge(x1_stored[i % 2], 16 * total(i % 2))
                else:
                    sp.wait_ge(out_stored[i % 2], 16 * uses(i - 2))
                sp.dma_start(stg(i % 2, i), x1_d[span(i), :]).then_inc(x1_loaded[i % 2], 16)

            load_panel(0, product_made, 4 * NT - 1)
            load_panel(1, product_made, 4 * NT)
            load_x1(0)
            load_x1(1)
            for i in range(NT):
                if i + 2 < NT:
                    load_panel(i + 2, last_made, i + 1)
                sp.wait_ge(out_made, i + 1)
                sp.dma_start(out[span(i), :], stg(i % 2, i)).then_inc(out_stored[i % 2], 16)
                if i + 2 < NT:
                    load_x1(i + 2)
            for k in range(2):
                sp.wait_ge(out_stored[k], 16 * total(k))

        @block.gpsimd
        def _(pool):
            nc.gpsimd.memset(draft_ident, 0.0).then_inc(ident_zeroed, 1)
            pool.wait_ge(ident_zeroed, 1)
            nc.gpsimd.affine_select(out=draft_ident, in_=draft_ident, compare_op=ALU.not_equal, fill=1.0, base=0,
                                    pattern=[[-1, P]], channel_multiplier=1).then_inc(ident_made, 1)
            for i in range(NT):
                pool.wait_ge(h_high, i + 1)
                nc.gpsimd.tensor_tensor(nat(XA, 1, i), xh(i), nat(XA, 0, i).bitcast(F32),
                                        ALU.subtract).then_inc(h_low, 1)
            own = [0]

            def link(ins):
                own[0] += 1
                ins.then_inc(pool_own, 1)
                pool.wait_ge(pool_own, own[0])

            def join_flags(m):
                pool.wait_ge(flags_made, m + 1)
                nc.gpsimd.partition_all_reduce(flag[:, 1:2], flag[:, 0:1], P, RMAX).then_inc(flags_joined, 1)

            def weights(i):
                pool.wait_ge(taken, i + 1)
                nc.gpsimd.tensor_tensor(xs(i), Et(i), xs(i), ALU.subtract).then_inc(weights_made, 1)

            def x1_tile(i):
                R = rows(i)
                pool.wait_ge(y_normed, i + 1)
                if i == 0:
                    pool.wait_ge(gb_loaded, 32)
                pool.wait_ge(xin_loaded[i % 2], 16 * uses(i))
                y = stg(i % 2, i)
                link(nc.gpsimd.tensor_tensor(y, y, AR[0:R, 0:D], ALU.mult))
                link(nc.gpsimd.tensor_tensor(y, y, AR[0:R, D:2 * D], ALU.add))
                nc.gpsimd.tensor_tensor(stg(2 + i % 2, i), stg(2 + i % 2, i), y, ALU.add).then_inc(x1_made, 1)

            def w_low_part(i):
                o = (2 + i % 2) * D
                pool.wait_ge(w_high, i + 1)
                nc.gpsimd.tensor_tensor(nat(XA, 1, i), AR[0:rows(i), o:o + D], nat(XA, 0, i).bitcast(F32),
                                        ALU.subtract).then_inc(w_low, 1)

            for m in range(NT + 2):
                join_flags(m)
                if m == NT:
                    weights(0)
            for i in range(NT + 4):
                if i + 1 < NT:
                    weights(i + 1)
                if 0 <= i - 2 < NT:
                    x1_tile(i - 2)
                if i + 2 < NT:
                    join_flags(NT + i + 2)
                if 0 <= i - 3 < NT:
                    w_low_part(i - 3)

        @block.scalar
        def _(act):
            own = [0]

            def link(ins):
                own[0] += 1
                ins.then_inc(act_own, 1)
                act.wait_ge(act_own, own[0])

            act.wait_ge(w1t_turned, 1)
            nc.scalar.copy(STG[0:DA, 3 * D:4 * D], ACC[0][0:DA, :]).then_inc(w1t_copied, 1)
            act.wait_ge(w12_made, 1)
            for which, src in ((0, ACC[1][:, 0:KB * DA]), (1, stg(1)[:, 0:KB * DA])):
                for twin in range(2):
                    last = nc.scalar.copy(
                        wqk(which, 0).rearrange("p (k a) -> p k a", k=KB)[:, :, twin * DA:(twin + 1) * DA],
                        src.rearrange("p (k a) -> p k a", k=KB))
            last.then_inc(wqk_high, 1)

            def ln_roots(b):
                act.wait_ge(ln_var, b + 1)
                g = slice(b * BT, min((b + 1) * BT, NT))
                nc.scalar.activation(m_lo[:, g], lo_var[:, g], ACT.Sqrt).then_inc(ln_root, 1)

            def ht_high_part(i):
                act.wait_ge(turned, i + 1)
                if i // BT >= 2:
                    act.wait_ge(qk_made, i // BT - 1)
                    act.wait_ge(ht_stored[i // BT % 2], 32 * BT)
                nc.scalar.copy(ht(i, 0), ACC[i % 2][:, :].rearrange("p (k c) -> p k c", k=KB)).then_inc(t_high, 1)

            def batch_high_part(b):
                act.wait_ge(qk_made, b + 1)
                o = b * BT * P
                c = min(BT * P, N - o)
                nc.scalar.copy(Q[:, o:o + c], BIG[b % 2][:, 0:c])
                nc.scalar.copy(keys(0, o, o + c), BIG[b % 2][:, 512:512 + c]).then_inc(qk_high, 1)

            def t_high_part(n):
                act.wait_ge(turned, n + 1)
                if n >= NT + 2:
                    tile_used(act, n - 2)
                if n >= NT + 2 and tr_stores(n - 2):
                    act.wait_ge(tr_stored[n % 2], 16 * tr_stores(n - 2))
                nc.scalar.copy(tr(n % 2, 0), ACC[bank(n)][:, :]).then_inc(t_high, 1)

            def qk_high_part(i):
                act.wait_ge(qk_made, qk_count(i))
                o = i * P
                c = rows(i)
                a = ACC[1]
                nc.scalar.copy(Q[:, o:o + c], a[:, 0:c])
                nc.scalar.copy(keys(0, o, o + c), a[:, P:P + c]).then_inc(qk_high, 1)

            for i in range(NT + 1):
                if i in (0, 3, 7):
                    ln_roots((i + 1) // BT)
                if i < NT:
                    act.wait_ge(ln_scale, i // BT + 1)
                    nc.scalar.activation(xh(i), xh(i), ACT.Relu, bias=ln_shift[0:rows(i), i:i + 1],
                                         scale=ln_rstd[0:rows(i), i:i + 1]).then_inc(h_made, 1)
                    act.wait_ge(h_made, i + 1)
                    nc.scalar.copy(nat(XA, 0, i), xh(i)).then_inc(h_high, 1)
                if i >= 1:
                    ht_high_part(i - 1)
                if i == 2 * BT:
                    batch_high_part(0)
            for b in range(1, NB):
                batch_high_part(b)

            def exps(s, i):
                act.wait_ge(max_made, NT * s + i + 1)
                R = rows(i)
                nc.scalar.activation(Et(i), BIG[i % 2][0:R, 0:N], ACT.Exp, bias=nmax[0:R, i:i + 1],
                                     accum_out=S[0:R, i:i + 1]).then_inc(exp_made, 1)

            for i in range(NT):
                if i == 0:
                    act.wait_ge(h_stored, 16 * NT)
                    act.wait_ge(h_low, NT)
                    act.wait_ge(turned, NT)
                    act.wait_ge(u_loaded, 32)
                    act.wait_ge(ht_stored[0], 32 * len([i for i in range(NT) if i // BT % 2 == 0]))
                    act.wait_ge(ht_stored[1], 32 * len([i for i in range(NT) if i // BT % 2 == 1]))
                    for j in range(2):
                        last = nc.scalar.copy(XB[:, 2 * j * HALF:(2 * j + 1) * HALF], u1_raw(j))
                    last.then_inc(u1_high, 1)
                if i == u1_first_tile:
                    act.wait_ge(u1_low, 1)
                exps(0, i)

            def row_sum(i):
                act.wait_ge(adj_loaded[i % 2], 16 * uses(i))
                R = rows(i)
                if i:
                    act.wait_ge(row_summed, i)
                nc.scalar.activation(X[0:R, N + 8:2 * N + 8], ar(i), ACT.Copy,
                                     accum_out=rowsum[0:R, i:i + 1]).then_inc(row_summed, 1)

            def panel_high_part(p):
                act.wait_ge(panel_turned, p + 1)
                if p >= 2:
                    act.wait_ge(product_made, p - 1)
                if 2 <= p < NT + 2:
                    act.wait_ge(panel_stored[p % 2], 16 * uses(p - 2))
                if p == 2 * NT:
                    act.wait_ge(rg_made, NT)
                nc.scalar.copy(pan(p % 2, 0), BIG[p % 2][:, 0:NW]).then_inc(panel_high, 1)

            def g_high_part(i):
                act.wait_ge(g_made, i + 1)
                if i >= 1:
                    act.wait_ge(g_stored, 16 * i)
                nc.scalar.copy(gst(0, i), ACC[1][0:rows(i), :]).then_inc(g_high, 1)

            def product_out(p, scale):
                i = p % NT
                act.wait_ge(product_made, p + 1)
                if p >= 2:
                    act.wait_ge(turned, NT + p - 1)
                nc.scalar.activation(stg(2 + p % 2, i), ACC[0][0:rows(i), :], ACT.Copy,
                                     scale=scale[0:rows(i), i:i + 1]).then_inc(product_read, 1)

            row_sum(0)
            panel_high_part(0)
            for i in range(NT):
                if i + 1 < NT:
                    row_sum(i + 1)
                    panel_high_part(i + 1)
                if i >= 1:
                    t_high_part(NT + i - 1)
                act.wait_ge(rR_made, i + 1)
                product_out(i, rR)
                if i >= 1:
                    g_high_part(i - 1)
            t_high_part(2 * NT - 1)
            panel_high_part(NT)
            g_high_part(NT - 1)

            for i in range(NT):
                if i + 1 < NT:
                    panel_high_part(NT + i + 1)
                if i >= 1:
                    t_high_part(2 * NT + i - 1)
                act.wait_ge(weights_made, i + 1)
                product_out(NT + i, rD)
                if i >= 1:
                    qk_high_part(i - 1)
            t_high_part(3 * NT - 1)
            qk_high_part(NT - 1)
            def u2_high_part(j):
                act.wait_ge(u2_loaded, 16 * (j + 1))
                if j == 0:
                    act.wait_ge(product_made, 2 * NT)
                    act.wait_ge(qk_made, qk_count(NT - 1))
                nc.scalar.copy(u2(j, 0), AR[:, 0:HALF]).then_inc(u2_high, 1)

            u2_high_part(0)
            for i in range(NT):
                exps(1, i)
                if i == 6:
                    u2_high_part(1)

            for i in range(NT):
                act.wait_ge(v_made, i + 1)
                nc.scalar.copy(nat(XB, 0, i), BIG[i % 2][0:rows(i), D:2 * D]).then_inc(v_high, 1)

            act.wait_ge(dinv_root_in, 1)
            nc.scalar.activation(colsum, rowsum, ACT.Sqrt).then_inc(dinv_root, 1)

            def y_root_of(i):
                act.wait_ge(y_var, i + 1)
                R = rows(i)
                nc.scalar.activation(small[0:R, 8:9], small[0:R, 2:3], ACT.Sqrt).then_inc(y_root, 1)

            def y_norm(i):
                act.wait_ge(y_scale, i + 1)
                R = rows(i)
                nc.scalar.activation(stg(i % 2, i), stg(i % 2, i), ACT.Identity, bias=small[0:R, 4:5],
                                     scale=small[0:R, 3:4]).then_inc(y_normed, 1)

            def x1_root_of(i):
                act.wait_ge(x1_var, i + 1)
                R = rows(i)
                nc.scalar.activation(small[0:R, 9:10], small[0:R, 12:13], ACT.Sqrt).then_inc(x1_root, 1)

            def wst(i):
                o = (2 + i % 2) * D
                return AR[0:rows(i), o:o + D]

            def w_parts(i):
                act.wait_ge(x1_scale, i + 1)
                if i >= 2:
                    act.wait_ge(w_low, i - 1)
                R = rows(i)
                nc.scalar.activation(wst(i), stg(2 + i % 2, i), ACT.Relu, bias=small[0:R, 14:15],
                                     scale=small[0:R, 13:14]).then_inc(w_normed, 1)
                act.wait_ge(w_normed, i + 1)
                act.wait_ge(rg_made, NT)
                nc.scalar.copy(nat(XA, 0, i), wst(i)).then_inc(w_high, 1)

            panel_high_part(2 * NT)
            for i in range(NT + 4):
                if 0 <= i - 2 < NT:
                    y_norm(i - 2)
                if 0 <= i - 3 < NT:
                    w_parts(i - 3)
                if i + 1 < NT:
                    panel_high_part(2 * NT + i + 1)
                if 0 <= i - 2 < NT:
                    x1_root_of(i - 2)
                if 0 <= i - 1 < NT:
                    y_root_of(i - 1)

            def sum_high_part(p):
                i = p - 3 * NT
                act.wait_ge(both_summed, i + 1)
                act.wait_ge(product_made, p - 1)
                nc.scalar.copy(pan(p % 2, 0), col2(i)).then_inc(panel_high, 1)

            def y1_part(i):
                act.wait_ge(product_made, 3 * NT + i + 1)
                if i >= 2:
                    act.wait_ge(y1_low, i - 1)
                else:
                    act.wait_ge(x1_stored[i % 2], 16 * total(i % 2))
                    act.wait_ge(x1_stored[1 - i % 2], 16 * total(1 - i % 2))
                R = rows(i)
                nc.scalar.activation(stg(2 + i % 2, i), ACC[(3 * NT + i) % 2][0:R, :], ACT.Copy,
                                     scale=half_dinv[0:R, i:i + 1]).then_inc(product_read, 1)
                act.wait_ge(product_read, 3 * NT + i + 1)
                nc.scalar.copy(nat(XB, 0, i), stg(2 + i % 2, i)).then_inc(y1_high, 1)

            sum_high_part(3 * NT)
            for i in range(NT):
                if i + 1 < NT:
                    sum_high_part(3 * NT + i + 1)
                y1_part(i)

        @block.vector
        def _(dve):
            own = [0]

            def link(ins):
                own[0] += 1
                ins.then_inc(dve_own, 1)
                dve.wait_ge(dve_own, own[0])

            nc.vector.memset(state[:, :], 1.0)
            nc.vector.memset(mask[:, :], 0)
            nc.vector.memset(small[:, :], 1.0)
            nc.vector.memset(flag[:, :], 0.0)
            nc.vector.memset(cum[:, :], 0.0)
            for k in range(2):
                nc.vector.memset(X[:, k * (N + 8) + N:(k + 1) * (N + 8)], 0.0)
            nc.vector.memset(ACC[0][:, :], 0.0)
            nc.vector.memset(ACC[1][:, :], 0.0).then_inc(zeroed, 1)
            dve.wait_ge(zeroed, 1)
            dve.wait_ge(ident_made, 1)
            nc.vector.tensor_copy(ident_r[:], draft_ident)
            nc.vector.tensor_scalar(ident2_r[:], draft_ident, 2.0, None, ALU.mult).then_inc(idents_r_made, 1)

            dve.wait_ge(wqk_high, 1)
            for which, src in ((0, ACC[1][:, 0:KB * DA]), (1, stg(1)[:, 0:KB * DA])):
                for twin in range(2):
                    def part(half):
                        return wqk(which, half).rearrange("p (k a) -> p k a", k=KB)[:, :, twin * DA:(twin + 1) * DA]
                    last = nc.vector.tensor_tensor(part(1), src.rearrange("p (k a) -> p k a", k=KB),
                                                   part(0).bitcast(F32), ALU.subtract)
            last.then_inc(wqk_low, 1)

            def inverse_root(out_, a, root, t):
                link(nc.vector.reciprocal(out_, root))
                link(nc.vector.tensor_tensor(t, out_, out_, ALU.mult))
                link(nc.vector.tensor_tensor(t, t, a, ALU.mult))
                link(nc.vector.tensor_scalar(t, t, -0.5, 1.5, ALU.mult, ALU.add))
                link(nc.vector.tensor_tensor(out_, out_, t, ALU.mult))

            def ln_stats(b):
                for i in batch(b):
                    R = rows(i)
                    dve.wait_ge(x_loaded[i], 16)
                    link(nc.vector.bn_stats(small[0:R, 0:6], xh(i)))
                    link(nc.vector.bn_aggr(mean_var[0:R, 2 * i:2 * i + 2], small[0:R, 0:6]))
                g = slice(b * BT, min((b + 1) * BT, NT))
                mv = mean_var.rearrange("p (t c) -> p c t", c=2)
                nc.vector.tensor_copy(ln_shift[:, g], mv[:, 0, g])
                nc.vector.tensor_scalar(lo_var[:, g], mv[:, 1, g], LAYER_EPS, None, ALU.add).then_inc(ln_var, 1)
                dve.wait_ge(ln_var, b + 1)
                dve.wait_ge(ln_root, b + 1)
                inverse_root(ln_rstd[:, g], lo_var[:, g], m_lo[:, g], up_f[:, g])
                nc.vector.scalar_tensor_tensor(out=ln_shift[:, g], in0=ln_shift[:, g], scalar=-1.0,
                                               in1=ln_rstd[:, g], op0=ALU.mult, op1=ALU.mult).then_inc(ln_scale, 1)

            def ht_low_part(i):
                dve.wait_ge(t_high, i + 1)
                nc.vector.tensor_tensor(ht(i, 1), ACC[i % 2][:, :].rearrange("p (k c) -> p k c", k=KB),
                                        ht(i, 0).bitcast(F32), ALU.subtract).then_inc(t_low, 1)

            def batch_low_part(b):
                dve.wait_ge(qk_high, b + 1)
                o = b * BT * P
                c = min(BT * P, N - o)
                nc.vector.tensor_tensor(Q[DA:P, o:o + c], BIG[b % 2][DA:P, 0:c], Q[DA:P, o:o + c].bitcast(F32),
                                        ALU.subtract)
                nc.vector.tensor_tensor(keys(1, o, o + c), BIG[b % 2][:, 512:512 + c],
                                        keys(0, o, o + c).bitcast(F32), ALU.subtract).then_inc(qk_low, 1)

            ln_stats(0)
            nc.vector.memset(BIG[0][:, :], 0.0)
            nc.vector.memset(BIG[1][:, :], 0.0).then_inc(big_zeroed, 1)
            ln_stats(1)
            for i in range(NT):
                if i == BT:
                    ln_stats(2)
                ht_low_part(i)
                if i == 2 * BT - 1:
                    batch_low_part(0)
            for b in range(1, NB):
                batch_low_part(b)

            def t_low_part(n):
                dve.wait_ge(t_high, n + 1)
                nc.vector.tensor_tensor(tr(n % 2, 1), ACC[bank(n)][:, :], tr(n % 2, 0).bitcast(F32),
                                        ALU.subtract).then_inc(t_low, 1)

            def qk_low_part(i):
                dve.wait_ge(qk_high, qk_count(i))
                o, c = i * P, rows(i)
                a = ACC[1]
                nc.vector.tensor_tensor(Q[DA:P, o:o + c], a[DA:P, 0:c], Q[DA:P, o:o + c].bitcast(F32), ALU.subtract)
                nc.vector.tensor_tensor(keys(1, o, o + c), a[:, P:P + c], keys(0, o, o + c).bitcast(F32),
                                        ALU.subtract).then_inc(qk_low, 1)

            def row_max(s, i):
                dve.wait_ge(logits_made, NT * s + i + 1)
                R = rows(i)
                nc.vector.tensor_reduce(nmax[0:R, i:i + 1], BIG[i % 2][0:R, 0:N], AX.X, ALU.max,
                                        negate=True).then_inc(max_made, 1)

            for i in range(NT):
                row_max(0, i)
                if i == 2:
                    dve.wait_ge(u1_high, 1)
                    for j in range(2):
                        o = 2 * j * HALF
                        last = nc.vector.tensor_tensor(XB[:, o + HALF:o + 2 * HALF], u1_raw(j),
                                                       XB[:, o:o + HALF].bitcast(F32), ALU.subtract)
                    last.then_inc(u1_low, 1)

            def panel_low_part(p):
                dve.wait_ge(panel_high, p + 1)
                nc.vector.tensor_tensor(pan(p % 2, 1), BIG[p % 2][:, 0:NW], pan(p % 2, 0).bitcast(F32),
                                        ALU.subtract).then_inc(panel_low, 1)

            def column_sum(i):
                dve.wait_ge(panel_high, i + 1)
                c = BIG[i % 2][:, 0:NW].rearrange("p (k c) -> p k c", c=P)[:, :, 0:rows(i)]
                if i == 0:
                    link(nc.vector.tensor_reduce(colsum, c, AX.X, ALU.add))
                else:
                    link(nc.vector.tensor_reduce(up_f, c, AX.X, ALU.add))
                    link(nc.vector.tensor_tensor(colsum, colsum, up_f, ALU.add))

            def row_scale(i):
                dve.wait_ge(row_summed, i + 1)
                R = rows(i)
                link(nc.vector.tensor_scalar(rR[0:R, i:i + 1], rowsum[0:R, i:i + 1], 1.0, 1e-12, ALU.add, ALU.max))
                nc.vector.reciprocal(rR[0:R, i:i + 1], rR[0:R, i:i + 1]).then_inc(rR_made, 1)

            def g_low_part(i):
                dve.wait_ge(g_high, i + 1)
                nc.vector.tensor_tensor(gst(1, i), ACC[1][0:rows(i), :], gst(0, i).bitcast(F32),
                                        ALU.subtract).then_inc(g_low, 1)

            def rg1_step(i):
                if 0 <= i - 2 < NT:
                    g_low_part(i - 2)
                if 0 <= i + 1 < NT:
                    row_scale(i + 1)
                    column_sum(i + 1)
                    panel_low_part(i + 1)
                if 0 <= i - 1 < NT:
                    t_low_part(NT + i - 1)

            def u2_low_part(j):
                dve.wait_ge(u2_high, j + 1)
                nc.vector.tensor_tensor(u2(j, 1), AR[:, 0:HALF], u2(j, 0).bitcast(F32),
                                        ALU.subtract).then_inc(u2_low, 1)

            def v_step(i):
                dve.wait_ge(v_made, i + 1)
                dve.wait_ge(h_loaded[i % 2], 16 * uses(i))
                R = rows(i)
                nc.vector.tensor_tensor(stg(i % 2, i), BIG[i % 2][0:R, 0:D], stg(i % 2, i),
                                        ALU.add).then_inc(part_made, 1)
                dve.wait_ge(v_high, i + 1)
                nc.vector.tensor_tensor(nat(XB, 1, i), BIG[i % 2][0:R, D:2 * D], nat(XB, 0, i).bitcast(F32),
                                        ALU.subtract).then_inc(v_low, 1)

            def rg2_step(i):
                dve.wait_ge(rg_made, i + 1)
                dve.wait_ge(part_loaded[i % 2], 16 * uses(i))
                R = rows(i)
                nc.vector.scalar_tensor_tensor(out=stg(i % 2, i), in0=ACC[i % 2][0:R, :], scalar=rR[0:R, i:i + 1],
                                               in1=stg(i % 2, i), op0=ALU.mult, op1=ALU.add).then_inc(part2_made, 1)

            def evaluate(i):
                R = rows(i)
                evaluated.append(own[0] + 1)
                if len(evaluated) > 2:
                    dve.wait_ge(dve_own, evaluated[-3])
                nc.vector.scalar_tensor_tensor(out=scratch(len(evaluated))[0:R, :], in0=Et(i), scalar=t_try[0:R, i:i + 1], in1=Et(i),
                                               op0=ALU.is_gt, op1=ALU.mult,
                                               accum_out=m_try[0:R, i:i + 1]).then_inc(dve_own, 1)
                own[0] += 1

            evaluated = []

            def scratch(n):
                return X[:, 0:N].bitcast(BF16)[:, (n % 2) * N:(n % 2 + 1) * N]

            def narrow():
                dve.wait_ge(dve_own, own[0])
                link(nc.vector.tensor_tensor(up, m_try, T, ALU.is_ge))
                link(nc.vector.tensor_tensor(down, m_try, T, ALU.is_lt))
                nc.vector.copy_predicated(lo, up, t_try)
                nc.vector.copy_predicated(m_lo, up, m_try)
                nc.vector.copy_predicated(hi, down, t_try)
                link(nc.vector.copy_predicated(m_hi, down, m_try))

            def halve():
                link(nc.vector.tensor_scalar(t_try.bitcast(I32), hi.bitcast(I32), 0.5, None, ALU.mult))
                link(nc.vector.scalar_tensor_tensor(out=t_try.bitcast(I32), in0=lo.bitcast(I32), scalar=0.5,
                                                    in1=t_try.bitcast(I32), op0=ALU.mult, op1=ALU.add))

            def interpolate(aim):
                link(nc.vector.scalar_tensor_tensor(out=t_try, in0=hi, scalar=-aim, in1=T, op0=ALU.mult, op1=ALU.add))
                nc.vector.tensor_tensor(m_try, m_lo, m_hi, ALU.subtract)
                link(nc.vector.tensor_tensor(t_try, t_try, m_hi, ALU.subtract))
                link(nc.vector.reciprocal(m_try, m_try))
                link(nc.vector.tensor_tensor(t_try, t_try, m_try, ALU.mult))
                nc.vector.tensor_tensor(m_try, lo, hi, ALU.subtract)
                link(nc.vector.tensor_scalar(t_try, t_try, CLIP, 1 - CLIP, ALU.max, ALU.min))
                link(nc.vector.tensor_tensor(t_try, t_try, m_try, ALU.mult))
                link(nc.vector.tensor_tensor(t_try, t_try, hi, ALU.add))

            def search(s, between):
                dve.wait_ge(exp_made, NT * (s + 1))
                dve.wait_ge(panel_turned, 2 * NT * s) if s else None
                nc.vector.tensor_scalar(lo, S, FLOOR, None, ALU.mult)
                nc.vector.memset(hi, CEILING)
                nc.vector.tensor_scalar(T, S, TOP_P, None, ALU.mult)
                nc.vector.tensor_copy(m_lo, S)
                link(nc.vector.memset(m_hi, 0.0))
                n = 0
                for r in range(HALVINGS[s] + len(AIMS[s])):
                    if r < HALVINGS[s]:
                        halve()
                    else:
                        interpolate(AIMS[s][r - HALVINGS[s]])
                    for i in range(NT):
                        evaluate(i)
                        between(n)
                        n += 1
                    narrow()

            def round_of_eight(i, sync):
                R = rows(i)
                sync(nc.vector.max(cand[0:R, :], xs(i)))
                sync(nc.vector.tensor_tensor_scan(cum[0:R, 1:9], cand[0:R, :], cand[0:R, :], cum[0:R, 0:1],
                                                  ALU.add, ALU.max))
                sync(nc.vector.scalar_tensor_tensor(out=take[0:R, :], in0=cum[0:R, 0:8], scalar=T[0:R, i:i + 1],
                                                    in1=cand[0:R, :], op0=ALU.is_lt, op1=ALU.mult,
                                                    accum_out=small[0:R, 0:1]))
                nc.vector.tensor_copy(cum[0:R, 0:1], cum[0:R, 8:9])
                nc.vector.tensor_tensor(rD[0:R, i:i + 1], rD[0:R, i:i + 1], small[0:R, 0:1], ALU.add)
                sync(nc.vector.match_replace(xs(i, pad=True), take[0:R, :], xs(i, pad=True), 0.0))

            def choose(s, i):
                R = rows(i)
                p = NT * (1 + s) + i
                if i >= 2 or s:
                    dve.wait_ge(panel_turned, p - 1)
                if i == 1 and s == 0:
                    dve.wait_ge(row_summed, NT)
                nc.vector.tensor_copy(cum[0:R, 0:1], m_hi[0:R, i:i + 1])
                nc.vector.tensor_copy(rD[0:R, i:i + 1], m_hi[0:R, i:i + 1])
                if i == NT - 1:
                    nc.vector.memset(flag[:, 0:1], 0.0)
                link(nc.vector.scalar_tensor_tensor(out=xs(i), in0=Et(i), scalar=hi[0:R, i:i + 1], in1=Et(i),
                                                    op0=ALU.is_le, op1=ALU.mult))
                for _ in range(ROUNDS[s]):
                    round_of_eight(i, link)
                nc.vector.tensor_tensor(flag[0:R, 0:1], cum[0:R, 0:1], T[0:R, i:i + 1],
                                        ALU.is_lt).then_inc(flags_made, 1)

            def drained(ins):
                dve.drain()

            def weigh(s, i):
                R = rows(i)
                dve.wait_ge(flags_joined, NT * s + i + 1)
                short = dve.value_load(flag[0:1, 1:2].bitcast(I32), min_val=0, max_val=2 ** 30)
                with dve.If(short > 0):
                    with dve.Fori(0, MORE_ROUNDS):
                        round_of_eight(i, drained)
                    nc.vector.memset(turn[:, :], 0.0)
                    dve.drain()
                    nc.vector.tensor_tensor(turn[0:R, 0:1], cum[0:R, 0:1], T[0:R, i:i + 1], ALU.is_lt)
                    dve.drain()
                    nc.vector.transpose(turned_flags[:, :], turn[:, :])
                    dve.drain()
                    nc.vector.tensor_reduce(small[:, 1:2], turned_flags[:, :], AX.X, ALU.max)
                    dve.drain()
                    counts = [dve.value_load(small[q:q + 1, 1:2].bitcast(I32), min_val=0, max_val=2 ** 30)
                              for q in range(0, P, 32)]
                    for q in range(4):
                        with dve.If(counts[q] > 0):
                            with dve.Fori(0, ALL_ROUNDS):
                                round_of_eight(i, drained)
                            dve.drain()
                        dve.drain()
                if s == 0:
                    link(nc.vector.reciprocal(rD[0:R, i:i + 1], rD[0:R, i:i + 1]))
                    nc.vector.tensor_tensor(xs(i), Et(i), xs(i), ALU.subtract).then_inc(weights_made, 1)
                else:
                    nc.vector.reciprocal(rD[0:R, i:i + 1], rD[0:R, i:i + 1]).then_inc(taken, 1)

            row_scale(0)
            column_sum(0)
            panel_low_part(0)
            every0 = HALVINGS[0] + len(AIMS[0])

            def between0(n):
                if n % every0 == 0 and n // every0 < NT:
                    rg1_step(n // every0)

            search(0, between0)

            choose(0, 0)
            rg1_step(NT)
            weigh(0, 0)
            choose(0, 1)
            panel_low_part(NT)
            rg1_step(NT + 1)
            link(nc.vector.tensor_tensor(rowsum, colsum, rowsum, ALU.add))
            link(nc.vector.tensor_scalar(rowsum, rowsum, 0.5, 1.0, ALU.mult, ALU.add))

            for i in range(NT):
                if i + 1 < NT:
                    weigh(0, i + 1)
                if i >= 2:
                    qk_low_part(i - 2)
                if i + 2 < NT:
                    choose(0, i + 2)
                if i >= 1:
                    t_low_part(2 * NT + i - 1)
                if i + 1 < NT:
                    panel_low_part(NT + i + 1)
            qk_low_part(NT - 2)
            t_low_part(3 * NT - 1)
            qk_low_part(NT - 1)
            for i in range(NT):
                row_max(1, i)
                if i in (1, 7):
                    u2_low_part(i // 7)

            evals = NT * (HALVINGS[1] + len(AIMS[1]))

            v_after = [3 + 3 * i for i in range(NT)]
            rg2_after = [v_after[-1] + 10 + 3 * i for i in range(NT)]

            def between1(n):
                if n in v_after:
                    v_step(v_after.index(n))
                if n in rg2_after:
                    rg2_step(rg2_after.index(n))

            search(1, between1)
            for i in range(NT):
                if rg2_after[i] >= evals:
                    rg2_step(i)

            link(nc.vector.tensor_scalar(up_f, rowsum, 0.0, None, ALU.is_gt))
            link(nc.vector.tensor_scalar(rowsum, rowsum, 1e-30, None, ALU.max))
            nc.vector.tensor_copy(nmax, rowsum).then_inc(dinv_root_in, 1)
            dve.wait_ge(dinv_root, 1)
            inverse_root(dinv, rowsum, colsum, nmax)
            link(nc.vector.tensor_tensor(dinv, dinv, up_f, ALU.mult))
            link(nc.vector.tensor_scalar(half_dinv, dinv, 0.5, None, ALU.mult))

            def y_stats(i):
                R = rows(i)
                dve.wait_ge(product_made, 2 * NT + i + 1)
                dve.wait_ge(part_loaded[i % 2], 16 * (total(i % 2) + uses(i)))
                dve.wait_ge(taken, i + 1)
                nc.vector.scalar_tensor_tensor(out=stg(i % 2, i), in0=ACC[i % 2][0:R, :], scalar=rD[0:R, i:i + 1],
                                               in1=stg(i % 2, i), op0=ALU.mult, op1=ALU.add).then_inc(product_read, 1)
                dve.wait_ge(product_read, 2 * NT + i + 1)
                link(nc.vector.bn_stats(stats[0:R, :], stg(i % 2, i)))
                link(nc.vector.bn_aggr(small[0:R, 6:8], stats[0:R, :]))
                nc.vector.tensor_scalar(small[0:R, 2:3], small[0:R, 7:8], LN_EPS, None, ALU.add).then_inc(y_var, 1)

            def y_scales(i):
                R = rows(i)
                dve.wait_ge(y_root, i + 1)
                inverse_root(small[0:R, 3:4], small[0:R, 2:3], small[0:R, 8:9], small[0:R, 5:6])
                nc.vector.scalar_tensor_tensor(out=small[0:R, 4:5], in0=small[0:R, 6:7], scalar=-1.0,
                                               in1=small[0:R, 3:4], op0=ALU.mult, op1=ALU.mult).then_inc(y_scale, 1)

            def x1_scales(i):
                R = rows(i)
                dve.wait_ge(x1_root, i + 1)
                if i >= 1:
                    dve.wait_ge(w_normed, i)
                inverse_root(small[0:R, 13:14], small[0:R, 12:13], small[0:R, 9:10], small[0:R, 5:6])
                link(nc.vector.tensor_tensor(small[0:R, 13:14], small[0:R, 13:14], dinv[0:R, i:i + 1], ALU.mult))
                nc.vector.scalar_tensor_tensor(out=small[0:R, 14:15], in0=small[0:R, 10:11], scalar=-1.0,
                                               in1=small[0:R, 13:14], op0=ALU.mult, op1=ALU.mult).then_inc(x1_scale, 1)

            def x1_stats(i):
                R = rows(i)
                xt = stg(2 + i % 2, i)
                dve.wait_ge(x1_made, i + 1)
                link(nc.vector.bn_stats(stats[0:R, :], xt))
                link(nc.vector.bn_aggr(small[0:R, 10:12], stats[0:R, :]))
                nc.vector.tensor_scalar(small[0:R, 12:13], small[0:R, 11:12], LAYER_EPS, None,
                                        ALU.add).then_inc(x1_var, 1)

            choose(1, 0)
            weigh(1, 0)
            choose(1, 1)
            panel_low_part(2 * NT)
            for i in range(NT + 4):
                if i + 1 < NT:
                    weigh(1, i + 1)
                if 0 <= i - 2 < NT:
                    y_scales(i - 2)
                if 0 <= i - 3 < NT:
                    x1_scales(i - 3)
                if i + 2 < NT:
                    choose(1, i + 2)
                if i + 1 < NT:
                    panel_low_part(2 * NT + i + 1)
                if 0 <= i - 2 < NT:
                    x1_stats(i - 2)
                if 0 <= i - 1 < NT:
                    y_stats(i - 1)

            def both(i):
                p = 3 * NT + i
                dve.wait_ge(panel_turned, p + 1)
                dve.wait_ge(row2_loaded[i % 2], 48 * uses(i))
                c = col2(i).rearrange("p (k c) -> p k c", c=P)
                b = BIG[p % 2][:, 0:NW].rearrange("p (k c) -> p k c", c=P)
                R = rows(i)
                nc.vector.tensor_tensor(c[:, 0:NT - 1, 0:R], b[:, 0:NT - 1, 0:R], c[:, 0:NT - 1, 0:R], ALU.add)
                nc.vector.tensor_tensor(c[0:LAST, NT - 1, 0:R], b[0:LAST, NT - 1, 0:R], c[0:LAST, NT - 1, 0:R],
                                        ALU.add).then_inc(both_summed, 1)
                dve.wait_ge(panel_high, p + 1)
                nc.vector.tensor_tensor(pan(p % 2, 1), col2(i), pan(p % 2, 0).bitcast(F32),
                                        ALU.subtract).then_inc(panel_low, 1)

            def y1_low_part(i):
                dve.wait_ge(y1_high, i + 1)
                nc.vector.tensor_tensor(nat(XB, 1, i), stg(2 + i % 2, i), nat(XB, 0, i).bitcast(F32),
                                        ALU.subtract).then_inc(y1_low, 1)

            both(0)
            for i in range(NT):
                if i + 1 < NT:
                    both(i + 1)
                y1_low_part(i)

            for i in range(NT):
                dve.wait_ge(last_made, i + 1)
                dve.wait_ge(x1_loaded[i % 2], 16 * uses(i))
                nc.vector.tensor_tensor(stg(i % 2, i), ACC[i % 2][0:rows(i), :], stg(i % 2, i),
                                        ALU.add).then_inc(out_made, 1)

        @block.tensor
        def _(pe):
            PASSES = ((0, 0), (0, 1), (1, 0))

            pe.wait_ge(idents_r_made, 1)
            pe.wait_ge(zeroed, 1)
            pe.wait_ge(w_loaded, 48)
            for k in range(KB):
                last = nc.tensor.transpose(ACC[0][0:DA, k * P:(k + 1) * P], stg(0)[:, k * DA:(k + 1) * DA], ident)
            last.then_inc(w1t_turned, 1)
            pe.wait_ge(w1t_copied, 1)
            for k in range(KB):
                last = nc.tensor.matmul(ACC[1][:, k * DA:(k + 1) * DA], STG[0:DA, 3 * D + k * P:3 * D + (k + 1) * P],
                                        stg(2)[0:DA, 0:DA], start=True, stop=True)
            last.then_inc(w12_made, 1)
            pe.wait_ge(wqk_low, 1)

            def turn_tile(n, src, i):
                R = rows(i)
                for k in range(KB):
                    last = nc.tensor.transpose(ACC[bank(n)][:, k * P:k * P + R], src[:, k * P:(k + 1) * P],
                                               ident[0:R, 0:R])
                last.then_inc(turned, 1)

            def project(i, n):
                pe.wait_ge(t_high, n + 1)
                pe.wait_ge(t_low, n + 1)
                c = rows(i)
                for which in range(2):
                    m = 0
                    for wh, th in PASSES:
                        for k in range(KB):
                            last = nc.tensor.matmul(ACC[1][:, which * P:which * P + c], wqk(which, wh, k),
                                                    tr(n % 2, th, k)[:, 0:c], start=(m == 0),
                                                    stop=(m == 3 * KB - 1))
                            m += 1
                last.then_inc(qk_made, 1)

            def project_batch(b):
                pe.wait_ge(t_low, batch(b)[-1] + 1)
                if b >= 2:
                    pe.wait_ge(qk_low, b - 1)
                c = min(BT * P, N - b * BT * P)
                for which in range(2):
                    m = 0
                    for wh, th in PASSES:
                        for k in range(KB):
                            last = nc.tensor.matmul(BIG[b % 2][:, which * 512:which * 512 + c], wqk(which, wh, k),
                                                    ht_batch(b, th, k, c), start=(m == 0), stop=(m == 3 * KB - 1))
                            m += 1
                last.then_inc(qk_made, 1)

            pe.wait_ge(big_zeroed, 1)
            for i in range(NT):
                pe.wait_ge(h_made, i + 1)
                if i >= 2:
                    pe.wait_ge(t_low, i - 1)
                turn_tile(i, xh(i), i)
                if i >= BT and i % BT == 1:
                    project_batch(i // BT - 1)
            project_batch(NB - 1)

            def logits(s, i):
                pe.wait_ge(qk_low, NB + NT * s)
                if i >= 2:
                    pe.wait_ge(exp_made, NT * s + i - 1)
                elif s == 1:
                    pe.wait_ge(panel_low, 2 * NT)
                R = rows(i)
                for a, b in chunks:
                    for half in range(2):
                        last = nc.tensor.matmul(BIG[i % 2][0:R, a:b], Q[:, i * P:i * P + R], keys(half, a, b),
                                                start=(half == 0), stop=(half == 1))
                last.then_inc(logits_made, 1)

            for i in range(NT):
                logits(0, i)

            def turn_panel(p, src):
                R = rows(p % NT)
                for k in range(NT):
                    c = rows(k)
                    last = nc.tensor.transpose(BIG[p % 2][0:c, k * P:k * P + R], src[:, k * P:k * P + c],
                                               ident[0:R, 0:R])
                last.then_inc(panel_turned, 1)

            def graph_product(i, slot, rhs, acc, also=None, ready=None):
                R = rows(i)
                m = 0
                n = 3 * NT + (2 if also is not None else 0)
                if also is not None:
                    for half in range(2):
                        nc.tensor.matmul(acc[0:R, :], also[0:R, 0:R], nat(rhs, half, i), start=(m == 0), stop=False)
                        m += 1
                for k in range(NT):
                    c = rows(k)
                    if ready is not None:
                        pe.wait_ge(ready, k + 1)
                    for ph, rh in PASSES:
                        last = nc.tensor.matmul(acc[0:R, :], pan(slot, ph)[0:c, k * P:k * P + R], nat(rhs, rh, k),
                                                start=(m == 0), stop=(m == n - 1))
                        m += 1
                return last

            def g_tile(i):
                n = NT + i
                pe.wait_ge(t_high, n + 1)
                pe.wait_ge(t_low, n + 1)
                pe.wait_ge(ht_loaded[i % 2], 16 * uses(i))
                R = rows(i)
                m = 0
                for j in range(2):
                    for th, uh in PASSES:
                        for k in range(KB):
                            o = th * D + k * P
                            lhs = htl(i % 2)[:, o:o + P] if j == 0 else tr(n % 2, th, k)
                            last = nc.tensor.matmul(ACC[1][0:R, :], lhs[:, 0:R], u1(j, uh, k), start=(m == 0),
                                                    stop=(m == 6 * KB - 1))
                            m += 1
                last.then_inc(g_made, 1)

            def panel_of_adj(i):
                pe.wait_ge(adj_loaded[i % 2], 16 * uses(i))
                if i < 2:
                    pe.wait_ge(exp_made, NT)
                else:
                    pe.wait_ge(panel_high, i - 1)
                    pe.wait_ge(panel_low, i - 1)
                turn_panel(i, ar(i))

            def turn_product(n, i):
                pe.wait_ge(product_read, n - NT + 1)
                turn_tile(n, stg(2 + (n - NT) % 2, i), i)

            def panel_of_weights(p):
                i = p % NT
                pe.wait_ge(weights_made, p - NT + 1)
                if i >= 2 or p < 2 * NT:
                    pe.wait_ge(panel_high, p - 1)
                    pe.wait_ge(panel_low, p - 1)
                else:
                    pe.wait_ge(part_made, NT)
                    pe.wait_ge(v_low, NT)
                turn_panel(p, xs(i))

            panel_of_adj(0)
            for i in range(NT):
                if i + 1 < NT:
                    panel_of_adj(i + 1)
                if i >= 1:
                    if i >= 2:
                        pe.wait_ge(g_low, i - 1)
                    turn_product(NT + i - 1, i - 1)
                pe.wait_ge(panel_high, i + 1)
                pe.wait_ge(panel_low, i + 1)
                pe.wait_ge(product_read, i) if i else None
                graph_product(i, i % 2, XA, ACC[0], also=ident_r).then_inc(product_made, 1)
                if i == 1:
                    pe.wait_ge(u1_low, 1)
                if i >= 1:
                    g_tile(i - 1)
            pe.wait_ge(g_low, NT - 1)
            turn_product(2 * NT - 1, NT - 1)
            panel_of_weights(NT)
            g_tile(NT - 1)

            for i in range(NT):
                if i + 1 < NT:
                    panel_of_weights(NT + i + 1)
                if i >= 1:
                    if i == 1:
                        pe.wait_ge(g_low, NT)
                    else:
                        pe.wait_ge(qk_low, qk_count(i - 2))
                    turn_product(2 * NT + i - 1, i - 1)
                pe.wait_ge(panel_high, NT + i + 1)
                pe.wait_ge(panel_low, NT + i + 1)
                pe.wait_ge(product_read, NT + i)
                graph_product(i, (NT + i) % 2, XA, ACC[0]).then_inc(product_made, 1)
                if i >= 1:
                    project(i - 1, 2 * NT + i - 1)
            pe.wait_ge(qk_low, qk_count(NT - 2))
            turn_product(3 * NT - 1, NT - 1)
            project(NT - 1, 3 * NT - 1)

            for i in range(NT):
                logits(1, i)

            pe.wait_ge(u2_high, 2)
            pe.wait_ge(u2_low, 2)
            for i in range(NT):
                R = rows(i)
                pe.wait_ge(xat_loaded[i % 2], 16 * uses(i))
                if i < 2:
                    pe.wait_ge(exp_made, 2 * NT)
                else:
                    pe.wait_ge(part_made, i - 1)
                    pe.wait_ge(v_low, i - 1)
                for j in range(2):
                    m = 0
                    for th, uh in PASSES:
                        for k in range(KB):
                            last = nc.tensor.matmul(BIG[i % 2][0:R, j * D:(j + 1) * D], tr(i % 2, th, k)[:, 0:R],
                                                    u2(j, uh, k), start=(m == 0), stop=(m == 3 * KB - 1))
                            m += 1
                last.then_inc(v_made, 1)

            pe.wait_ge(g_loaded, 64)
            pe.wait_ge(product_read, 2 * NT)
            for i in range(NT):
                pe.wait_ge(panel_loaded[i % 2], 16 * uses(i))
                if i >= 2:
                    pe.wait_ge(part2_made, i - 1)
                graph_product(i, i % 2, XA, ACC[i % 2], also=ident_r).then_inc(rg_made, 1)

            panel_of_weights(2 * NT)
            for i in range(NT):
                p = 2 * NT + i
                if i + 1 < NT:
                    panel_of_weights(p + 1)
                pe.wait_ge(panel_high, p + 1)
                pe.wait_ge(panel_low, p + 1)
                if i < 2:
                    pe.wait_ge(part2_made, NT)
                else:
                    pe.wait_ge(product_read, p - 1)
                graph_product(i, p % 2, XB, ACC[i % 2]).then_inc(product_made, 1)

            def panel_of_adj2(i):
                pe.wait_ge(row2_loaded[i % 2], 48 * uses(i))
                if i < 2:
                    pe.wait_ge(panel_low, 3 * NT)
                    pe.wait_ge(panel_high, 3 * NT)
                else:
                    pe.wait_ge(both_summed, i - 1)
                turn_panel(3 * NT + i, row2(i))

            panel_of_adj2(0)
            for i in range(NT):
                p = 3 * NT + i
                if i + 1 < NT:
                    panel_of_adj2(i + 1)
                pe.wait_ge(panel_high, p + 1)
                pe.wait_ge(panel_low, p + 1)
                pe.wait_ge(product_read, p - 1)
                if i == 0:
                    pe.wait_ge(w_low, 1)
                graph_product(i, p % 2, XA, ACC[p % 2], also=ident2_r,
                              ready=w_low if i == 0 else None).then_inc(product_made, 1)

            for i in range(NT):
                pe.wait_ge(panel_loaded[i % 2], 16 * (total(i % 2) + uses(i)))
                if i >= 2:
                    pe.wait_ge(out_made, i - 1)
                if i < 2:
                    pe.wait_ge(product_read, 4 * NT - 1 + i)
                graph_product(i, i % 2, XB, ACC[i % 2], ready=y1_low if i == 0 else None).then_inc(last_made, 1)


_INS = ['x', 'adj', 'L0_gnn_W1', 'L0_gnn_W2', 'L0_gnn_W3', 'L0_gnn_U1_0', 'L0_gnn_U1_1', 'L0_gnn_U2_0',
        'L0_gnn_U2_1', 'L0_gnn_gamma', 'L0_gnn_beta']


def kernel(**inputs):
    import numpy as _np
    import concourse.bacc as _bacc
    from concourse import mybir as _mybir
    from concourse.bass_utils import run_bass_kernel_spmd as _run

    nc = _bacc.Bacc("TRN2", target_bir_lowering=False, num_devices=1, dynamic_dma_scratch_size=1024)
    arrays, args = {}, []
    for name in _INS:
        a = _np.ascontiguousarray(inputs[name])
        arrays[f"in_{name}_dram"] = a
        args.append(nc.dram_tensor(f"in_{name}_dram", a.shape, _mybir.dt.from_np(a.dtype), kind="ExternalInput").ap())
    shape = inputs['x'].shape
    args.append(nc.dram_tensor("out_0_dram", shape, _mybir.dt.float32, kind="ExternalOutput").ap())
    gnn_kernel(nc, *args)
    r = _run(nc, [arrays], core_ids=[0])
    return r.results[0]["out_0_dram"]
```

```python
from contextlib import ExitStack

import concourse.bass as bass
from concourse import mybir

F32 = mybir.dt.float32
F32R = mybir.dt.float32r
BF16 = mybir.dt.bfloat16
I32 = mybir.dt.int32
U32 = mybir.dt.uint32
ALU = mybir.AluOpType
ACT = mybir.ActivationFunctionType
AX = mybir.AxisListType
RMAX = bass.bass_isa.ReduceOp.max

P = 128
TOP_P = 0.9
LN_EPS = 1e-5
LAYER_EPS = 1e-5
HALVINGS = (3, 3)
AIMS = ((3.0, 3.0), (4.4, 2.7, 4.1, 3.1))
CLIP = 0.1
ACT_TILES = 4
ROUNDS = (1, 2)
MORE_ROUNDS = 2
AHEAD = 2


def gnn_kernel(nc, x, adj, w1, w2, w3, u1_0, u1_1, u2_0, u2_1, gamma, beta, out):
    N, D = x.shape
    NT = -(-N // P)
    KB = D // P
    DA = w2.shape[0]
    LAST = N - (NT - 1) * P
    FULL = (NT - 1) * P
    NW = NT * P
    HALF = KB * D
    ALL_ROUNDS = -(-N // 8)
    FLOOR = (1 - TOP_P) * 0.999 / N
    CEILING = 1.001

    BT = 512 // P
    NB = -(-NT // BT)

    def batch(b):
        return range(b * BT, min((b + 1) * BT, NT))

    def rows(i):
        return P if i < NT - 1 else LAST

    def span(i):
        return slice(i * P, i * P + rows(i))

    chunks = [(a, min(a + 512, N)) for a in range(0, N, 512)]

    ctx = ExitStack()
    with ctx:
        def sb(name, shape, dt=F32):
            return ctx.enter_context(nc.sbuf_tensor(name, shape, dt))

        def sem(name):
            return ctx.enter_context(nc.semaphore(name))

        def dram(name, shape, dt):
            return nc.dram_tensor(name, shape, dt, kind="Internal").ap()

        panels_d = dram("panels_d", (NT, P, 2 * NW), F32)
        ht_d = dram("ht_d", (NT, P, 2 * D), F32)
        xat_d = dram("xat_d", (NT, P, 2 * D), F32)
        g_d = dram("g_d", (N, 2, D), F32)
        h_d = dram("h_d", (N, D), F32)
        part_d = dram("part_d", (N, D), F32)
        part2_d = dram("part2_d", (N, D), F32)
        x1_d = dram("x1_d", (N, D), F32)

        E = sb("E", [P, NT * N])
        XA = sb("XA", [P, 2 * NT * D], F32R)
        XB = sb("XB", [P, 2 * NT * D], F32R)
        PAN = sb("PAN", [P, 4 * HALF], F32R)
        AR = sb("AR", [P, 2 * N])
        X = sb("X", [P, 2 * (N + 8)])
        Q = sb("Q", [P, N], F32R)
        TR = sb("TR", [P, 2 * 2 * D], F32R)
        STG = sb("STG", [P, 4 * D])
        ident_r = sb("ident_r", [P, P], F32R)
        ident2_r = sb("ident2_r", [P, P], F32R)
        ident = ident_r[:, :].bitcast(F32)
        state = sb("state", [P, 13 * NT])
        mask = sb("mask", [P, 2 * NT], U32)
        cand = sb("cand", [P, 8])
        take = sb("take", [P, 8])
        cum = sb("cum", [P, 9])
        flag = sb("flag", [P, 2])
        small = sb("small", [P, 16])
        pairs = sb("pairs", [P, 16])
        variances, root_pair, scale_pair, shift_pair, means, temp_pair = (
            pairs[:, 2 * k:2 * k + 2] for k in range(6))
        y_mean_var, x1_mean_var = pairs[:, 12:14], pairs[:, 14:16]
        mean_vars = pairs[:, 12:16].rearrange("p (a c) -> p a c", c=2)
        act_scratch = small[:, 15:16]
        y_bn, x1_bn = small[:, 2:8], small[:, 8:14]
        turn = sb("turn", [P, 32], BF16)
        turned_flags = sb("turned_flags", [P, 32], BF16)

        S, T, lo, hi, m_lo, m_hi, t_try, m_try, nmax, rD, rowsum, colsum, rR = (
            state[:, k * NT:(k + 1) * NT] for k in range(13))
        lo_var, ln_rstd, ln_shift, up_f = nmax, m_hi, t_try, rD
        mean_var = state[:, 2 * NT:4 * NT]
        half_dinv = t_try
        positive = lo
        dinv = m_try
        minus_try, sign_sum = colsum, nmax
        up, down = mask[:, 0:NT], mask[:, NT:2 * NT]

        def Et(i):
            return E[0:rows(i), i * N:(i + 1) * N]

        def xh(i):
            return E[0:rows(i), i * D:(i + 1) * D]

        def u1_raw(j):
            o = NT * D + j * HALF
            return E[:, o:o + HALF]

        def nat(buf, half, i):
            o = (half * NT + i) * D
            return buf[0:rows(i), o:o + D]

        def u1(j, half, k):
            o = (2 * j + half) * HALF + k * D
            return XB[:, o:o + D]

        def ht(i, half):
            o = (i // BT % 2) * 2 * BT * D + half * BT * D
            return XB[:, o:o + BT * D].rearrange("p (k t c) -> p t k c", k=KB, t=BT)[:, i % BT]

        def ht_batch(b, half, k, c):
            o = (b % 2) * 2 * BT * D + half * BT * D + k * BT * P
            return XB[:, o:o + c]

        KO = 4 * HALF

        def keys(half, a, b):
            o = KO + half * N
            return XB[:, o + a:o + b]

        def htl(slot):
            o = KO + slot * 2 * D
            return XB[:, o:o + 2 * D]

        def gst(half, i):
            o = KO + 4 * D + half * D
            return XB[0:rows(i), o:o + D]

        def pan(slot, half):
            o = (2 * slot + half) * NW
            return PAN[:, o:o + NW]

        WO = 4 * NW

        def wqk(which, half, k=None):
            o = WO + (2 * which + half) * D
            return PAN[:, o:o + D] if k is None else PAN[:, o + k * P:o + (k + 1) * P]

        def u2(j, half, k=None):
            o = (2 * j + half) * HALF
            return PAN[:, o:o + HALF] if k is None else PAN[:, o + k * D:o + (k + 1) * D]

        def tr(slot, half, k=None):
            o = (2 * slot + half) * D
            return TR[:, o:o + D] if k is None else TR[:, o + k * P:o + (k + 1) * P]

        def ar(i):
            return AR[0:rows(i), (i % 2) * N:(i % 2 + 1) * N]

        def xs(i, pad=False):
            o = (i % 2) * (N + 8)
            return X[0:rows(i), o:o + N + (8 if pad else 0)]

        def stg(slot, i=0):
            return STG[0:rows(i), slot * D:(slot + 1) * D]

        def row2(i):
            o = (i % 2) * NW
            return E[0:rows(i), o:o + N]

        def col2(i):
            o = (2 + i % 2) * NW
            return E[:, o:o + NW]

        draft_ident = X[:, 0:P]

        BIG = [ctx.enter_context(nc.psum_tensor(f"BIG{k}", [P, 3 * 512], F32)) for k in range(2)]
        ACC = [ctx.enter_context(nc.psum_tensor(f"ACC{k}", [P, 512], F32)) for k in range(2)]

        x_loaded = [sem(f"x_loaded{i}") for i in range(NT)]
        w_loaded = sem("w_loaded")
        u_loaded = sem("u_loaded")
        u2_loaded = sem("u2_loaded")
        adj_loaded = [sem(f"adj_loaded{k}") for k in range(2)]
        ht_loaded = [sem(f"ht_loaded{k}") for k in range(2)]
        xat_loaded = [sem(f"xat_loaded{k}") for k in range(2)]
        h_loaded = [sem(f"h_loaded{k}") for k in range(2)]
        g_loaded = sem("g_loaded")
        panel_loaded = [sem(f"panel_loaded{k}") for k in range(2)]
        part_loaded = [sem(f"part_loaded{k}") for k in range(2)]
        xin_loaded = [sem(f"xin_loaded{k}") for k in range(2)]
        gb_loaded = sem("gb_loaded")
        row2_loaded = [sem(f"row2_loaded{k}") for k in range(2)]
        x1_loaded = [sem(f"x1_loaded{k}") for k in range(2)]
        ht_stored = [sem(f"ht_stored{k}") for k in range(2)]
        tr_stored = [sem(f"tr_stored{k}") for k in range(2)]
        h_stored = sem("h_stored")
        panel_stored = [sem(f"panel_stored{k}") for k in range(2)]
        g_stored = sem("g_stored")
        part_stored = [sem(f"part_stored{k}") for k in range(2)]
        part2_stored = [sem(f"part2_stored{k}") for k in range(2)]
        x1_stored = [sem(f"x1_stored{k}") for k in range(2)]
        out_stored = [sem(f"out_stored{k}") for k in range(2)]

        ident_zeroed = sem("ident_zeroed")
        ident_made = sem("ident_made")
        idents_r_made = sem("idents_r_made")
        zeroed = sem("zeroed")
        big_zeroed = sem("big_zeroed")
        ln_var = sem("ln_var")
        ln_root = sem("ln_root")
        ln_scale = sem("ln_scale")
        h_made = sem("h_made")
        h_high = sem("h_high")
        h_low = sem("h_low")
        w1t_turned = sem("w1t_turned")
        w1t_copied = sem("w1t_copied")
        w12_made = sem("w12_made")
        wqk_high = sem("wqk_high")
        wqk_low = sem("wqk_low")
        u1_high = sem("u1_high")
        u1_low = sem("u1_low")
        u2_high = sem("u2_high")
        u2_low = sem("u2_low")
        turned = sem("turned")
        t_high = sem("t_high")
        t_low = sem("t_low")
        qk_made = sem("qk_made")
        qk_high = sem("qk_high")
        qk_low = sem("qk_low")
        logits_made = sem("logits_made")
        max_made = sem("max_made")
        exp_made = sem("exp_made")
        row_summed = sem("row_summed")
        rR_made = sem("rR_made")
        panel_turned = sem("panel_turned")
        panel_high = sem("panel_high")
        panel_low = sem("panel_low")
        product_made = sem("product_made")
        product_read = sem("product_read")
        g_made = sem("g_made")
        g_high = sem("g_high")
        g_low = sem("g_low")
        weights_made = sem("weights_made")
        flags_made = sem("flags_made")
        flags_joined = sem("flags_joined")
        v_made = sem("v_made")
        v_high = sem("v_high")
        v_low = sem("v_low")
        part_made = sem("part_made")
        rg_made = sem("rg_made")
        part2_made = sem("part2_made")
        dinv_root_in = sem("dinv_root_in")
        dinv_root = sem("dinv_root")
        var_made = sem("var_made")
        root_made = sem("root_made")
        reciprocals_made = sem("reciprocals_made")
        scales_made = sem("scales_made")
        y_normed = sem("y_normed")
        x1_made = sem("x1_made")
        w_normed = sem("w_normed")
        w_high = sem("w_high")
        w_low = sem("w_low")
        both_summed = sem("both_summed")
        y1_high = sem("y1_high")
        y1_low = sem("y1_low")
        last_made = sem("last_made")
        out_made = sem("out_made")
        act_own = sem("act_own")
        dve_own = sem("dve_own")
        pool_own = sem("pool_own")
        taken = sem("taken")
        try_made = sem("try_made")
        act_scratched = sem("act_scratched")
        act_evaluated = sem("act_evaluated")

        def uses(i):
            return i // 2 + 1

        def total(slot):
            return (NT - slot + 1) // 2

        def tr_stores(n):
            return sum(1 for m in range(n % 2, n + 1, 2) if m >= 2 * NT)

        def qk_count(i):
            return NB + i + 1

        def bank(n):
            return n % 2 if n < NT else 1

        def tile_used(eng, n):
            if n < 2 * NT:
                eng.wait_ge(g_made, n - NT + 1)
            else:
                eng.wait_ge(qk_made, qk_count(n - 2 * NT))

        u1_first_tile = (NT * D) // N

        v_after = [1 + 8 * i // 5 for i in range(NT)]

        block = ctx.enter_context(nc.Block())

        @block.sync
        def _(sp):
            for i in range(NT):
                sp.dma_start(xh(i), x[span(i), :]).then_inc(x_loaded[i], 16)
                if i == 1:
                    sp.dma_start(stg(0)[:, 0:KB * DA].rearrange("p (k a) -> p k a", k=KB),
                                 w1.rearrange("(k p) a -> p k a", p=P)).then_inc(w_loaded, 16)
                    sp.dma_start(stg(1)[:, 0:KB * DA].rearrange("p (k a) -> p k a", k=KB),
                                 w3.rearrange("(k p) a -> p k a", p=P)).then_inc(w_loaded, 16)
                    sp.dma_start(stg(2)[0:DA, 0:DA], w2).then_inc(w_loaded, 16)
            for j, u in enumerate((u1_0, u1_1)):
                sp.dma_start(u1_raw(j).rearrange("p (k d) -> p k d", k=KB),
                             u.rearrange("(k p) d -> p k d", p=P)).then_inc(u_loaded, 16)
            for i in range(2):
                sp.dma_start(ar(i), adj[span(i), :]).then_inc(adj_loaded[i], 16)
            for i in range(NT):
                sp.wait_ge(h_made, i + 1)
                sp.dma_start(h_d[span(i), :], xh(i)).then_inc(h_stored, 16)
                sp.wait_ge(t_high, i + 1)
                sp.wait_ge(t_low, i + 1)
                for half in range(2):
                    sp.dma_start(ht_d[i, :, half * D:(half + 1) * D].rearrange("p (k c) -> p k c", k=KB),
                                 ht(i, half).bitcast(F32)).then_inc(ht_stored[i // BT % 2], 16)

            def store_g(i):
                sp.wait_ge(g_high, i + 1)
                sp.wait_ge(g_low, i + 1)
                o = KO + 4 * D
                sp.dma_start(g_d[span(i)], XB[0:rows(i), o:o + 2 * D].bitcast(F32).rearrange("p (a d) -> p a d", a=2)
                             ).then_inc(g_stored, 16)

            def load_ht(i):
                if i >= 2:
                    sp.wait_ge(g_made, i - 1)
                sp.dma_start(htl(i % 2).bitcast(F32), ht_d[i]).then_inc(ht_loaded[i % 2], 16)

            sp.wait_ge(logits_made, NT)
            sp.wait_ge(ht_stored[0], 32 * len([i for i in range(NT) if i // BT % 2 == 0]))
            sp.wait_ge(ht_stored[1], 32 * len([i for i in range(NT) if i // BT % 2 == 1]))
            load_ht(0)
            load_ht(1)
            for i in range(NT):
                if i + 2 < NT:
                    sp.wait_ge(panel_turned, i + 1)
                    sp.wait_ge(row_summed, i + 1)
                    sp.dma_start(ar(i + 2), adj[span(i + 2), :]).then_inc(adj_loaded[i % 2], 16)
                sp.wait_ge(panel_high, i + 1)
                sp.wait_ge(panel_low, i + 1)
                sp.dma_start(panels_d[i], PAN[:, (i % 2) * 2 * NW:(i % 2 + 1) * 2 * NW].bitcast(F32)).then_inc(panel_stored[i % 2], 16)
                if i >= 2:
                    store_g(i - 2)
                    if i < NT:
                        load_ht(i)

            store_g(NT - 2)
            store_g(NT - 1)

            sp.wait_ge(panel_turned, NT)
            sp.wait_ge(row_summed, NT)
            sp.dma_start(AR[:, 0:HALF].rearrange("p (k d) -> p k d", k=KB),
                         u2_0.rearrange("(k p) d -> p k d", p=P)).then_inc(u2_loaded, 16)
            for i in range(NT):
                n = 2 * NT + i
                sp.wait_ge(t_high, n + 1)
                sp.wait_ge(t_low, n + 1)
                sp.dma_start(xat_d[i], TR[:, (n % 2) * 2 * D:(n % 2 + 1) * 2 * D].bitcast(F32)).then_inc(tr_stored[n % 2], 16)

            def load_xat(i):
                n = 2 * NT + i
                if i < 2:
                    tile_used(sp, 3 * NT - 1)
                    sp.wait_ge(tr_stored[(3 * NT - 2) % 2], 16 * tr_stores(3 * NT - 2))
                    sp.wait_ge(tr_stored[(3 * NT - 1) % 2], 16 * tr_stores(3 * NT - 1))
                    sp.wait_ge(h_stored, 16 * NT)
                else:
                    sp.wait_ge(v_made, i - 1)
                sp.dma_start(TR[:, (i % 2) * 2 * D:(i % 2 + 1) * 2 * D].bitcast(F32), xat_d[i]).then_inc(xat_loaded[i % 2], 16)

            def load_h(i):
                if i >= 2:
                    sp.wait_ge(part_stored[i % 2], 16 * uses(i - 2))
                sp.dma_start(stg(i % 2, i), h_d[span(i), :]).then_inc(h_loaded[i % 2], 16)

            def load_g():
                sp.wait_ge(product_made, 2 * NT)
                sp.wait_ge(g_stored, 16 * NT)
                for half in range(2):
                    o = half * NT * D
                    sp.dma_start(XA[:, o:o + (NT - 1) * D].bitcast(F32).rearrange("p (t d) -> p t d", d=D),
                                 g_d[0:FULL, half, :].rearrange("(t p) d -> p t d", p=P)).then_inc(g_loaded, 16)
                    sp.dma_start(nat(XA, half, NT - 1).bitcast(F32), g_d[FULL:N, half, :]).then_inc(g_loaded, 16)

            load_xat(0)
            load_h(0)
            load_xat(1)
            load_h(1)
            sp.wait_ge(u2_high, 1)
            sp.wait_ge(u2_low, 1)
            sp.dma_start(AR[:, 0:HALF].rearrange("p (k d) -> p k d", k=KB),
                         u2_1.rearrange("(k p) d -> p k d", p=P)).then_inc(u2_loaded, 16)
            load_g()
            for i in range(NT):
                sp.wait_ge(part_made, i + 1)
                sp.dma_start(part_d[span(i), :], stg(i % 2, i)).then_inc(part_stored[i % 2], 16)
                if i + 2 < NT:
                    load_xat(i + 2)
                    load_h(i + 2)
            sp.wait_ge(u2_high, 2)
            sp.wait_ge(u2_low, 2)
            for j, v in enumerate((gamma, beta)):
                sp.dma_start(AR[:, j * D:(j + 1) * D],
                             v.partition_broadcast(P)).then_inc(gb_loaded, 16)

            def load_panel(i, free, count):
                sp.wait_ge(free, count)
                sp.wait_ge(panel_stored[i % 2], 16 * total(i % 2))
                sp.dma_start(PAN[:, (i % 2) * 2 * NW:(i % 2 + 1) * 2 * NW].bitcast(F32), panels_d[i]).then_inc(panel_loaded[i % 2], 16)

            def load_part(i):
                if i >= 2:
                    sp.wait_ge(part2_stored[i % 2], 16 * uses(i - 2))
                sp.wait_ge(part_stored[i % 2], 16 * uses(i))
                if i < 2:
                    sp.wait_ge(part_stored[i % 2], 16 * total(i % 2))
                sp.dma_start(stg(i % 2, i), part_d[span(i), :]).then_inc(part_loaded[i % 2], 16)

            for i in range(2):
                load_panel(i, v_made, NT)
                load_part(i)
            for i in range(NT):
                if i + 2 < NT:
                    load_panel(i + 2, rg_made, i + 1)
                sp.wait_ge(part2_made, i + 1)
                sp.dma_start(part2_d[span(i), :], stg(i % 2, i)).then_inc(part2_stored[i % 2], 16)
                if i + 2 < NT:
                    load_part(i + 2)

            def load_part2(i):
                if i < 2:
                    sp.wait_ge(part2_stored[i % 2], 16 * total(i % 2))
                else:
                    sp.wait_ge(x1_made, i - 1)
                sp.dma_start(stg(i % 2, i), part2_d[span(i), :]).then_inc(part_loaded[i % 2], 16)
                if i >= 2:
                    sp.wait_ge(x1_stored[i % 2], 16 * uses(i - 2))
                    sp.wait_ge(w_normed, i - 1)
                sp.dma_start(stg(2 + i % 2, i), x[span(i), :]).then_inc(xin_loaded[i % 2], 16)

            def load_row2(i):
                if i < 2:
                    sp.wait_ge(panel_turned, 2 * NT + -(-4 * NW // N))
                else:
                    sp.wait_ge(panel_turned, 3 * NT + i - 1)
                    sp.wait_ge(panel_high, 3 * NT + i - 1)
                    sp.wait_ge(panel_low, 3 * NT + i - 1)
                sp.dma_start(row2(i), adj[span(i), :]).then_inc(row2_loaded[i % 2], 16)
                c = col2(i).rearrange("p (k c) -> p k c", c=P)
                sp.dma_start(c[:, 0:NT - 1, 0:rows(i)],
                             adj[0:FULL, span(i)].rearrange("(k p) c -> p k c", p=P)).then_inc(row2_loaded[i % 2], 16)
                sp.dma_start(c[0:LAST, NT - 1, 0:rows(i)], adj[FULL:N, span(i)]).then_inc(row2_loaded[i % 2], 16)

            load_part2(0)
            load_part2(1)
            for i in range(NT):
                sp.wait_ge(x1_made, i + 1)
                sp.dma_start(x1_d[span(i), :], stg(2 + i % 2, i)).then_inc(x1_stored[i % 2], 16)
                if i + 2 < NT:
                    load_part2(i + 2)
                if i == NT // 2:
                    load_row2(0)
                    load_row2(1)

            for i in range(2, NT):
                load_row2(i)

            def load_x1(i):
                if i < 2:
                    sp.wait_ge(y1_low, NT)
                    sp.wait_ge(x1_stored[i % 2], 16 * total(i % 2))
                else:
                    sp.wait_ge(out_stored[i % 2], 16 * uses(i - 2))
                sp.dma_start(stg(i % 2, i), x1_d[span(i), :]).then_inc(x1_loaded[i % 2], 16)

            load_panel(0, product_made, 4 * NT - 1)
            load_panel(1, product_made, 4 * NT)
            load_x1(0)
            load_x1(1)
            for i in range(NT):
                if i + 2 < NT:
                    load_panel(i + 2, last_made, i + 1)
                sp.wait_ge(out_made, i + 1)
                sp.dma_start(out[span(i), :], stg(i % 2, i)).then_inc(out_stored[i % 2], 16)
                if i + 2 < NT:
                    load_x1(i + 2)
            for k in range(2):
                sp.wait_ge(out_stored[k], 16 * total(k))

        @block.gpsimd
        def _(pool):
            nc.gpsimd.memset(draft_ident, 0.0).then_inc(ident_zeroed, 1)
            pool.wait_ge(ident_zeroed, 1)
            nc.gpsimd.affine_select(out=draft_ident, in_=draft_ident, compare_op=ALU.not_equal, fill=1.0, base=0,
                                    pattern=[[-1, P]], channel_multiplier=1).then_inc(ident_made, 1)
            for i in range(NT):
                pool.wait_ge(h_high, i + 1)
                nc.gpsimd.tensor_tensor(nat(XA, 1, i), xh(i), nat(XA, 0, i).bitcast(F32),
                                        ALU.subtract).then_inc(h_low, 1)
            own = [0]

            def link(ins):
                own[0] += 1
                ins.then_inc(pool_own, 1)
                pool.wait_ge(pool_own, own[0])

            def join_flags(m):
                pool.wait_ge(flags_made, m + 1)
                nc.gpsimd.partition_all_reduce(flag[:, 1:2], flag[:, 0:1], P, RMAX).then_inc(flags_joined, 1)

            def weights(i):
                pool.wait_ge(taken, i + 1)
                nc.gpsimd.tensor_tensor(Et(i), Et(i), xs(i), ALU.subtract).then_inc(weights_made, 1)

            def x1_tile(i):
                R = rows(i)
                pool.wait_ge(y_normed, i + 1)
                if i == 0:
                    pool.wait_ge(gb_loaded, 32)
                pool.wait_ge(xin_loaded[i % 2], 16 * uses(i))
                y = stg(i % 2, i)
                link(nc.gpsimd.tensor_tensor(y, y, AR[0:R, 0:D], ALU.mult))
                link(nc.gpsimd.tensor_tensor(y, y, AR[0:R, D:2 * D], ALU.add))
                nc.gpsimd.tensor_tensor(stg(2 + i % 2, i), stg(2 + i % 2, i), y, ALU.add).then_inc(x1_made, 1)

            def w_low_part(i):
                o = (2 + i % 2) * D
                pool.wait_ge(w_high, i + 1)
                nc.gpsimd.tensor_tensor(nat(XA, 1, i), AR[0:rows(i), o:o + D], nat(XA, 0, i).bitcast(F32),
                                        ALU.subtract).then_inc(w_low, 1)

            def scales(t):
                pool.wait_ge(reciprocals_made, t)
                link(nc.gpsimd.tensor_tensor(temp_pair, scale_pair, scale_pair, ALU.mult))
                link(nc.gpsimd.tensor_tensor(temp_pair, temp_pair, variances, ALU.mult))
                link(nc.gpsimd.tensor_scalar(temp_pair, temp_pair, -0.5, 1.5, ALU.mult, ALU.add))
                link(nc.gpsimd.tensor_tensor(scale_pair, scale_pair, temp_pair, ALU.mult))
                i = t - 2
                if 0 <= i < NT:
                    R = rows(i)
                    link(nc.gpsimd.tensor_tensor(scale_pair[0:R, 1:2], scale_pair[0:R, 1:2], dinv[0:R, i:i + 1], ALU.mult))
                link(nc.gpsimd.tensor_tensor(shift_pair, means, scale_pair, ALU.mult))
                nc.gpsimd.tensor_scalar(shift_pair, shift_pair, -1.0, None, ALU.mult).then_inc(scales_made, 1)

            for m in range(NT):
                join_flags(m)
            for i in range(AHEAD + 2):
                join_flags(NT + i)
                if i <= AHEAD:
                    weights(i)
            for i in range(NT + 3):
                if 1 <= i - 1 <= NT + 1:
                    scales(i - 1)
                if i + 1 + AHEAD < NT:
                    weights(i + 1 + AHEAD)
                if 0 <= i - 2 < NT:
                    x1_tile(i - 2)
                if i + 2 + AHEAD < NT:
                    join_flags(NT + i + 2 + AHEAD)
                if 0 <= i - 3 < NT:
                    w_low_part(i - 3)

        @block.scalar
        def _(act):
            own = [0]

            def link(ins):
                own[0] += 1
                ins.then_inc(act_own, 1)
                act.wait_ge(act_own, own[0])

            act.wait_ge(w1t_turned, 1)
            nc.scalar.copy(STG[0:DA, 3 * D:4 * D], ACC[0][0:DA, :]).then_inc(w1t_copied, 1)

            def wqk_high_part():
                act.wait_ge(w12_made, 1)
                for which, src in ((0, ACC[1][:, 0:KB * DA]), (1, stg(1)[:, 0:KB * DA])):
                    for twin in range(2):
                        last = nc.scalar.copy(
                            wqk(which, 0).rearrange("p (k a) -> p k a", k=KB)[:, :, twin * DA:(twin + 1) * DA],
                            src.rearrange("p (k a) -> p k a", k=KB))
                last.then_inc(wqk_high, 1)

            def ln_roots(b):
                act.wait_ge(ln_var, b + 1)
                g = slice(b * BT, min((b + 1) * BT, NT))
                nc.scalar.activation(m_lo[:, g], lo_var[:, g], ACT.Sqrt).then_inc(ln_root, 1)

            def ht_high_part(i):
                act.wait_ge(turned, i + 1)
                if i // BT >= 2:
                    act.wait_ge(qk_made, i // BT - 1)
                    act.wait_ge(ht_stored[i // BT % 2], 32 * BT)
                nc.scalar.copy(ht(i, 0), ACC[i % 2][:, :].rearrange("p (k c) -> p k c", k=KB)).then_inc(t_high, 1)

            def batch_high_part(b):
                act.wait_ge(qk_made, b + 1)
                o = b * BT * P
                c = min(BT * P, N - o)
                nc.scalar.copy(Q[:, o:o + c], BIG[b % 2][:, 0:c])
                nc.scalar.copy(keys(0, o, o + c), BIG[b % 2][:, 512:512 + c]).then_inc(qk_high, 1)

            def t_high_part(n):
                act.wait_ge(turned, n + 1)
                if n >= NT + 2:
                    tile_used(act, n - 2)
                if n >= NT + 2 and tr_stores(n - 2):
                    act.wait_ge(tr_stored[n % 2], 16 * tr_stores(n - 2))
                nc.scalar.copy(tr(n % 2, 0), ACC[bank(n)][:, :]).then_inc(t_high, 1)

            def qk_high_part(i):
                act.wait_ge(qk_made, qk_count(i))
                o = i * P
                c = rows(i)
                a = ACC[1]
                nc.scalar.copy(Q[:, o:o + c], a[:, 0:c])
                nc.scalar.copy(keys(0, o, o + c), a[:, P:P + c]).then_inc(qk_high, 1)

            for i in range(NT + 1):
                if i in (0, 3, 7):
                    ln_roots((i + 1) // BT)
                if i < NT:
                    act.wait_ge(ln_scale, i // BT + 1)
                    nc.scalar.activation(xh(i), xh(i), ACT.Relu, bias=ln_shift[0:rows(i), i:i + 1],
                                         scale=ln_rstd[0:rows(i), i:i + 1]).then_inc(h_made, 1)
                    act.wait_ge(h_made, i + 1)
                    nc.scalar.copy(nat(XA, 0, i), xh(i)).then_inc(h_high, 1)
                if i == 0:
                    wqk_high_part()
                if i >= 1:
                    ht_high_part(i - 1)
                if i == 2 * BT:
                    batch_high_part(0)
            nc.scalar.activation(act_scratch, act_scratch, ACT.Exp)
            for b in range(1, NB):
                batch_high_part(b)

            def exps(s, i):
                act.wait_ge(max_made, NT * s + i + 1)
                R = rows(i)
                nc.scalar.activation(Et(i), BIG[i % 2][0:R, 0:N], ACT.Exp, bias=nmax[0:R, i:i + 1],
                                     accum_out=S[0:R, i:i + 1]).then_inc(exp_made, 1)

            for i in range(NT):
                if i == 0:
                    act.wait_ge(h_stored, 16 * NT)
                    act.wait_ge(h_low, NT)
                    act.wait_ge(turned, NT)
                    act.wait_ge(u_loaded, 32)
                    act.wait_ge(ht_stored[0], 32 * len([i for i in range(NT) if i // BT % 2 == 0]))
                    act.wait_ge(ht_stored[1], 32 * len([i for i in range(NT) if i // BT % 2 == 1]))
                if i == u1_first_tile:
                    act.wait_ge(u1_low, 2)
                exps(0, i)
                if i in (1, 2):
                    j = i - 1
                    nc.scalar.copy(XB[:, 2 * j * HALF:(2 * j + 1) * HALF], u1_raw(j)).then_inc(u1_high, 1)

            def row_sum(i):
                act.wait_ge(adj_loaded[i % 2], 16 * uses(i))
                R = rows(i)
                if i:
                    act.wait_ge(row_summed, i)
                nc.scalar.activation(X[0:R, N + 8:2 * N + 8], ar(i), ACT.Copy,
                                     accum_out=rowsum[0:R, i:i + 1]).then_inc(row_summed, 1)

            def panel_high_part(p):
                act.wait_ge(panel_turned, p + 1)
                if p >= 2:
                    act.wait_ge(product_made, p - 1)
                if 2 <= p < NT + 2:
                    act.wait_ge(panel_stored[p % 2], 16 * uses(p - 2))
                if p == 2 * NT:
                    act.wait_ge(rg_made, NT)
                nc.scalar.copy(pan(p % 2, 0), BIG[p % 2][:, 0:NW]).then_inc(panel_high, 1)

            def g_high_part(i):
                act.wait_ge(g_made, i + 1)
                if i >= 1:
                    act.wait_ge(g_stored, 16 * i)
                nc.scalar.copy(gst(0, i), ACC[1][0:rows(i), :]).then_inc(g_high, 1)

            def product_out(p, scale):
                i = p % NT
                act.wait_ge(product_made, p + 1)
                if p >= 2:
                    act.wait_ge(turned, NT + p - 1)
                nc.scalar.activation(stg(2 + p % 2, i), ACC[0][0:rows(i), :], ACT.Copy,
                                     scale=scale[0:rows(i), i:i + 1]).then_inc(product_read, 1)

            row_sum(0)
            panel_high_part(0)
            for i in range(NT):
                if i + 1 < NT:
                    row_sum(i + 1)
                    panel_high_part(i + 1)
                if i >= 1:
                    t_high_part(NT + i - 1)
                act.wait_ge(rR_made, i + 1)
                product_out(i, rR)
                if i >= 1:
                    g_high_part(i - 1)
            t_high_part(2 * NT - 1)
            panel_high_part(NT)
            g_high_part(NT - 1)

            for i in range(NT):
                if i + 1 < NT:
                    panel_high_part(NT + i + 1)
                if i >= 1:
                    t_high_part(2 * NT + i - 1)
                act.wait_ge(weights_made, i + 1)
                product_out(NT + i, rD)
                if i >= 1:
                    qk_high_part(i - 1)
            t_high_part(3 * NT - 1)
            qk_high_part(NT - 1)
            def u2_high_part(j):
                act.wait_ge(u2_loaded, 16 * (j + 1))
                if j == 0:
                    act.wait_ge(product_made, 2 * NT)
                    act.wait_ge(qk_made, qk_count(NT - 1))
                nc.scalar.copy(u2(j, 0), AR[:, 0:HALF]).then_inc(u2_high, 1)

            u2_high_part(0)
            for i in range(NT):
                exps(1, i)
                if i == 6:
                    u2_high_part(1)

            def v_high_part(i):
                act.wait_ge(v_made, i + 1)
                nc.scalar.copy(nat(XB, 0, i), BIG[i % 2][0:rows(i), D:2 * D]).then_inc(v_high, 1)

            def act_evaluate(i):
                R = rows(i)
                for f, out_ in ((ACT.Relu, m_try), (ACT.Sign, sign_sum)):
                    scratched[0] += 1
                    if scratched[0] > 2:
                        act.wait_ge(act_scratched, scratched[0] - 2)
                    o = (scratched[0] % 2) * N
                    last = nc.scalar.activation(X[0:R, N + 8:2 * N + 8].bitcast(BF16)[:, o:o + N], Et(i), f,
                                                bias=minus_try[0:R, i:i + 1], accum_out=out_[0:R, i:i + 1])
                    last.then_inc(act_scratched, 1)

            scratched = [0]
            share = NT - ACT_TILES
            for r in range(HALVINGS[1] + len(AIMS[1])):
                act.wait_ge(try_made, r + 1)
                v_due = [i for i in range(NT) if r * share <= v_after[i] < (r + 1) * share]
                for k in range(ACT_TILES):
                    if k < len(v_due):
                        v_high_part(v_due[k])
                    act_evaluate(NT - ACT_TILES + k)
                for i in v_due[ACT_TILES:]:
                    v_high_part(i)
                act.wait_ge(act_scratched, scratched[0])
                nc.scalar.copy(act_scratch, act_scratch).then_inc(act_evaluated, 1)

            act.wait_ge(dinv_root_in, 1)
            nc.scalar.activation(colsum, rowsum, ACT.Sqrt).then_inc(dinv_root, 1)

            def roots(t):
                act.wait_ge(var_made, t)
                nc.scalar.activation(root_pair, variances, ACT.Sqrt).then_inc(root_made, 1)

            def y_norm(i):
                act.wait_ge(scales_made, i + 1)
                R = rows(i)
                nc.scalar.activation(stg(i % 2, i), stg(i % 2, i), ACT.Identity, bias=shift_pair[0:R, 0:1],
                                     scale=scale_pair[0:R, 0:1]).then_inc(y_normed, 1)

            def wst(i):
                o = (2 + i % 2) * D
                return AR[0:rows(i), o:o + D]

            def w_parts(i):
                act.wait_ge(scales_made, i + 2)
                if i >= 2:
                    act.wait_ge(w_low, i - 1)
                R = rows(i)
                nc.scalar.activation(wst(i), stg(2 + i % 2, i), ACT.Relu, bias=shift_pair[0:R, 1:2],
                                     scale=scale_pair[0:R, 1:2]).then_inc(w_normed, 1)
                act.wait_ge(w_normed, i + 1)
                act.wait_ge(rg_made, NT)
                nc.scalar.copy(nat(XA, 0, i), wst(i)).then_inc(w_high, 1)

            def sum_high_part(p):
                i = p - 3 * NT
                act.wait_ge(both_summed, i + 1)
                act.wait_ge(product_made, p - 1)
                nc.scalar.copy(pan(p % 2, 0), col2(i)).then_inc(panel_high, 1)

            panel_high_part(2 * NT)
            for i in range(NT + 3):
                if 0 <= i - 2 < NT:
                    y_norm(i - 2)
                if 0 <= i - 3 < NT:
                    w_parts(i - 3)
                if i + 1 < NT:
                    panel_high_part(2 * NT + i + 1)
                if NT <= i < NT + 2:
                    sum_high_part(2 * NT + i)
                if 1 <= i <= NT + 1:
                    roots(i)

            def y1_part(i):
                act.wait_ge(product_made, 3 * NT + i + 1)
                if i >= 2:
                    act.wait_ge(y1_low, i - 1)
                else:
                    act.wait_ge(x1_stored[i % 2], 16 * total(i % 2))
                    act.wait_ge(x1_stored[1 - i % 2], 16 * total(1 - i % 2))
                R = rows(i)
                nc.scalar.activation(stg(2 + i % 2, i), ACC[(3 * NT + i) % 2][0:R, :], ACT.Copy,
                                     scale=half_dinv[0:R, i:i + 1]).then_inc(product_read, 1)
                act.wait_ge(product_read, 3 * NT + i + 1)
                nc.scalar.copy(nat(XB, 0, i), stg(2 + i % 2, i)).then_inc(y1_high, 1)

            for i in range(NT):
                if 2 <= i + 1 < NT:
                    sum_high_part(3 * NT + i + 1)
                y1_part(i)

        @block.vector
        def _(dve):
            own = [0]

            def link(ins):
                own[0] += 1
                ins.then_inc(dve_own, 1)
                dve.wait_ge(dve_own, own[0])

            nc.vector.memset(state[:, :], 1.0)
            nc.vector.memset(mask[:, :], 0)
            nc.vector.memset(small[:, :], 1.0)
            nc.vector.memset(pairs[:, :], 1.0)
            nc.vector.memset(flag[:, :], 0.0)
            nc.vector.memset(cum[:, :], 0.0)
            for k in range(2):
                nc.vector.memset(X[:, k * (N + 8) + N:(k + 1) * (N + 8)], 0.0)
            nc.vector.memset(ACC[0][:, :], 0.0)
            nc.vector.memset(ACC[1][:, :], 0.0).then_inc(zeroed, 1)
            dve.wait_ge(zeroed, 1)
            dve.wait_ge(ident_made, 1)
            nc.vector.tensor_copy(ident_r[:], draft_ident)
            nc.vector.tensor_scalar(ident2_r[:], draft_ident, 2.0, None, ALU.mult).then_inc(idents_r_made, 1)

            def inverse_root(out_, a, root, t):
                link(nc.vector.reciprocal(out_, root))
                link(nc.vector.tensor_tensor(t, out_, out_, ALU.mult))
                link(nc.vector.tensor_tensor(t, t, a, ALU.mult))
                link(nc.vector.tensor_scalar(t, t, -0.5, 1.5, ALU.mult, ALU.add))
                link(nc.vector.tensor_tensor(out_, out_, t, ALU.mult))

            def ln_stats(b):
                for i in batch(b):
                    R = rows(i)
                    dve.wait_ge(x_loaded[i], 16)
                    link(nc.vector.bn_stats(small[0:R, 0:6], xh(i)))
                    link(nc.vector.bn_aggr(mean_var[0:R, 2 * i:2 * i + 2], small[0:R, 0:6]))
                g = slice(b * BT, min((b + 1) * BT, NT))
                mv = mean_var.rearrange("p (t c) -> p c t", c=2)
                nc.vector.tensor_copy(ln_shift[:, g], mv[:, 0, g])
                nc.vector.tensor_scalar(lo_var[:, g], mv[:, 1, g], LAYER_EPS, None, ALU.add).then_inc(ln_var, 1)
                dve.wait_ge(ln_var, b + 1)
                dve.wait_ge(ln_root, b + 1)
                inverse_root(ln_rstd[:, g], lo_var[:, g], m_lo[:, g], up_f[:, g])
                nc.vector.scalar_tensor_tensor(out=ln_shift[:, g], in0=ln_shift[:, g], scalar=-1.0,
                                               in1=ln_rstd[:, g], op0=ALU.mult, op1=ALU.mult).then_inc(ln_scale, 1)

            def ht_low_part(i):
                dve.wait_ge(t_high, i + 1)
                nc.vector.tensor_tensor(ht(i, 1), ACC[i % 2][:, :].rearrange("p (k c) -> p k c", k=KB),
                                        ht(i, 0).bitcast(F32), ALU.subtract).then_inc(t_low, 1)

            def batch_low_part(b):
                dve.wait_ge(qk_high, b + 1)
                o = b * BT * P
                c = min(BT * P, N - o)
                nc.vector.tensor_tensor(Q[DA:P, o:o + c], BIG[b % 2][DA:P, 0:c], Q[DA:P, o:o + c].bitcast(F32),
                                        ALU.subtract)
                nc.vector.tensor_tensor(keys(1, o, o + c), BIG[b % 2][:, 512:512 + c],
                                        keys(0, o, o + c).bitcast(F32), ALU.subtract).then_inc(qk_low, 1)

            ln_stats(0)
            nc.vector.memset(BIG[0][:, :], 0.0).then_inc(big_zeroed, 1)
            dve.wait_ge(wqk_high, 1)
            for which, src in ((0, ACC[1][:, 0:KB * DA]), (1, stg(1)[:, 0:KB * DA])):
                for twin in range(2):
                    def part(half):
                        return wqk(which, half).rearrange("p (k a) -> p k a", k=KB)[:, :, twin * DA:(twin + 1) * DA]
                    last = nc.vector.tensor_tensor(part(1), src.rearrange("p (k a) -> p k a", k=KB),
                                                   part(0).bitcast(F32), ALU.subtract)
            last.then_inc(wqk_low, 1)
            ln_stats(1)
            nc.vector.memset(BIG[1][:, :], 0.0).then_inc(big_zeroed, 1)
            for i in range(NT):
                if i == BT:
                    ln_stats(2)
                ht_low_part(i)
                if i == 2 * BT - 1:
                    batch_low_part(0)
            for b in range(1, NB):
                batch_low_part(b)

            def t_low_part(n):
                dve.wait_ge(t_high, n + 1)
                nc.vector.tensor_tensor(tr(n % 2, 1), ACC[bank(n)][:, :], tr(n % 2, 0).bitcast(F32),
                                        ALU.subtract).then_inc(t_low, 1)

            def qk_low_part(i):
                dve.wait_ge(qk_high, qk_count(i))
                o, c = i * P, rows(i)
                a = ACC[1]
                nc.vector.tensor_tensor(Q[DA:P, o:o + c], a[DA:P, 0:c], Q[DA:P, o:o + c].bitcast(F32), ALU.subtract)
                nc.vector.tensor_tensor(keys(1, o, o + c), a[:, P:P + c], keys(0, o, o + c).bitcast(F32),
                                        ALU.subtract).then_inc(qk_low, 1)

            def row_max(s, i):
                dve.wait_ge(logits_made, NT * s + i + 1)
                R = rows(i)
                nc.vector.tensor_reduce(nmax[0:R, i:i + 1], BIG[i % 2][0:R, 0:N], AX.X, ALU.max,
                                        negate=True).then_inc(max_made, 1)

            for i in range(NT):
                row_max(0, i)
                if i in (2, 3):
                    j = i - 2
                    dve.wait_ge(u1_high, j + 1)
                    o = 2 * j * HALF
                    nc.vector.tensor_tensor(XB[:, o + HALF:o + 2 * HALF], u1_raw(j),
                                            XB[:, o:o + HALF].bitcast(F32), ALU.subtract).then_inc(u1_low, 1)

            def panel_low_part(p):
                dve.wait_ge(panel_high, p + 1)
                nc.vector.tensor_tensor(pan(p % 2, 1), BIG[p % 2][:, 0:NW], pan(p % 2, 0).bitcast(F32),
                                        ALU.subtract).then_inc(panel_low, 1)

            def column_sum(i):
                dve.wait_ge(panel_high, i + 1)
                c = BIG[i % 2][:, 0:NW].rearrange("p (k c) -> p k c", c=P)[:, :, 0:rows(i)]
                if i == 0:
                    link(nc.vector.tensor_reduce(colsum, c, AX.X, ALU.add))
                else:
                    link(nc.vector.tensor_reduce(up_f, c, AX.X, ALU.add))
                    link(nc.vector.tensor_tensor(colsum, colsum, up_f, ALU.add))

            def row_scale(i):
                dve.wait_ge(row_summed, i + 1)
                R = rows(i)
                link(nc.vector.tensor_scalar(rR[0:R, i:i + 1], rowsum[0:R, i:i + 1], 1.0, 1e-12, ALU.add, ALU.max))
                nc.vector.reciprocal(rR[0:R, i:i + 1], rR[0:R, i:i + 1]).then_inc(rR_made, 1)

            def g_low_part(i):
                dve.wait_ge(g_high, i + 1)
                nc.vector.tensor_tensor(gst(1, i), ACC[1][0:rows(i), :], gst(0, i).bitcast(F32),
                                        ALU.subtract).then_inc(g_low, 1)

            def rg1_step(i):
                if 0 <= i - 2 < NT:
                    g_low_part(i - 2)
                if 0 <= i + 1 < NT:
                    row_scale(i + 1)
                    column_sum(i + 1)
                    panel_low_part(i + 1)
                if 0 <= i - 1 < NT:
                    t_low_part(NT + i - 1)

            def u2_low_part(j):
                dve.wait_ge(u2_high, j + 1)
                nc.vector.tensor_tensor(u2(j, 1), AR[:, 0:HALF], u2(j, 0).bitcast(F32),
                                        ALU.subtract).then_inc(u2_low, 1)

            def v_step(i):
                dve.wait_ge(v_made, i + 1)
                dve.wait_ge(h_loaded[i % 2], 16 * uses(i))
                R = rows(i)
                nc.vector.tensor_tensor(stg(i % 2, i), BIG[i % 2][0:R, 0:D], stg(i % 2, i),
                                        ALU.add).then_inc(part_made, 1)
                dve.wait_ge(v_high, i + 1)
                nc.vector.tensor_tensor(nat(XB, 1, i), BIG[i % 2][0:R, D:2 * D], nat(XB, 0, i).bitcast(F32),
                                        ALU.subtract).then_inc(v_low, 1)

            def rg2_step(i):
                dve.wait_ge(rg_made, i + 1)
                dve.wait_ge(part_loaded[i % 2], 16 * uses(i))
                R = rows(i)
                nc.vector.scalar_tensor_tensor(out=stg(i % 2, i), in0=ACC[i % 2][0:R, :], scalar=rR[0:R, i:i + 1],
                                               in1=stg(i % 2, i), op0=ALU.mult, op1=ALU.add).then_inc(part2_made, 1)

            def evaluate(i):
                R = rows(i)
                evaluated.append(own[0] + 1)
                if len(evaluated) > 2:
                    dve.wait_ge(dve_own, evaluated[-3])
                nc.vector.scalar_tensor_tensor(out=scratch(len(evaluated))[0:R, :], in0=Et(i), scalar=t_try[0:R, i:i + 1], in1=Et(i),
                                               op0=ALU.is_gt, op1=ALU.mult,
                                               accum_out=m_try[0:R, i:i + 1]).then_inc(dve_own, 1)
                own[0] += 1

            evaluated = []

            def scratch(n):
                return X[:, 0:N].bitcast(BF16)[:, (n % 2) * N:(n % 2 + 1) * N]

            def narrow():
                dve.wait_ge(dve_own, own[0])
                link(nc.vector.tensor_tensor(up, m_try, T, ALU.is_ge))
                link(nc.vector.tensor_tensor(down, m_try, T, ALU.is_lt))
                nc.vector.copy_predicated(lo, up, t_try)
                nc.vector.copy_predicated(m_lo, up, m_try)
                nc.vector.copy_predicated(hi, down, t_try)
                link(nc.vector.copy_predicated(m_hi, down, m_try))

            def halve():
                link(nc.vector.tensor_scalar(t_try.bitcast(I32), hi.bitcast(I32), 0.5, None, ALU.mult))
                link(nc.vector.scalar_tensor_tensor(out=t_try.bitcast(I32), in0=lo.bitcast(I32), scalar=0.5,
                                                    in1=t_try.bitcast(I32), op0=ALU.mult, op1=ALU.add))

            def interpolate(aim):
                link(nc.vector.scalar_tensor_tensor(out=t_try, in0=hi, scalar=-aim, in1=T, op0=ALU.mult, op1=ALU.add))
                nc.vector.tensor_tensor(m_try, m_lo, m_hi, ALU.subtract)
                link(nc.vector.tensor_tensor(t_try, t_try, m_hi, ALU.subtract))
                link(nc.vector.reciprocal(m_try, m_try))
                link(nc.vector.tensor_tensor(t_try, t_try, m_try, ALU.mult))
                nc.vector.tensor_tensor(m_try, lo, hi, ALU.subtract)
                link(nc.vector.tensor_scalar(t_try, t_try, CLIP, 1 - CLIP, ALU.max, ALU.min))
                link(nc.vector.tensor_tensor(t_try, t_try, m_try, ALU.mult))
                link(nc.vector.tensor_tensor(t_try, t_try, hi, ALU.add))

            def search(s, between):
                dve.wait_ge(exp_made, NT * (s + 1))
                nc.vector.tensor_scalar(lo, S, FLOOR, None, ALU.mult)
                nc.vector.memset(hi, CEILING)
                nc.vector.tensor_scalar(T, S, TOP_P, None, ALU.mult)
                nc.vector.tensor_copy(m_lo, S)
                link(nc.vector.memset(m_hi, 0.0))
                n = 0
                for r in range(HALVINGS[s] + len(AIMS[s])):
                    if r < HALVINGS[s]:
                        halve()
                    else:
                        interpolate(AIMS[s][r - HALVINGS[s]])
                    if s:
                        nc.vector.tensor_scalar(minus_try, t_try, -1.0, None, ALU.mult).then_inc(try_made, 1)
                    for i in range(NT - ACT_TILES * s):
                        evaluate(i)
                        between(n)
                        n += 1
                    if s:
                        dve.wait_ge(act_evaluated, r + 1)
                        a = slice(NT - ACT_TILES, NT)
                        link(nc.vector.scalar_tensor_tensor(out=sign_sum[:, a], in0=sign_sum[:, a], scalar=float(N),
                                                            in1=t_try[:, a], op0=ALU.add, op1=ALU.mult))
                        link(nc.vector.scalar_tensor_tensor(out=m_try[:, a], in0=sign_sum[:, a], scalar=0.5,
                                                            in1=m_try[:, a], op0=ALU.mult, op1=ALU.add))
                    narrow()

            def round_of_eight(i, sync):
                R = rows(i)
                sync(nc.vector.max(cand[0:R, :], xs(i)))
                sync(nc.vector.tensor_tensor_scan(cum[0:R, 1:9], cand[0:R, :], cand[0:R, :], cum[0:R, 0:1],
                                                  ALU.add, ALU.max))
                sync(nc.vector.scalar_tensor_tensor(out=take[0:R, :], in0=cum[0:R, 0:8], scalar=T[0:R, i:i + 1],
                                                    in1=cand[0:R, :], op0=ALU.is_lt, op1=ALU.mult,
                                                    accum_out=small[0:R, 0:1]))
                nc.vector.tensor_copy(cum[0:R, 0:1], cum[0:R, 8:9])
                nc.vector.tensor_tensor(rD[0:R, i:i + 1], rD[0:R, i:i + 1], small[0:R, 0:1], ALU.add)
                sync(nc.vector.match_replace(xs(i, pad=True), take[0:R, :], xs(i, pad=True), 0.0))

            def choose(s, i):
                R = rows(i)
                if i >= 2:
                    dve.wait_ge(weights_made, NT * s + i - 1)
                if i == 1 and s == 0:
                    dve.wait_ge(row_summed, NT)
                if i == NT - 1:
                    nc.vector.memset(flag[:, 0:1], 0.0)
                link(nc.vector.scalar_tensor_tensor(out=xs(i), in0=Et(i), scalar=hi[0:R, i:i + 1], in1=Et(i),
                                                    op0=ALU.is_le, op1=ALU.mult, accum_out=small[0:R, 0:1]))
                nc.vector.tensor_tensor(cum[0:R, 0:1], S[0:R, i:i + 1], small[0:R, 0:1], ALU.subtract)
                link(nc.vector.tensor_tensor(rD[0:R, i:i + 1], S[0:R, i:i + 1], small[0:R, 0:1], ALU.subtract))
                for _ in range(ROUNDS[s]):
                    round_of_eight(i, link)
                nc.vector.tensor_tensor(flag[0:R, 0:1], cum[0:R, 0:1], T[0:R, i:i + 1],
                                        ALU.is_lt).then_inc(flags_made, 1)

            def drained(ins):
                dve.drain()

            def weigh(s, i):
                R = rows(i)
                dve.wait_ge(flags_joined, NT * s + i + 1)
                short = dve.value_load(flag[0:1, 1:2].bitcast(I32), min_val=0, max_val=2 ** 30)
                with dve.If(short > 0):
                    with dve.Fori(0, MORE_ROUNDS):
                        round_of_eight(i, drained)
                    nc.vector.memset(turn[:, :], 0.0)
                    dve.drain()
                    nc.vector.tensor_tensor(turn[0:R, 0:1], cum[0:R, 0:1], T[0:R, i:i + 1], ALU.is_lt)
                    dve.drain()
                    nc.vector.transpose(turned_flags[:, :], turn[:, :])
                    dve.drain()
                    nc.vector.tensor_reduce(small[:, 1:2], turned_flags[:, :], AX.X, ALU.max)
                    dve.drain()
                    counts = [dve.value_load(small[q:q + 1, 1:2].bitcast(I32), min_val=0, max_val=2 ** 30)
                              for q in range(0, P, 32)]
                    for q in range(4):
                        with dve.If(counts[q] > 0):
                            with dve.Fori(0, ALL_ROUNDS):
                                round_of_eight(i, drained)
                            dve.drain()
                        dve.drain()
                if s == 0:
                    link(nc.vector.reciprocal(rD[0:R, i:i + 1], rD[0:R, i:i + 1]))
                    nc.vector.tensor_tensor(Et(i), Et(i), xs(i), ALU.subtract).then_inc(weights_made, 1)
                else:
                    nc.vector.reciprocal(rD[0:R, i:i + 1], rD[0:R, i:i + 1]).then_inc(taken, 1)

            row_scale(0)
            column_sum(0)
            panel_low_part(0)
            every0 = HALVINGS[0] + len(AIMS[0])
            first_left = -(-NT * (HALVINGS[0] + len(AIMS[0])) // every0)

            def between0(n):
                if n % every0 == 0 and n // every0 < NT:
                    rg1_step(n // every0)

            search(0, between0)

            for i in range(first_left, NT):
                rg1_step(i)
            choose(0, 0)
            rg1_step(NT)
            weigh(0, 0)
            choose(0, 1)
            panel_low_part(NT)
            weigh(0, 1)
            choose(0, 2)
            rg1_step(NT + 1)
            link(nc.vector.tensor_tensor(rowsum, colsum, rowsum, ALU.add))
            link(nc.vector.tensor_scalar(rowsum, rowsum, 0.5, 1.0, ALU.mult, ALU.add))

            for i in range(NT):
                if i + 2 < NT:
                    weigh(0, i + 2)
                if i >= 2:
                    qk_low_part(i - 2)
                if i + 3 < NT:
                    choose(0, i + 3)
                if i >= 1:
                    t_low_part(2 * NT + i - 1)
                if i + 1 < NT:
                    panel_low_part(NT + i + 1)
            qk_low_part(NT - 2)
            t_low_part(3 * NT - 1)
            qk_low_part(NT - 1)
            for i in range(NT):
                row_max(1, i)
                if i in (1, 7):
                    u2_low_part(i // 7)

            evals = (NT - ACT_TILES) * (HALVINGS[1] + len(AIMS[1]))
            rg2_after = [v_after[-1] + 8 + 5 * i for i in range(NT)]

            def between1(n):
                if n in v_after:
                    v_step(v_after.index(n))
                if n in rg2_after:
                    rg2_step(rg2_after.index(n))

            search(1, between1)
            left = [i for i in range(NT) if rg2_after[i] >= evals]

            def rest(n):
                for _ in range(min(n, len(left))):
                    rg2_step(left.pop(0))

            rest(1)
            for j in range(AHEAD + 2):
                choose(1, j)
                rest(1 + j % 2)
                if j < AHEAD + 1:
                    weigh(1, j)
            rest(NT)

            link(nc.vector.tensor_scalar(positive, rowsum, 0.0, None, ALU.is_gt))
            link(nc.vector.tensor_scalar(rowsum, rowsum, 1e-30, None, ALU.max))
            nc.vector.tensor_copy(nmax, rowsum).then_inc(dinv_root_in, 1)
            dve.wait_ge(dinv_root, 1)
            inverse_root(dinv, rowsum, colsum, nmax)
            link(nc.vector.tensor_tensor(dinv, dinv, positive, ALU.mult))
            link(nc.vector.tensor_scalar(half_dinv, dinv, 0.5, None, ALU.mult))

            def statistics(t):
                i = t - 2
                if 0 <= i < NT:
                    R = rows(i)
                    dve.wait_ge(x1_made, i + 1)
                    link(nc.vector.bn_stats(x1_bn[0:R, :], stg(2 + i % 2, i)))
                i = t - 1
                if 0 <= i < NT:
                    R = rows(i)
                    dve.wait_ge(product_made, 2 * NT + i + 1)
                    dve.wait_ge(part_loaded[i % 2], 16 * (total(i % 2) + uses(i)))
                    dve.wait_ge(taken, i + 1)
                    nc.vector.scalar_tensor_tensor(out=stg(i % 2, i), in0=ACC[i % 2][0:R, :], scalar=rD[0:R, i:i + 1],
                                                   in1=stg(i % 2, i), op0=ALU.mult, op1=ALU.add).then_inc(product_read, 1)
                    dve.wait_ge(product_read, 2 * NT + i + 1)
                    link(nc.vector.bn_stats(y_bn[0:R, :], stg(i % 2, i)))
                    nc.vector.bn_aggr(y_mean_var[0:R, :], y_bn[0:R, :])
                i = t - 2
                if 0 <= i < NT:
                    R = rows(i)
                    nc.vector.bn_aggr(x1_mean_var[0:R, :], x1_bn[0:R, :])
                if t >= 2:
                    dve.wait_ge(scales_made, t - 1)
                dve.drain()
                nc.vector.tensor_copy(means, mean_vars[:, :, 0])
                assert LN_EPS == LAYER_EPS
                nc.vector.tensor_scalar(variances, mean_vars[:, :, 1], LN_EPS, None, ALU.add).then_inc(var_made, 1)

            def reciprocals(t):
                dve.wait_ge(root_made, t)
                if t >= 2:
                    dve.wait_ge(y_normed, min(t - 1, NT))
                if t >= 3:
                    dve.wait_ge(w_normed, t - 2)
                nc.vector.reciprocal(scale_pair, root_pair).then_inc(reciprocals_made, 1)

            def both(i):
                p = 3 * NT + i
                dve.wait_ge(panel_turned, p + 1)
                dve.wait_ge(row2_loaded[i % 2], 48 * uses(i))
                c = col2(i).rearrange("p (k c) -> p k c", c=P)
                b = BIG[p % 2][:, 0:NW].rearrange("p (k c) -> p k c", c=P)
                R = rows(i)
                nc.vector.tensor_tensor(c[:, 0:NT - 1, 0:R], b[:, 0:NT - 1, 0:R], c[:, 0:NT - 1, 0:R], ALU.add)
                nc.vector.tensor_tensor(c[0:LAST, NT - 1, 0:R], b[0:LAST, NT - 1, 0:R], c[0:LAST, NT - 1, 0:R],
                                        ALU.add).then_inc(both_summed, 1)
                dve.wait_ge(panel_high, p + 1)
                nc.vector.tensor_tensor(pan(p % 2, 1), col2(i), pan(p % 2, 0).bitcast(F32),
                                        ALU.subtract).then_inc(panel_low, 1)

            panel_low_part(2 * NT)
            for i in range(NT + 3):
                if 1 <= i - 1 <= NT + 1:
                    reciprocals(i - 1)
                if i + 1 + AHEAD < NT:
                    weigh(1, i + 1 + AHEAD)
                if NT <= i < NT + 2:
                    both(i - NT)
                if i + 2 + AHEAD < NT:
                    choose(1, i + 2 + AHEAD)
                if i + 1 < NT:
                    panel_low_part(2 * NT + i + 1)
                if 1 <= i <= NT + 1:
                    statistics(i)

            def y1_low_part(i):
                dve.wait_ge(y1_high, i + 1)
                nc.vector.tensor_tensor(nat(XB, 1, i), stg(2 + i % 2, i), nat(XB, 0, i).bitcast(F32),
                                        ALU.subtract).then_inc(y1_low, 1)

            for i in range(NT):
                if 2 <= i + 1 < NT:
                    both(i + 1)
                y1_low_part(i)

            for i in range(NT):
                dve.wait_ge(last_made, i + 1)
                dve.wait_ge(x1_loaded[i % 2], 16 * uses(i))
                nc.vector.tensor_tensor(stg(i % 2, i), ACC[i % 2][0:rows(i), :], stg(i % 2, i),
                                        ALU.add).then_inc(out_made, 1)

        @block.tensor
        def _(pe):
            PASSES = ((0, 0), (0, 1), (1, 0))

            pe.wait_ge(idents_r_made, 1)
            pe.wait_ge(zeroed, 1)
            pe.wait_ge(w_loaded, 48)
            for k in range(KB):
                last = nc.tensor.transpose(ACC[0][0:DA, k * P:(k + 1) * P], stg(0)[:, k * DA:(k + 1) * DA], ident)
            last.then_inc(w1t_turned, 1)
            pe.wait_ge(w1t_copied, 1)
            for k in range(KB):
                last = nc.tensor.matmul(ACC[1][:, k * DA:(k + 1) * DA], STG[0:DA, 3 * D + k * P:3 * D + (k + 1) * P],
                                        stg(2)[0:DA, 0:DA], start=True, stop=True)
            last.then_inc(w12_made, 1)

            def turn_tile(n, src, i):
                R = rows(i)
                for k in range(KB):
                    last = nc.tensor.transpose(ACC[bank(n)][:, k * P:k * P + R], src[:, k * P:(k + 1) * P],
                                               ident[0:R, 0:R])
                last.then_inc(turned, 1)

            def project(i, n):
                pe.wait_ge(t_high, n + 1)
                pe.wait_ge(t_low, n + 1)
                c = rows(i)
                for which in range(2):
                    m = 0
                    for wh, th in PASSES:
                        for k in range(KB):
                            last = nc.tensor.matmul(ACC[1][:, which * P:which * P + c], wqk(which, wh, k),
                                                    tr(n % 2, th, k)[:, 0:c], start=(m == 0),
                                                    stop=(m == 3 * KB - 1))
                            m += 1
                last.then_inc(qk_made, 1)

            def project_batch(b):
                pe.wait_ge(t_low, batch(b)[-1] + 1)
                if b >= 2:
                    pe.wait_ge(qk_low, b - 1)
                else:
                    pe.wait_ge(big_zeroed, b + 1)
                c = min(BT * P, N - b * BT * P)
                for which in range(2):
                    m = 0
                    for wh, th in PASSES:
                        for k in range(KB):
                            last = nc.tensor.matmul(BIG[b % 2][:, which * 512:which * 512 + c], wqk(which, wh, k),
                                                    ht_batch(b, th, k, c), start=(m == 0), stop=(m == 3 * KB - 1))
                            m += 1
                last.then_inc(qk_made, 1)

            for i in range(NT):
                pe.wait_ge(h_made, i + 1)
                if i == 1:
                    pe.wait_ge(wqk_low, 1)
                if i >= 2:
                    pe.wait_ge(t_low, i - 1)
                turn_tile(i, xh(i), i)
                if i >= BT and i % BT == 1:
                    project_batch(i // BT - 1)
            project_batch(NB - 1)

            def logits(s, i):
                pe.wait_ge(qk_low, NB + NT * s)
                if i >= 2:
                    pe.wait_ge(exp_made, NT * s + i - 1)
                elif s == 1:
                    pe.wait_ge(panel_low, 2 * NT)
                R = rows(i)
                for a, b in chunks:
                    for half in range(2):
                        last = nc.tensor.matmul(BIG[i % 2][0:R, a:b], Q[:, i * P:i * P + R], keys(half, a, b),
                                                start=(half == 0), stop=(half == 1))
                last.then_inc(logits_made, 1)

            for i in range(NT):
                logits(0, i)

            def turn_panel(p, src):
                R = rows(p % NT)
                for k in range(NT):
                    c = rows(k)
                    last = nc.tensor.transpose(BIG[p % 2][0:c, k * P:k * P + R], src[:, k * P:k * P + c],
                                               ident[0:R, 0:R])
                last.then_inc(panel_turned, 1)

            def graph_product(i, slot, rhs, acc, also=None, ready=None, blocks=(0, NT)):
                R = rows(i)
                n = 3 * NT + (2 if also is not None else 0)
                m = n - 3 * (NT - blocks[0]) if blocks[0] else 0
                if also is not None and blocks[0] == 0:
                    for half in range(2):
                        nc.tensor.matmul(acc[0:R, :], also[0:R, 0:R], nat(rhs, half, i), start=(m == 0), stop=False)
                        m += 1
                for k in range(*blocks):
                    c = rows(k)
                    if ready is not None:
                        pe.wait_ge(ready, k + 1)
                    for ph, rh in PASSES:
                        last = nc.tensor.matmul(acc[0:R, :], pan(slot, ph)[0:c, k * P:k * P + R], nat(rhs, rh, k),
                                                start=(m == 0), stop=(m == n - 1))
                        m += 1
                return last

            def g_tile(i):
                n = NT + i
                pe.wait_ge(t_high, n + 1)
                pe.wait_ge(t_low, n + 1)
                pe.wait_ge(ht_loaded[i % 2], 16 * uses(i))
                R = rows(i)
                m = 0
                for j in range(2):
                    for th, uh in PASSES:
                        for k in range(KB):
                            o = th * D + k * P
                            lhs = htl(i % 2)[:, o:o + P] if j == 0 else tr(n % 2, th, k)
                            last = nc.tensor.matmul(ACC[1][0:R, :], lhs[:, 0:R], u1(j, uh, k), start=(m == 0),
                                                    stop=(m == 6 * KB - 1))
                            m += 1
                last.then_inc(g_made, 1)

            def panel_of_adj(i):
                pe.wait_ge(adj_loaded[i % 2], 16 * uses(i))
                if i < 2:
                    pe.wait_ge(exp_made, NT)
                else:
                    pe.wait_ge(panel_high, i - 1)
                    pe.wait_ge(panel_low, i - 1)
                turn_panel(i, ar(i))

            def turn_product(n, i):
                pe.wait_ge(product_read, n - NT + 1)
                turn_tile(n, stg(2 + (n - NT) % 2, i), i)

            def panel_of_weights(p):
                i = p % NT
                pe.wait_ge(weights_made, p - NT + 1)
                if i >= 2 or p < 2 * NT:
                    pe.wait_ge(panel_high, p - 1)
                    pe.wait_ge(panel_low, p - 1)
                else:
                    pe.wait_ge(part_made, NT)
                    pe.wait_ge(v_low, NT)
                turn_panel(p, Et(i))

            panel_of_adj(0)
            for i in range(NT):
                if i + 1 < NT:
                    panel_of_adj(i + 1)
                if i >= 1:
                    if i >= 2:
                        pe.wait_ge(g_low, i - 1)
                    turn_product(NT + i - 1, i - 1)
                pe.wait_ge(panel_high, i + 1)
                pe.wait_ge(panel_low, i + 1)
                if i >= 1:
                    pe.wait_ge(product_read, i)
                graph_product(i, i % 2, XA, ACC[0], also=ident_r).then_inc(product_made, 1)
                if i == 1:
                    pe.wait_ge(u1_low, 2)
                if i >= 1:
                    g_tile(i - 1)
            pe.wait_ge(g_low, NT - 1)
            turn_product(2 * NT - 1, NT - 1)
            panel_of_weights(NT)
            g_tile(NT - 1)

            for i in range(NT):
                if i + 1 < NT:
                    panel_of_weights(NT + i + 1)
                if i >= 1:
                    if i == 1:
                        pe.wait_ge(g_low, NT)
                    else:
                        pe.wait_ge(qk_low, qk_count(i - 2))
                    turn_product(2 * NT + i - 1, i - 1)
                pe.wait_ge(panel_high, NT + i + 1)
                pe.wait_ge(panel_low, NT + i + 1)
                pe.wait_ge(product_read, NT + i)
                graph_product(i, (NT + i) % 2, XA, ACC[0]).then_inc(product_made, 1)
                if i >= 1:
                    project(i - 1, 2 * NT + i - 1)
            pe.wait_ge(qk_low, qk_count(NT - 2))
            turn_product(3 * NT - 1, NT - 1)
            project(NT - 1, 3 * NT - 1)

            for i in range(NT):
                logits(1, i)

            pe.wait_ge(u2_high, 2)
            pe.wait_ge(u2_low, 2)
            for i in range(NT):
                R = rows(i)
                pe.wait_ge(xat_loaded[i % 2], 16 * uses(i))
                if i < 2:
                    pe.wait_ge(exp_made, 2 * NT)
                else:
                    pe.wait_ge(part_made, i - 1)
                    pe.wait_ge(v_low, i - 1)
                for j in range(2):
                    m = 0
                    for th, uh in PASSES:
                        for k in range(KB):
                            last = nc.tensor.matmul(BIG[i % 2][0:R, j * D:(j + 1) * D], tr(i % 2, th, k)[:, 0:R],
                                                    u2(j, uh, k), start=(m == 0), stop=(m == 3 * KB - 1))
                            m += 1
                last.then_inc(v_made, 1)

            pe.wait_ge(g_loaded, 64)
            pe.wait_ge(product_read, 2 * NT)
            for i in range(NT):
                pe.wait_ge(panel_loaded[i % 2], 16 * uses(i))
                if i >= 2:
                    pe.wait_ge(part2_made, i - 1)
                graph_product(i, i % 2, XA, ACC[i % 2], also=ident_r).then_inc(rg_made, 1)

            def panel_of_adj2(i):
                pe.wait_ge(row2_loaded[i % 2], 48 * uses(i))
                if i < 2:
                    pe.wait_ge(panel_low, 3 * NT - 1 + i)
                    pe.wait_ge(panel_high, 3 * NT - 1 + i)
                else:
                    pe.wait_ge(both_summed, i - 1)
                turn_panel(3 * NT + i, row2(i))

            panel_of_weights(2 * NT)
            for i in range(NT):
                p = 2 * NT + i
                if i + 1 < NT:
                    panel_of_weights(p + 1)
                else:
                    panel_of_adj2(0)
                pe.wait_ge(panel_high, p + 1)
                pe.wait_ge(panel_low, p + 1)
                if i < 2:
                    pe.wait_ge(part2_made, NT)
                else:
                    pe.wait_ge(product_read, p - 1)
                graph_product(i, p % 2, XB, ACC[i % 2]).then_inc(product_made, 1)

            panel_of_adj2(1)
            EARLY = NT - 2
            for blocks in ((0, EARLY), (EARLY, NT)):
                for i in range(2):
                    p = 3 * NT + i
                    pe.wait_ge(panel_high, p + 1)
                    pe.wait_ge(panel_low, p + 1)
                    pe.wait_ge(product_read, p - 1)
                    pe.wait_ge(w_low, i + 1)
                    last = graph_product(i, p % 2, XA, ACC[p % 2], also=ident2_r, ready=w_low, blocks=blocks)
                    if blocks[1] == NT:
                        last.then_inc(product_made, 1)
                        if i == 0:
                            panel_of_adj2(2)
            for i in range(2, NT):
                p = 3 * NT + i
                if i + 1 < NT:
                    panel_of_adj2(i + 1)
                pe.wait_ge(panel_high, p + 1)
                pe.wait_ge(panel_low, p + 1)
                pe.wait_ge(product_read, p - 1)
                graph_product(i, p % 2, XA, ACC[p % 2], also=ident2_r).then_inc(product_made, 1)

            for i in range(NT):
                pe.wait_ge(panel_loaded[i % 2], 16 * (total(i % 2) + uses(i)))
                if i >= 2:
                    pe.wait_ge(out_made, i - 1)
                if i < 2:
                    pe.wait_ge(product_read, 4 * NT - 1 + i)
                graph_product(i, i % 2, XB, ACC[i % 2], ready=y1_low if i == 0 else None).then_inc(last_made, 1)


_INS = ['x', 'adj', 'L0_gnn_W1', 'L0_gnn_W2', 'L0_gnn_W3', 'L0_gnn_U1_0', 'L0_gnn_U1_1', 'L0_gnn_U2_0',
        'L0_gnn_U2_1', 'L0_gnn_gamma', 'L0_gnn_beta']


def kernel(**inputs):
    import numpy as _np
    import concourse.bacc as _bacc
    from concourse import mybir as _mybir
    from concourse.bass_utils import run_bass_kernel_spmd as _run

    nc = _bacc.Bacc("TRN2", target_bir_lowering=False, num_devices=1, dynamic_dma_scratch_size=1024)
    arrays, args = {}, []
    for name in _INS:
        a = _np.ascontiguousarray(inputs[name])
        arrays[f"in_{name}_dram"] = a
        args.append(nc.dram_tensor(f"in_{name}_dram", a.shape, _mybir.dt.from_np(a.dtype), kind="ExternalInput").ap())
    shape = inputs['x'].shape
    args.append(nc.dram_tensor("out_0_dram", shape, _mybir.dt.float32, kind="ExternalOutput").ap())
    gnn_kernel(nc, *args)
    r = _run(nc, [arrays], core_ids=[0])
    return r.results[0]["out_0_dram"]
```
